# Optimizing a Trainium2 kernel written in Bass

```python
import numpy as np
import jax
import jax.numpy as jnp

def _softmax(x, axis=-1):
    return jax.nn.softmax(x, axis=axis)

def _gelu(x):
    return jax.nn.gelu(x, approximate=True)

def _silu(x):
    return jax.nn.silu(x)

def _sigmoid(x):
    return jax.nn.sigmoid(x)

def _layernorm(x, axis=-1, eps=1e-05):
    m = jnp.mean(x, axis=axis, keepdims=True)
    v = jnp.var(x, axis=axis, keepdims=True)
    return (x - m) / jnp.sqrt(v + eps)

def _scatter_add(tgt, idx, src, axis=0):
    return tgt.at[idx].add(src)

def _segment_sum(src, seg, n):
    return jax.ops.segment_sum(src, seg, n)
kernel_name = 'mk_xattn_ffn_d2_seqx_r4_03ad41'

def setup_inputs(seed: int=0):
    np.random.seed(seed)
    _w = jnp.asarray

    def _rec_inputs():
        import jax
        import jax.numpy as jnp
        _rk = jax.random.key(seed)
        x = 0.5 + 0.2887 * jax.random.normal(jax.random.fold_in(_rk, 1), (4, 512, 512), jnp.float32)
        _lenS = 512 - jax.random.randint(jax.random.fold_in(_rk, 7), (4,), 0, max(1, 512 // 4) + 1, jnp.int32)
        _lenS2 = 512 - jax.random.randint(jax.random.fold_in(_rk, 8), (4,), 0, max(1, 512 // 4) + 1, jnp.int32)
        _ctx_512P = jax.random.normal(jax.random.fold_in(_rk, 11), (4, 16, 128), jnp.float32)
        _ctx_512c = jax.random.dirichlet(jax.random.fold_in(_rk, 511), 0.3 * jnp.ones((16,), jnp.float32), (4, 512))
        _ctx_512t = jnp.einsum('bsk,bkd->bsd', _ctx_512c, _ctx_512P)
        _ctx_512t = _ctx_512t * jax.lax.rsqrt(jnp.mean(jnp.square(_ctx_512t)) + 1e-12) * 0.953939
        ctx_512 = -0.000392918 + 0.999932 * (_ctx_512t + 0.3 * jax.random.normal(jax.random.fold_in(_rk, 611), (4, 512, 128), jnp.float32))
        return (x, ctx_512)
    x, ctx_512 = _rec_inputs()

    def _L0_xattn_setup():
        import jax, jax.numpy as jnp
        import numpy as np
        B, N, D = (16, 512, 128)
        H = 4
        TOP_K_RATIO = 0.3
        key = jax.random.key(seed)
        k1, k2, k3, k4 = jax.random.split(key, 4)
        h = jax.random.normal(k1, (B, N, D), dtype=jnp.float32)
        adj_raw = jax.random.uniform(k2, (B, N, N), dtype=jnp.float32)
        lim = 1.0 / np.sqrt(D)
        Wq = jax.random.uniform(k3, (D, D), minval=-lim, maxval=lim, dtype=jnp.float32)
        Wk = jax.random.uniform(k4, (D, D), minval=-lim, maxval=lim, dtype=jnp.float32)
        gamma_raw = jnp.float32(-0.85)
        return {'h': h, 'adj_raw': adj_raw, 'Wq': Wq, 'Wk': Wk, 'gamma_raw': gamma_raw}
    _L0_xattn_all = _L0_xattn_setup()
    _L0_xattn_in = {k: v for k, v in _L0_xattn_all.items() if k in ('Wq', 'Wk', 'gamma_raw')}
    del _L0_xattn_all

    def _L0_ffn_setup():
        import jax, jax.numpy as jnp
        import numpy as np
        DIM = 512
        E = 8
        TOPK = 2
        H = 352
        HS = H * 2
        TEMP = 1.0
        key = jax.random.key(seed)
        ks = jax.random.split(key, 8)
        s = 0.02
        return {'x': jax.random.normal(ks[0], (2, 256, DIM), dtype=jnp.float32), 'gate_w': jax.random.normal(ks[1], (E, DIM), dtype=jnp.float32) * (1.0 / np.sqrt(DIM)), 'w1': jax.random.normal(ks[2], (E, H, DIM), dtype=jnp.float32) * s, 'w2': jax.random.normal(ks[3], (E, DIM, H), dtype=jnp.float32) * s, 'w3': jax.random.normal(ks[4], (E, H, DIM), dtype=jnp.float32) * s, 'sw1': jax.random.normal(ks[5], (HS, DIM), dtype=jnp.float32) * s, 'sw2': jax.random.normal(ks[6], (DIM, HS), dtype=jnp.float32) * s, 'sw3': jax.random.normal(ks[7], (HS, DIM), dtype=jnp.float32) * s}
    _L0_ffn_all = _L0_ffn_setup()
    _L0_ffn_in = {k: v for k, v in _L0_ffn_all.items() if k in ('gate_w', 'w1', 'w2', 'w3', 'sw1', 'sw2', 'sw3')}
    del _L0_ffn_all

    def _L1_xattn_setup():
        import jax, jax.numpy as jnp
        import numpy as np
        B, S, L = (2, 256, 256)
        DIM_Q, H, K, D_C, D_CQ, R = (512, 16, 128, 128, 384, 64)

        def _rope_tables(seq_len, dim, dtype):
            inv_freq = 1.0 / 10000.0 ** (jnp.arange(0, dim, 2, dtype=dtype) / dim)
            t = jnp.arange(seq_len, dtype=dtype)
            freqs = t[:, None] * inv_freq[None, :]
            sin = jnp.repeat(jnp.sin(freqs), 2, axis=-1)
            cos = jnp.repeat(jnp.cos(freqs), 2, axis=-1)
            return (sin, cos)

        def _rotate_half(x):
            h = x.shape[-1] // 2
            return jnp.concatenate([-x[..., h:], x[..., :h]], axis=-1)
        key = jax.random.key(seed)
        ks = jax.random.split(key, 8)
        s_in = 1.0 / np.sqrt(DIM_Q)
        s_k = 1.0 / np.sqrt(K)
        s_cq = 1.0 / np.sqrt(D_CQ)
        s_c = 1.0 / np.sqrt(D_C)
        return {'hidden_q': jax.random.normal(ks[0], (B, S, DIM_Q), jnp.float32), 'kv_c': jax.random.normal(ks[1], (B, L, D_C), jnp.float32), 'Wq': jax.random.normal(ks[2], (H * K, DIM_Q), jnp.float32) * s_in, 'w_kc_q': jax.random.normal(ks[3], (H, K, D_CQ), jnp.float32) * s_k, 'w_kc_kv': jax.random.normal(ks[4], (H, K, D_C), jnp.float32) * s_k, 'W_qr': jax.random.normal(ks[5], (H, D_CQ, R), jnp.float32) * s_cq / np.sqrt(R), 'W_kr': jax.random.normal(ks[6], (H, D_C, R), jnp.float32) * s_c, 'Wo': jax.random.normal(ks[7], (DIM_Q, H * K), jnp.float32) * s_k}
    _L1_xattn_all = _L1_xattn_setup()
    _L1_xattn_in = {k: v for k, v in _L1_xattn_all.items() if k in ('Wq', 'w_kc_q', 'w_kc_kv', 'W_qr', 'W_kr', 'Wo')}
    del _L1_xattn_all

    def _L1_ffn_setup():
        import jax, jax.numpy as jnp
        import numpy as np
        DIM_IN = 512
        DIM_HIDDEN = 2048
        key = jax.random.key(seed)
        k_x, k_g, k_u, k_d = jax.random.split(key, 4)
        s_in = 1.0 / np.sqrt(DIM_IN)
        s_hid = 1.0 / np.sqrt(DIM_HIDDEN)
        x = jax.random.normal(k_x, (4, 512, DIM_IN), dtype=jnp.float32)
        w_gate = jax.random.uniform(k_g, (DIM_HIDDEN, DIM_IN), jnp.float32, -s_in, s_in)
        w_up = jax.random.uniform(k_u, (DIM_HIDDEN, DIM_IN), jnp.float32, -s_in, s_in)
        w_down = jax.random.uniform(k_d, (DIM_IN, DIM_HIDDEN), jnp.float32, -s_hid, s_hid)
        return {'x': x, 'w_gate': w_gate, 'w_up': w_up, 'w_down': w_down}
    _L1_ffn_all = _L1_ffn_setup()
    _L1_ffn_in = {k: v for k, v in _L1_ffn_all.items() if k in ('w_gate', 'w_up', 'w_down')}
    del _L1_ffn_all
    return {'x': x, 'ctx_512': ctx_512, 'L0_xattn_Wq': _L0_xattn_in['Wq'], 'L0_xattn_Wk': _L0_xattn_in['Wk'], 'L0_xattn_gamma_raw': _L0_xattn_in['gamma_raw'], 'L0_ffn_gate_w': _L0_ffn_in['gate_w'], 'L0_ffn_w1': _L0_ffn_in['w1'], 'L0_ffn_w2': _L0_ffn_in['w2'], 'L0_ffn_w3': _L0_ffn_in['w3'], 'L0_ffn_sw1': _L0_ffn_in['sw1'], 'L0_ffn_sw2': _L0_ffn_in['sw2'], 'L0_ffn_sw3': _L0_ffn_in['sw3'], 'L1_xattn_Wq': _L1_xattn_in['Wq'], 'L1_xattn_w_kc_q': _L1_xattn_in['w_kc_q'], 'L1_xattn_w_kc_kv': _L1_xattn_in['w_kc_kv'], 'L1_xattn_W_qr': _L1_xattn_in['W_qr'], 'L1_xattn_W_kr': _L1_xattn_in['W_kr'], 'L1_xattn_Wo': _L1_xattn_in['Wo'], 'L1_ffn_w_gate': _L1_ffn_in['w_gate'], 'L1_ffn_w_up': _L1_ffn_in['w_up'], 'L1_ffn_w_down': _L1_ffn_in['w_down']}

def reference(x, ctx_512, L0_xattn_Wq, L0_xattn_Wk, L0_xattn_gamma_raw, L0_ffn_gate_w, L0_ffn_w1, L0_ffn_w2, L0_ffn_w3, L0_ffn_sw1, L0_ffn_sw2, L0_ffn_sw3, L1_xattn_Wq, L1_xattn_w_kc_q, L1_xattn_w_kc_kv, L1_xattn_W_qr, L1_xattn_W_kr, L1_xattn_Wo, L1_ffn_w_gate, L1_ffn_w_up, L1_ffn_w_down):
    import jax
    import jax.numpy as jnp

    def _L0_xattn_ref(h, adj_raw, Wq, Wk, gamma_raw):
        import jax, jax.numpy as jnp
        import numpy as np
        B, N, D = (16, 512, 128)
        H = 4
        TOP_K_RATIO = 0.3
        b, n, dm = h.shape
        d = dm // H
        Q = (h @ Wq.T).reshape(b, n, H, d).transpose(0, 2, 1, 3)
        K = (h @ Wk.T).reshape(b, n, H, d).transpose(0, 2, 1, 3)
        sim = jnp.einsum('bhnd,bhmd->bnm', Q, K) / (jnp.sqrt(jnp.float32(d)) * H)
        k = max(1, int(n * TOP_K_RATIO))
        topk_vals = jax.lax.top_k(sim, k)[0]
        threshold = topk_vals[:, :, -1:]
        sparse_mask = (sim >= threshold).astype(sim.dtype)
        A_learned = jax.nn.sigmoid(sim) * sparse_mask
        A_learned = (A_learned + jnp.swapaxes(A_learned, -1, -2)) * 0.5
        gamma = jax.nn.sigmoid(gamma_raw)
        return (1.0 - gamma) * adj_raw + gamma * A_learned

    def _L0_ffn_ref(x, gate_w, w1, w2, w3, sw1, sw2, sw3):
        import jax, jax.numpy as jnp
        import numpy as np
        DIM = 512
        E = 8
        TOPK = 2
        H = 352
        HS = H * 2
        TEMP = 1.0
        orig_shape = x.shape
        xf = x.reshape(-1, orig_shape[-1])
        N = xf.shape[0]
        scores = xf @ gate_w.T / TEMP
        probs = jax.nn.softmax(scores, axis=-1)
        topk_vals, topk_idx = jax.lax.top_k(probs, TOPK)
        expert_mask = jnp.zeros((N, E), dtype=xf.dtype)
        expert_mask = expert_mask.at[jnp.arange(N)[:, None], topk_idx].set(topk_vals)
        h = jax.nn.silu(jnp.einsum('nd,ehd->neh', xf, w1)) * jnp.einsum('nd,ehd->neh', xf, w3)
        expert_out = jnp.einsum('neh,edh->ned', h, w2)
        y = jnp.einsum('ned,ne->nd', expert_out, expert_mask)
        hs = jax.nn.silu(xf @ sw1.T) * (xf @ sw3.T)
        y = y + hs @ sw2.T
        return y.reshape(orig_shape)

    def _L1_xattn_ref(hidden_q, kv_c, Wq, w_kc_q, w_kc_kv, W_qr, W_kr, Wo):
        import jax, jax.numpy as jnp
        import numpy as np
        B, S, L = (2, 256, 256)
        DIM_Q, H, K, D_C, D_CQ, R = (512, 16, 128, 128, 384, 64)

        def _rope_tables(seq_len, dim, dtype):
            inv_freq = 1.0 / 10000.0 ** (jnp.arange(0, dim, 2, dtype=dtype) / dim)
            t = jnp.arange(seq_len, dtype=dtype)
            freqs = t[:, None] * inv_freq[None, :]
            sin = jnp.repeat(jnp.sin(freqs), 2, axis=-1)
            cos = jnp.repeat(jnp.cos(freqs), 2, axis=-1)
            return (sin, cos)

        def _rotate_half(x):
            h = x.shape[-1] // 2
            return jnp.concatenate([-x[..., h:], x[..., :h]], axis=-1)
        b, s, _ = hidden_q.shape
        l = kv_c.shape[1]
        q_hk = (hidden_q @ Wq.T).reshape(b, s, H, K)
        q_big = jnp.einsum('bshk,hkq->bshq', q_hk, w_kc_q)
        sin, cos = _rope_tables(l, D_C, kv_c.dtype)
        kv_rope = kv_c * cos[None] + _rotate_half(kv_c) * sin[None]
        q_r = jnp.einsum('bshq,hqr->bhsr', q_big, W_qr)
        k_r = jnp.einsum('bld,hdr->bhlr', kv_rope, W_kr)
        scores = jnp.einsum('bhsr,bhlr->bhsl', q_r, k_r)
        attn = jax.nn.softmax(scores, axis=-1)
        ctx_c = jnp.einsum('bhsl,bld->bhsd', attn, kv_rope)
        ctx_lat = jnp.einsum('bhsd,hkd->bshk', ctx_c, w_kc_kv)
        out = ctx_lat.reshape(b, s, H * K) @ Wo.T
        return out

    def _L1_ffn_ref(x, w_gate, w_up, w_down):
        import jax, jax.numpy as jnp
        import numpy as np
        DIM_IN = 512
        DIM_HIDDEN = 2048
        gate = jnp.einsum('bsd,hd->bsh', x, w_gate)
        up = jnp.einsum('bsd,hd->bsh', x, w_up)
        gated = jax.nn.silu(gate) * up
        return jnp.einsum('bsh,dh->bsd', gated, w_down)
    x = x + _L0_xattn_ref(ctx_512, _layernorm(x, axis=-1), L0_xattn_Wq, L0_xattn_Wk, L0_xattn_gamma_raw)
    x = x + _L0_ffn_ref(_layernorm(x, axis=-1), L0_ffn_gate_w, L0_ffn_w1, L0_ffn_w2, L0_ffn_w3, L0_ffn_sw1, L0_ffn_sw2, L0_ffn_sw3)
    x = x + _L1_xattn_ref(_layernorm(x, axis=-1), ctx_512, L1_xattn_Wq, L1_xattn_w_kc_q, L1_xattn_w_kc_kv, L1_xattn_W_qr, L1_xattn_W_kr, L1_xattn_Wo)
    x = x + _L1_ffn_ref(_layernorm(x, axis=-1), L1_ffn_w_gate, L1_ffn_w_up, L1_ffn_w_down)
    return x

_drawn_inputs = setup_inputs


def setup_inputs(seed=0):
    import zlib

    import numpy as np

    out = dict(_drawn_inputs(seed))
    spreads = {}
    factors = {'L0_ffn_gate_w': 5.239,
     'L0_ffn_w1': 4.683,
     'L0_ffn_w2': 4.592,
     'L0_ffn_w3': 4.602,
     'L0_ffn_sw1': 4.649,
     'L0_ffn_sw2': 4.535,
     'L0_ffn_sw3': 4.548,
     'L1_ffn_w_gate': 4.635,
     'L1_ffn_w_up': 4.49,
     'L1_ffn_w_down': 4.486}
    for name, (base, spread) in spreads.items():
        noise = np.random.default_rng([zlib.crc32(name.encode()), seed]).standard_normal(out[name].shape)
        drawn = base * np.exp(spread * noise) if base else spread * noise
        out[name] = jnp.asarray(drawn.astype(out[name].dtype))
    for name, factor in factors.items():
        out[name] = (out[name] * factor).astype(out[name].dtype)
    return out
```

```python
import concourse.bass as bass
from concourse import mybir
from contextlib import ExitStack

FP32 = mybir.dt.float32
FP16 = mybir.dt.float16
U32 = mybir.dt.uint32
ALU = mybir.AluOpType
ACT = mybir.ActivationFunctionType
AX = mybir.AxisListType

P = 128
B, S, D = 4, 512, 512
KD = D // P
NT = S // P
C = 128
TOPK = int(S * 0.3)
EPS = 1e-5
E = 8
HE = 384
NG0, NJ0 = 10, 3
NG1, NJ1 = 4, 4
H, R, Q3 = 16, 64, 3
SC = 64.0
PSC = 1024.0
PROBES = 4
TARGET = TOPK - 4.5
Z_TARGET = 0.527
DENSITY = 178.0
FAR = 3.0e38
BISECT = 30


def ds(start, size):
    return bass.ds(start, size)


def start_at_one(eng, *sems):
    for s in sems:
        eng.nop().then_inc(s, 1)


def after(eng, sem, n):
    eng.wait_ge(sem, n + 1)


class Scope:

    def __init__(self, nc, ctx):
        self.nc, self.ctx = nc, ctx

    def sb(self, name, shape, dt=FP32):
        return self.ctx.enter_context(self.nc.sbuf_tensor(name, shape, dt))

    def ps(self, name, shape=(P, 512), dt=FP32):
        return self.ctx.enter_context(self.nc.psum_tensor(name, list(shape), dt))

    def sem(self, name):
        return self.ctx.enter_context(self.nc.semaphore(name))


class LayerNorm:

    def __init__(self, sc, keep, tag, xn, psT):
        self.k, self.xn, self.psT = keep, xn, psT
        self.st = sc.sb(f"{tag}_stats", [P, NT, 6])
        self.mv = sc.sb(f"{tag}_meanvar", [P, NT, 2])
        self.std = sc.sb(f"{tag}_std", [P, NT])
        self.rstd = sc.sb(f"{tag}_rstd", [P, NT])
        self.s_var = sc.sem(f"{tag}_var_ready")
        self.s_std = sc.sem(f"{tag}_std_ready")
        self.s_xn = sc.sem(f"{tag}_xn_ready")
        self.s_xt = sc.sem(f"{tag}_transposed")
        self.s_hi = sc.sem(f"{tag}_hi_ready")
        self.s_lo = sc.sem(f"{tag}_lo_ready")

    def stats(self, nc, v, b):
        for n in range(NT):
            nc.vector.bn_stats(self.st[:, n, :], self.k.x[:, 4 * b + n, :])
        nc.vector.drain()
        for n in range(NT):
            last = nc.vector.bn_aggr(self.mv[:, n, :], self.st[:, n, :])
        last.then_inc(self.s_var, 1)

    def root(self, nc, a, done):
        a.wait_ge(self.s_var, done + 1)
        nc.scalar.activation(self.std[:, :], self.mv[:, :, 1], ACT.Sqrt,
                             bias=self.k.eps[:, 0:1]).then_inc(self.s_std, 1)

    def inverse(self, nc, v, done):
        v.wait_ge(self.s_std, done + 1)
        nc.vector.reciprocal(self.rstd[:, :], self.std[:, :])
        nc.vector.drain()

    def vector(self, nc, v, b, done):
        self.stats(nc, v, b)
        self.inverse(nc, v, done)
        for n in range(NT + 1):
            if n < NT:
                if n >= 2:
                    v.wait_ge(self.s_xt, 4 * done + n - 1)
                nc.vector.tensor_scalar(self.xn[n % 2][:, :], self.k.x[:, 4 * b + n, :], self.mv[:, n, 0:1],
                                        self.rstd[:, n:n + 1], ALU.subtract, ALU.mult).then_inc(self.s_xn, 1)
            if n >= 1:
                m = n - 1
                v.wait_ge(self.s_hi, 4 * done + m + 1)
                nc.vector.tensor_tensor(self.k.xT[:, b, :, 1, m * P:(m + 1) * P],
                                        self.psT[m % 2][:, :].rearrange("p (k t) -> p k t", k=KD),
                                        self.k.xT[:, b, :, 0, m * P:(m + 1) * P],
                                        ALU.subtract).then_inc(self.s_lo, 1)

    def scalar(self, nc, a, b, done):
        self.root(nc, a, done)
        for n in range(NT):
            a.wait_ge(self.s_xt, 4 * done + n + 1)
            nc.scalar.activation(self.k.xT[:, b, :, 0, n * P:(n + 1) * P],
                                 self.psT[n % 2][:, :].rearrange("p (k t) -> p k t", k=KD),
                                 ACT.Copy).then_inc(self.s_hi, 1)

    def tensor(self, nc, pe, done):
        for n in range(NT):
            pe.wait_ge(self.s_xn, 4 * done + n + 1)
            if n >= 2:
                after(pe, self.s_lo, 4 * done + n - 1)
            for k in range(KD):
                last = nc.tensor.transpose(self.psT[n % 2][:, k * P:(k + 1) * P],
                                           self.xn[n % 2][:, k * P:(k + 1) * P], self.k.ident[:, :])
            last.then_inc(self.s_xt, 1)


def split_matmuls(nc, out, pairs):
    n = len(pairs)
    for i, (lhs, rhs) in enumerate(pairs):
        nc.tensor.matmul(out, lhs(0), rhs(0), start=i == 0, stop=False)
        nc.tensor.matmul(out, lhs(0), rhs(1), start=False, stop=False)
        last = nc.tensor.matmul(out, lhs(1), rhs(0), start=False, stop=i == n - 1)
    return last


class Keep:

    def __init__(self, sc):
        self.x = sc.sb("x", [P, B * NT, D])
        self.xT = sc.sb("xT", [P, B, KD, 2, S], FP16)
        self.ident = sc.sb("ident", [P, P])
        self.ident16 = sc.sb("ident16", [P, P], FP16)
        self.eps = sc.sb("eps", [P, 1])

    def attention(self, sc):
        self.wvo = sc.sb("wvo", [P, 2, H, D], FP16)
        self.wqc = sc.sb("wqc", [P, KD, 2, H * R], FP16)
        self.wkr = sc.sb("wkr", [P, 2, H, 2, R], FP16)
        self.kvs = sc.sb("kvs", [P, 2, B, 2, S], FP16)
        self.gate_w = sc.sb("gate_w_split", [P, KD, 2, E], FP16)


def stage_adjacency(nc, keep, d):
    with ExitStack() as ctx:
        sc = Scope(nc, ctx)
        ctxT = sc.sb("ctxT", [P, B, S])
        wq, wk = sc.sb("wq0", [P, P]), sc.sb("wk0", [P, P])
        gam = sc.sb("gam", [P, 8])
        GR, GS, OMG, HG = (gam[:, i:i + 1] for i in range(4))
        gate_raw = sc.sb("gate_raw", [P, KD, E])
        gate32 = sc.sb("gate32", [P, KD, E])
        QT, KT = sc.sb("QT", [P, S]), sc.sb("KT", [P, S])
        sim = sc.sb("sim", [P, 2, NT, S])
        A = sc.sb("A", [P, NT, S])
        hit = sc.sb("hit", [P, NT, S], mybir.dt.uint8)
        rest = sc.sb("rest", [P, 2, D])
        xn = [rest[:, i, :] for i in range(2)]
        lo_t = sc.sb("lo_t", [P, NT])
        step = sc.sb("step", [P, NT])
        probe = sc.sb("probe", [P, NT])
        cnt = sc.sb("cnt", [P, NT])
        top = sc.sb("top", [P, NT])
        st1 = sc.sb("st1", [P, NT, 6])
        mvs = sc.sb("mvs", [P, NT, 2])
        sds = sc.sb("sds", [P, NT])
        cur, low2, high2, dif = (sc.sb(n, [P, 2, NT]) for n in ("cur", "low2", "high2", "dif"))
        off, nxt = sc.sb("off", [P, NT]), sc.sb("nxt", [P, NT])
        above, below, miss = (sc.sb(n, [P, NT], U32) for n in ("above", "below", "miss"))
        eight, pick = sc.sb("eight", [P, NT, 8]), sc.sb("pick", [P, NT, 8])
        place = sc.sb("place", [P, 8])
        bad, badi = sc.sb("bad", [P, 1]), sc.sb("badi", [1, 1], mybir.dt.int32)
        ones = sc.sb("ones", [P, 1])
        fa, fb = sc.sb("fa", [P, NT]), sc.sb("fb", [P, NT])
        st0 = sc.sb("st0", [P, NT, 6])
        mv0 = sc.sb("mv0", [P, NT, 2])
        std0, rstd0 = sc.sb("std0", [P, NT]), sc.sb("rstd0", [P, NT])
        r_wq = [sc.sb(f"r_wq{i}", [P, D]) for i in range(2)]
        r_kcq = [sc.sb(f"r_kcq{i}", [P, Q3, P]) for i in range(2)]
        r_qr = [sc.sb(f"r_qr{i}", [P, Q3, R]) for i in range(2)]
        r_kckv = [sc.sb(f"r_kckv{i}", [P, C]) for i in range(2)]
        r_wo = [sc.sb(f"r_wo{i}", [P, D]) for i in range(2)]
        r_kr = [sc.sb(f"r_kr{i}", [P, R]) for i in range(2)]
        wc = sc.sb("wc", [P, R])
        c_q, c_vo, c_kr = sc.sb("c_q", [P, KD, R]), sc.sb("c_vo", [P, D]), sc.sb("c_kr", [P, R])
        cos = sc.sb("cos", [P, S])
        sin = sc.sb("sin", [P, S])
        craw, crot = sc.sb("craw", [P, S]), sc.sb("crot", [P, S])
        rope = craw

        ps_proj = sc.ps("ps_proj")
        ps_sim = [sc.ps(f"ps_sim{i}") for i in range(2)]
        ps_T = [sc.ps(f"ps_T{i}") for i in range(2)]
        ps_wc = sc.ps("ps_wc")
        ps_wq = sc.ps("ps_wq")
        ps_vo = sc.ps("ps_vo")
        ps_bad = ps_wc
        ln = LayerNorm(sc, keep, "ln1", xn, ps_T)

        s_ctx, s_w0, s_x = sc.sem("ctx_loaded"), sc.sem("w0_loaded"), sc.sem("x_loaded")
        s_gam, s_gw = sc.sem("gamma_loaded"), sc.sem("gate_loaded")
        s_id = sc.sem("ident_built")
        s_const = sc.sem("constants_built")
        s_sig = sc.sem("gamma_sigmoid")
        s_qps, s_qk = sc.sem("proj_in_psum"), sc.sem("proj_in_sbuf")
        s_sps, s_sim = sc.sem("sim_in_psum"), sc.sem("sim_in_sbuf")
        s_sgm, s_mask, s_at = sc.sem("sigmoid_done"), sc.sem("masked"), sc.sem("A_transposed")
        s_blend, s_blend_t = sc.sem("blended"), sc.sem("blended_tile")
        s_var0, s_std0 = sc.sem("var0_ready"), sc.sem("std0_ready")
        s_raw = [sc.sem(f"prep_raw{i}") for i in range(2)]
        s_wcps, s_wc = sc.sem("wc_in_psum"), sc.sem("wc_in_sbuf")
        s_pps, s_p32 = sc.sem("prep_in_psum"), sc.sem("prep_in_sbuf")
        s_phi, s_plo = sc.sem("prep_hi"), sc.sem("prep_lo")
        s_rope_in, s_rope, s_rhi, s_rlo = sc.sem("rope_in"), sc.sem("rope_done"), sc.sem("rope_hi"), sc.sem("rope_lo")
        s_tab = sc.sem("rope_tables")
        s_gate = sc.sem("gate_split")
        s_vars, s_sds = sc.sem("row_var"), sc.sem("row_sd")
        s_bad, s_badsum = sc.sem("bad_rows"), sc.sem("bad_rows_summed")

        block = ctx.enter_context(nc.Block())

        @block.sync
        def _(sp):
            start_at_one(sp, ln.s_lo, s_phi, s_rhi, s_blend, s_qk, s_wc, s_plo, s_p32)
            sp.dma_start(ctxT[:, :, :], d["ctxT"].rearrange("b p s -> p b s")).then_inc(s_ctx, 16)
            sp.dma_start(wq[:, :], d["wq0T"]).then_inc(s_w0, 16)
            sp.dma_start(wk[:, :], d["wk0T"]).then_inc(s_w0, 16)
            sp.dma_start(GR, d["gamma"]).then_inc(s_gam, 16)
            for b in range(B):
                sp.dma_start(keep.x[:, 4 * b:4 * b + 4, :],
                             d["x"][b * S:(b + 1) * S, :].rearrange("(t p) n -> p t n", p=P)).then_inc(s_x, 16)
            sp.dma_start(gate_raw[:, :, :], d["gate_wT"].rearrange("(k p) e -> p k e", p=P)).then_inc(s_gw, 16)
            with sp.Fori(0, H // 2) as i:
                for par in range(2):
                    h = 2 * i + par
                    after(sp, s_phi, 6 * i)
                    rows = ds(h * P, P)
                    sp.dma_start(r_wq[par][:, :], d["wq1"][rows, :]).then_inc(s_raw[par], 16)
                    sp.dma_start(r_kcq[par][:, :, :], d["kcqT"][h, :, :].rearrange("(t p) k -> p t k", p=P)).then_inc(s_raw[par], 16)
                    sp.dma_start(r_qr[par][:, :, :], d["wqr"][h, :, :].rearrange("(t p) r -> p t r", p=P)).then_inc(s_raw[par], 16)
                    sp.dma_start(r_kckv[par][:, :], d["kckv"][h, :, :]).then_inc(s_raw[par], 16)
                    sp.dma_start(r_wo[par][:, :], d["woT"][rows, :]).then_inc(s_raw[par], 16)
                    sp.dma_start(r_kr[par][:, :], d["wkr"][h, :, :]).then_inc(s_raw[par], 16)

        @block.gpsimd
        def _(pool):
            nc.gpsimd.memset(keep.ident[:, :], 0.0)
            nc.gpsimd.memset(keep.eps[:, :], EPS)
            nc.gpsimd.memset(ones[:, :], 1.0)
            for j in range(8):
                nc.gpsimd.memset(place[:, j:j + 1], float(j))
            pool.drain()
            nc.gpsimd.affine_select(out=keep.ident[:, :], in_=keep.ident[:, :], compare_op=ALU.not_equal,
                                    fill=1.0, base=0, pattern=[[-1, P]], channel_multiplier=1)
            pool.drain()
            nc.gpsimd.tensor_copy(keep.ident16[:, :], keep.ident[:, :]).then_inc(s_id, 1)
            pool.wait_ge(s_gw, 16)
            nc.gpsimd.tensor_scalar(gate32[:, :, :], gate_raw[:, :, :], SC, 1.0, ALU.mult, ALU.mult)
            pool.drain()
            nc.gpsimd.tensor_copy(keep.gate_w[:, :, 0, :], gate32[:, :, :])
            pool.drain()
            nc.gpsimd.tensor_tensor(keep.gate_w[:, :, 1, :], gate32[:, :, :], keep.gate_w[:, :, 0, :],
                                    ALU.subtract).then_inc(s_gate, 1)
            with pool.Fori(0, 2) as i:
                after(pool, s_rhi, 4 * i)
                pool.dma_start(cos[:, :], d["rope_cos"][i, :, :]).then_inc(s_tab, 16)
                pool.dma_start(sin[:, :], d["rope_sin"][i, :, :]).then_inc(s_tab, 16)
                for par in range(2):
                    for hh in range(4):
                        n = 8 * i + 4 * par + hh
                        after(pool, s_phi, 3 * n + 3)
                        nc.gpsimd.tensor_tensor(keep.wqc[:, :, 1, ds(n * R, R)], c_q[:, :, :],
                                                keep.wqc[:, :, 0, ds(n * R, R)], ALU.subtract)
                        nc.gpsimd.tensor_tensor(keep.wvo[:, 1, n, :], c_vo[:, :], keep.wvo[:, 0, n, :], ALU.subtract)
                        for two in range(2):
                            last = nc.gpsimd.tensor_tensor(keep.wkr[:, 1, n, two, :], c_kr[:, :],
                                                           keep.wkr[:, 0, n, two, :], ALU.subtract)
                        last.then_inc(s_plo, 1)
                    for u in range(2):
                        n = 4 * i + 2 * par + u
                        if par + u > 0:
                            after(pool, s_rhi, n)
                        b = 2 * par + u
                        pool.dma_start(craw[:, :], d["ctx_both"][i, b, :, :]).then_inc(s_rope_in, 16)
                        pool.dma_start(crot[:, :], d["ctx_rot"][i, b, :, :]).then_inc(s_rope_in, 16)
                        pool.wait_ge(s_tab, 32 * i + 32)
                        pool.wait_ge(s_rope_in, 32 * n + 32)
                        nc.gpsimd.tensor_tensor(craw[:, :], craw[:, :], cos[:, :], ALU.mult)
                        nc.gpsimd.tensor_tensor(crot[:, :], crot[:, :], sin[:, :], ALU.mult)
                        pool.drain()
                        nc.gpsimd.tensor_tensor(rope[:, :], craw[:, :], crot[:, :], ALU.add).then_inc(s_rope, 1)
                        after(pool, s_rhi, n + 1)
                        nc.gpsimd.tensor_tensor(keep.kvs[:, i, b, 1, :], rope[:, :], keep.kvs[:, i, b, 0, :],
                                                ALU.subtract).then_inc(s_rlo, 1)
                        pool.drain()

        @block.scalar
        def _(a):
            a.wait_ge(s_gam, 16)
            nc.scalar.activation(GS, GR, ACT.Sigmoid).then_inc(s_sig, 1)
            a.wait_ge(s_id, 1)
            def similarities(b):
                for w, T in enumerate((QT, KT)):
                    a.wait_ge(s_qps, 2 * b + w + 1)
                    nc.scalar.activation(T[:, :], ps_proj[:, :], ACT.Copy).then_inc(s_qk, 1)
                for n in range(NT):
                    a.wait_ge(s_sps, 4 * b + n + 1)
                    nc.scalar.activation(sim[:, b % 2, n, :], ps_sim[n % 2][:, :], ACT.Copy,
                                         scale=1.0 / (float(C // 4) ** 0.5 * 4)).then_inc(s_sim, 1)

            def batch(b, more):
                a.wait_ge(s_vars, b + 1)
                nc.scalar.activation(sds[:, :], mvs[:, :, 1], ACT.Sqrt).then_inc(s_sds, 1)
                a.wait_ge(s_var0, b + 1)
                nc.scalar.activation(std0[:, :], mv0[:, :, 1], ACT.Sqrt, bias=keep.eps[:, 0:1]).then_inc(s_std0, 1)
                after(a, s_blend, b)
                nc.scalar.activation(A[:, :, :], sim[:, b % 2, :, :], ACT.Sigmoid).then_inc(s_sgm, 1)
                for hh in range(4):
                    n = 4 * b + hh
                    q = hh % 2
                    a.wait_ge(s_wcps, n + 1)
                    nc.scalar.activation(wc[:, :], ps_wc[:, 0:R], ACT.Copy).then_inc(s_wc, 1)
                    a.wait_ge(s_pps, n + 1)
                    after(a, s_plo, n)
                    nc.scalar.activation(c_q[:, :, :], ps_wq[:, 0:KD * R].rearrange("p (k r) -> p k r", k=KD),
                                         ACT.Copy, scale=SC)
                    nc.scalar.activation(c_vo[:, :], ps_vo[:, :], ACT.Copy, scale=SC).then_inc(s_p32, 1)
                    nc.scalar.activation(c_kr[:, :], r_kr[q][:, :], ACT.Copy, scale=SC)
                    a.drain()
                    nc.scalar.activation(keep.wqc[:, :, 0, ds(n * R, R)], c_q[:, :, :], ACT.Copy).then_inc(s_phi, 1)
                    nc.scalar.activation(keep.wvo[:, 0, n, :], c_vo[:, :], ACT.Copy).then_inc(s_phi, 1)
                    nc.scalar.activation(keep.wkr[:, 0, n, :, :], c_kr[:, :].unsqueeze(1).to_broadcast([P, 2, R]),
                                         ACT.Copy).then_inc(s_phi, 1)
                if more:
                    similarities(b + 1)
                ln.scalar(nc, a, b, b)
                for u in range(2):
                    n = 2 * b + u
                    a.wait_ge(s_rope, n + 1)
                    nc.scalar.activation(keep.kvs[:, n // 4, n % 4, 0, :], rope[:, :], ACT.Copy).then_inc(s_rhi, 1)

            similarities(0)
            with a.Fori(0, B - 1) as b:
                batch(b, True)
            batch(B - 1, False)

        def search(v, b, par):
            for n in range(NT):
                nc.vector.bn_stats(st1[:, n, :], sim[:, par, n, 0:S // 2])
            v.drain()
            for n in range(NT):
                nc.vector.bn_aggr(mvs[:, n, :], st1[:, n, :])
            v.drain()
            v.nop().then_inc(s_vars, 1)
            v.wait_ge(s_sds, b + 1)
            for dst, z in ((cur, Z_TARGET), (low2, -3.0), (high2, 3.0)):
                nc.vector.scalar_tensor_tensor(dst[:, 0, :], sds[:, :], z, mvs[:, :, 0], ALU.mult, ALU.add)
            nc.vector.memset(low2[:, 1, :], float(S))
            nc.vector.memset(high2[:, 1, :], 0.0)
            v.drain()
            for k in range(PROBES):
                for n in range(NT):
                    nc.vector.tensor_scalar(hit[:, n, :], sim[:, par, n, :], cur[:, 0, n:n + 1], None,
                                            ALU.is_ge, ALU.add, accum_out=cur[:, 1, n:n + 1])
                v.drain()
                nc.vector.tensor_scalar(above[:, :], cur[:, 1, :], TARGET, None, ALU.is_gt)
                nc.vector.tensor_scalar(below[:, :], cur[:, 1, :], TARGET, None, ALU.is_lt)
                nc.vector.tensor_scalar(off[:, :], cur[:, 1, :], TARGET - 4.0, None, ALU.is_lt)
                v.drain()
                nc.vector.copy_predicated(low2[:, :, :], above[:, :].unsqueeze(1).to_broadcast([P, 2, NT]), cur[:, :, :])
                nc.vector.copy_predicated(high2[:, :, :], below[:, :].unsqueeze(1).to_broadcast([P, 2, NT]), cur[:, :, :])
                nc.vector.scalar_tensor_tensor(miss[:, :], cur[:, 1, :], TARGET + 4.0, off[:, :], ALU.is_gt, ALU.add)
                v.drain()
                if k == 0:
                    nc.vector.tensor_scalar(off[:, :], cur[:, 1, :], TARGET, 1.0 / DENSITY, ALU.subtract, ALU.mult)
                    v.drain()
                    nc.vector.tensor_tensor(off[:, :], off[:, :], sds[:, :], ALU.mult)
                    v.drain()
                    nc.vector.tensor_tensor(nxt[:, :], cur[:, 0, :], off[:, :], ALU.add)
                else:
                    nc.vector.tensor_tensor(dif[:, :, :], high2[:, :, :], low2[:, :, :], ALU.subtract)
                    nc.vector.tensor_scalar(off[:, :], low2[:, 1, :], TARGET, None, ALU.subtract)
                    v.drain()
                    nc.vector.reciprocal(dif[:, 1, :], dif[:, 1, :])
                    nc.vector.tensor_tensor(off[:, :], off[:, :], dif[:, 0, :], ALU.mult)
                    v.drain()
                    nc.vector.tensor_tensor(off[:, :], off[:, :], dif[:, 1, :], ALU.mult)
                    v.drain()
                    nc.vector.tensor_tensor(nxt[:, :], low2[:, 0, :], off[:, :], ALU.subtract)
                v.drain()
                nc.vector.copy_predicated(cur[:, 0, :], miss[:, :], nxt[:, :])
                v.drain()
            for n in range(NT):
                nc.vector.tensor_scalar(hit[:, n, :], sim[:, par, n, :], cur[:, 0, n:n + 1], None,
                                        ALU.is_ge, ALU.add, accum_out=cur[:, 1, n:n + 1])
            v.drain()
            nc.vector.tensor_scalar(off[:, :], cur[:, 1, :], TARGET - 4.0, None, ALU.is_lt)
            v.drain()
            nc.vector.scalar_tensor_tensor(off[:, :], cur[:, 1, :], TARGET + 4.0, off[:, :], ALU.is_gt, ALU.add,
                                           accum_out=bad[:, 0:1])
            v.drain()
            v.nop().then_inc(s_bad, 1)
            for n in range(NT):
                nc.vector.scalar_tensor_tensor(rest[:, n % 2, :], hit[:, n, :], -FAR, sim[:, par, n, :], ALU.mult, ALU.add)
                v.drain()
                nc.vector.max(eight[:, n, :], rest[:, n % 2, :])
            nc.vector.tensor_scalar(off[:, :], cur[:, 1, :], -1.0, TOPK - 1.0, ALU.mult, ALU.add)
            v.drain()
            nc.vector.tensor_tensor(pick[:, :, :], place[:, :].unsqueeze(1).to_broadcast([P, NT, 8]),
                                    off[:, :].unsqueeze(2).to_broadcast([P, NT, 8]), ALU.is_equal)
            v.drain()
            nc.vector.tensor_tensor(pick[:, :, :], pick[:, :, :], eight[:, :, :], ALU.mult)
            v.drain()
            nc.vector.tensor_reduce(lo_t[:, :], pick[:, :, :], AX.X, ALU.add)
            v.wait_ge(s_badsum, b + 1)
            nc.vector.tensor_copy(badi[:, :], ps_bad[0:1, 0:1])
            v.drain()
            failed = v.value_load(badi[0:1, 0:1], min_val=0, max_val=P * NT)
            with v.If(failed > 0):
                bisect(v, par)

        def bisect(v, par):
            nc.vector.tensor_reduce(lo_t[:, :], sim[:, par, :, :], AX.X, ALU.min)
            nc.vector.tensor_reduce(top[:, :], sim[:, par, :, :], AX.X, ALU.max)
            v.drain()
            nc.vector.tensor_tensor(step[:, :], top[:, :], lo_t[:, :], ALU.subtract)
            v.drain()
            with v.Fori(0, BISECT):
                nc.vector.tensor_scalar(step[:, :], step[:, :], 0.5, None, ALU.mult)
                v.drain()
                nc.vector.tensor_tensor(probe[:, :], lo_t[:, :], step[:, :], ALU.add)
                v.drain()
                for n in range(NT):
                    nc.vector.tensor_scalar(hit[:, n, :], sim[:, par, n, :], probe[:, n:n + 1], None,
                                            ALU.is_ge, ALU.add, accum_out=cnt[:, n:n + 1])
                v.drain()
                nc.vector.scalar_tensor_tensor(probe[:, :], cnt[:, :], TOPK - 0.5, step[:, :],
                                               ALU.is_ge, ALU.mult)
                v.drain()
                nc.vector.tensor_tensor(lo_t[:, :], lo_t[:, :], probe[:, :], ALU.add)
                v.drain()

        @block.vector
        def _(v):
            v.wait_ge(s_sig, 1)
            nc.vector.tensor_scalar(OMG, GS, -1.0, 1.0, ALU.mult, ALU.add)
            nc.vector.tensor_scalar(HG, GS, 0.5, None, ALU.mult)
            with v.Fori(0, B) as b:
                par = b % 2
                v.wait_ge(s_x, 64)
                for n in range(NT):
                    nc.vector.bn_stats(st0[:, n, :], keep.x[:, 4 * b + n, :])
                v.drain()
                for n in range(NT):
                    last = nc.vector.bn_aggr(mv0[:, n, :], st0[:, n, :])
                last.then_inc(s_var0, 1)
                v.wait_ge(s_sim, 4 * b + 4)
                search(v, b, par)
                v.wait_ge(s_sgm, b + 1)
                for n in range(NT):
                    nc.vector.scalar_tensor_tensor(A[:, n, :], sim[:, par, n, :], lo_t[:, n:n + 1], A[:, n, :],
                                                   ALU.is_ge, ALU.mult).then_inc(s_mask, 1)
                v.wait_ge(s_std0, b + 1)
                nc.vector.reciprocal(rstd0[:, :], std0[:, :])
                v.drain()
                nc.vector.tensor_tensor(fb[:, :], mv0[:, :, 0], rstd0[:, :], ALU.mult)
                nc.vector.tensor_scalar(fa[:, :], rstd0[:, :], OMG, 1.0, ALU.mult, ALU.add)
                v.drain()
                nc.vector.tensor_scalar(fb[:, :], fb[:, :], OMG, -1.0, ALU.mult, ALU.mult)
                v.drain()
                for n in range(NT):
                    nc.vector.tensor_scalar(keep.x[:, 4 * b + n, :], keep.x[:, 4 * b + n, :], fa[:, n:n + 1],
                                            fb[:, n:n + 1], ALU.mult, ALU.add)
                v.drain()
                for n in range(NT):
                    nc.vector.scalar_tensor_tensor(keep.x[:, 4 * b + n, :], A[:, n, :], HG, keep.x[:, 4 * b + n, :],
                                                   ALU.mult, ALU.add)
                v.drain()
                for n in range(NT):
                    v.wait_ge(s_at, 4 * b + n + 1)
                    nc.vector.scalar_tensor_tensor(keep.x[:, 4 * b + n, :], ps_T[n % 2][:, :], HG,
                                                   keep.x[:, 4 * b + n, :], ALU.mult, ALU.add).then_inc(s_blend_t, 1)
                v.drain()
                v.nop().then_inc(s_blend, 1)
                ln.vector(nc, v, b, b)

        @block.tensor
        def _(pe):
            pe.wait_ge(s_ctx, 16)
            pe.wait_ge(s_w0, 32)
            pe.wait_ge(s_id, 1)
            def similarities(b):
                for w, W in enumerate((wq, wk)):
                    after(pe, s_qk, 2 * b + w)
                    nc.tensor.matmul(ps_proj[:, :], W[:, :], ctxT[:, b, :], start=True, stop=True).then_inc(s_qps, 1)
                after(pe, s_qk, 2 * b + 2)
                for n in range(NT):
                    if n >= 2:
                        pe.wait_ge(s_sim, 4 * b + n - 1)
                    nc.tensor.matmul(ps_sim[n % 2][:, :], QT[:, n * P:(n + 1) * P], KT[:, :],
                                     start=True, stop=True).then_inc(s_sps, 1)

            def batch(b, more):
                for hh in range(4):
                    n = 4 * b + hh
                    q = hh % 2
                    pe.wait_ge(s_raw[q], 96 * (2 * b + hh // 2 + 1))
                    after(pe, s_wc, n)
                    for t in range(Q3):
                        last = nc.tensor.matmul(ps_wc[:, 0:R], r_kcq[q][:, t, :], r_qr[q][:, t, :],
                                                start=t == 0, stop=t == Q3 - 1)
                    last.then_inc(s_wcps, 1)
                    after(pe, s_p32, n)
                    nc.tensor.matmul(ps_vo[:, :], r_kckv[q][:, :], r_wo[q][:, :], start=True, stop=True)
                    after(pe, s_wc, n + 1)
                    for k in range(KD):
                        last = nc.tensor.matmul(ps_wq[:, k * R:(k + 1) * R], r_wq[q][:, k * P:(k + 1) * P],
                                                wc[:, :], start=True, stop=True)
                    last.then_inc(s_pps, 1)
                pe.wait_ge(s_bad, b + 1)
                nc.tensor.matmul(ps_bad[0:1, 0:1], bad[:, 0:1], ones[:, 0:1], start=True, stop=True).then_inc(s_badsum, 1)
                if more:
                    similarities(b + 1)
                pe.wait_ge(s_mask, 4 * b + 4)
                for n in range(NT):
                    if n >= 2:
                        pe.wait_ge(s_blend_t, 4 * b + n - 1)
                    for m in range(NT):
                        last = nc.tensor.transpose(ps_T[n % 2][:, m * P:(m + 1) * P],
                                                   A[:, m, n * P:(n + 1) * P], keep.ident[:, :])
                    last.then_inc(s_at, 1)
                pe.wait_ge(s_blend_t, 4 * b + 4)
                ln.tensor(nc, pe, b)

            similarities(0)
            with pe.Fori(0, B - 1) as b:
                batch(b, True)
            batch(B - 1, False)


def stage_router(nc, keep, gate):
    T = B * NT
    with ExitStack() as ctx:
        sc = Scope(nc, ctx)
        s8 = sc.sb("scores8", [P, T, E])
        m8 = sc.sb("sorted8", [P, T, E])
        i8 = sc.sb("index8", [P, T, E], U32)
        if8 = sc.sb("index8f", [P, T, 2])
        iota = sc.sb("iota8", [P, E])
        one = sc.sb("one_hot", [P, T, E])
        two = sc.sb("two_hot", [P, T, E])
        tot = sc.sb("tot", [P, T])
        ps = sc.ps("ps_router")
        s_ps, s_cen, s_exp, s_iota, s_done = (sc.sem(n) for n in ("router_scores", "router_centred", "router_exp",
                                                                  "iota_ready", "router_done"))
        block = ctx.enter_context(nc.Block())

        @block.tensor
        def _(pe):
            with pe.Fori(0, B) as b:
                for n in range(NT):
                    col = ds((4 * b + n) * E, E)
                    last = split_matmuls(nc, ps[:, col],
                                         [(lambda hl, k=k, n=n: keep.xT[:, b, k, hl, n * P:(n + 1) * P],
                                           lambda hl, k=k: keep.gate_w[:, k, hl, :]) for k in range(KD)])
                last.then_inc(s_ps, 1)

        @block.gpsimd
        def _(pool):
            for e in range(E):
                last = nc.gpsimd.memset(iota[:, e:e + 1], float(e))
            last.then_inc(s_iota, 1)

        @block.scalar
        def _(a):
            a.wait_ge(s_cen, 1)
            nc.scalar.activation(s8[:, :, :], s8[:, :, :], ACT.Exp).then_inc(s_exp, 1)

        @block.vector
        def _(v):
            v.wait_ge(s_ps, B)
            nc.vector.tensor_scalar(s8[:, :, :], ps[:, 0:T * E].rearrange("p (t e) -> p t e", e=E), 1.0 / SC, None, ALU.mult)
            nc.vector.memset(gate[:, E:NG0, :], 1.0 / SC)
            v.drain()
            for t in range(T):
                nc.vector.max(m8[:, t, :], s8[:, t, :])
            v.drain()
            for t in range(T):
                nc.vector.max_index(i8[:, t, :], m8[:, t, :], s8[:, t, :])
            v.drain()
            nc.vector.tensor_tensor(s8[:, :, :], s8[:, :, :], m8[:, :, 0:1].to_broadcast([P, T, E]),
                                    ALU.subtract).then_inc(s_cen, 1)
            nc.vector.tensor_copy(if8[:, :, :], i8[:, :, 0:2])
            v.drain()
            v.wait_ge(s_iota, 1)
            it = iota[:, :].unsqueeze(1).to_broadcast([P, T, E])
            nc.vector.tensor_tensor(one[:, :, :], it, if8[:, :, 0:1].to_broadcast([P, T, E]), ALU.is_equal)
            nc.vector.tensor_tensor(two[:, :, :], it, if8[:, :, 1:2].to_broadcast([P, T, E]), ALU.is_equal)
            v.drain()
            nc.vector.tensor_tensor(one[:, :, :], one[:, :, :], two[:, :, :], ALU.add)
            v.wait_ge(s_exp, 1)
            nc.vector.tensor_reduce(tot[:, :], s8[:, :, :], AX.X, ALU.add)
            v.drain()
            nc.vector.tensor_scalar(tot[:, :], tot[:, :], SC, None, ALU.mult)
            v.drain()
            nc.vector.reciprocal(tot[:, :], tot[:, :])
            nc.vector.tensor_tensor(one[:, :, :], one[:, :, :], s8[:, :, :], ALU.mult)
            v.drain()
            nc.vector.tensor_tensor(gate[:, 0:E, :].rearrange("p e t -> p t e"), one[:, :, :],
                                    tot[:, :].unsqueeze(2).to_broadcast([P, T, E]), ALU.mult).then_inc(s_done, 1)


def stage_ffn(nc, keep, tag, w13, w2, NG, NJ, gate):
    HW = NJ * P
    with ExitStack() as ctx:
        sc = Scope(nc, ctx)
        raw = [sc.sb(f"{tag}_raw{i}", [P, NJ * 512]) for i in range(3)]
        wup = [[sc.sb(f"{tag}_w{m}_{par}", [P, 2, KD, HW], FP16) for m in range(2)] for par in range(2)]
        wdn = [sc.sb(f"{tag}_w2_{par}", [P, 2, NJ, D], FP16) for par in range(2)]
        hT = [sc.sb(f"{tag}_hT{par}", [P, NJ, 2, S], FP16) for par in range(2)]
        sg = [sc.sb(f"{tag}_silu{i}", [P, S]) for i in range(2)]
        h32 = sg
        with ExitStack() as ps_ctx:
            ps_scope = Scope(nc, ps_ctx)
            psG = [ps_scope.ps(f"{tag}_psG{i}") for i in range(2)]
            psU = [ps_scope.ps(f"{tag}_psU{i}") for i in range(2)]
            psD = [ps_scope.ps(f"{tag}_psD{i}") for i in range(4)]
            s_raw = [sc.sem(f"{tag}_raw_loaded{i}") for i in range(3)]
            s_whi, s_wlo = sc.sem(f"{tag}_w_hi"), sc.sem(f"{tag}_w_lo")
            s_up, s_silu, s_h32, s_h = (sc.sem(f"{tag}_{n}") for n in ("up", "silu", "h32", "h"))
            s_down, s_acc = sc.sem(f"{tag}_down"), sc.sem(f"{tag}_acc")
            block = ps_ctx.enter_context(nc.Block())

            def flat(t):
                return t.rearrange("p h k n -> p h (k n)")

            def split_dst(par, m):
                return flat((wup[par][m] if m < 2 else wdn[par])[:, :, :, :])

            @block.sync
            def _(sp):
                def load(g, m):
                    if m < 2:
                        src, k = w13[m, g, :, :, :], KD
                    else:
                        src, k = w2[g, :, :, :], NJ
                    sp.dma_start(raw[m][:, :].rearrange("p (k n) -> p k n", k=k), src).then_inc(s_raw[m], 16)

                for m in range(3):
                    load(0, m)
                with sp.Fori(1, NG) as g:
                    for m in range(3):
                        sp.wait_ge(s_wlo, 3 * g - 3 + m + 1)
                        load(g, m)

            def split_hi(a, g, par, m):
                a.wait_ge(s_raw[m], 16 * g + 16)
                nc.scalar.activation(split_dst(par, m)[:, 0, :], raw[m][:, :], ACT.Copy, scale=SC).then_inc(s_whi, 1)

            def split_lo(v, g, par, m):
                v.wait_ge(s_whi, 3 * g + m + 1)
                nc.vector.scalar_tensor_tensor(split_dst(par, m)[:, 1, :], raw[m][:, :], SC, split_dst(par, m)[:, 0, :],
                                               ALU.mult, ALU.subtract).then_inc(s_wlo, 1)

            @block.scalar
            def _(a):
                for m in range(3):
                    split_hi(a, 0, 0, m)

                def pair(i, last):
                    for par in range(2):
                        g = 2 * i + par
                        for b in range(B):
                            u = 4 * g + b
                            for j in range(NJ):
                                n = u * NJ + j
                                a.wait_ge(s_up, n + 1)
                                if not (isinstance(n, int) and n < 2):
                                    a.wait_ge(s_h, n - 1)
                                q = (b * NJ + j) % 2
                                nc.scalar.activation(sg[q][:, :], psG[q][:, :], ACT.Silu, scale=1.0 / SC).then_inc(s_silu, 1)
                            if b >= 1 and not (last and par == 1):
                                if b == 1 and not (isinstance(g, int) and g == 0):
                                    a.wait_ge(s_down, 16 * g)
                                split_hi(a, g + 1, 1 - par, b - 1)

                pair(0, NG == 2)
                if NG > 4:
                    with a.Fori(1, NG // 2 - 1) as i:
                        pair(i, False)
                pair(NG // 2 - 1, True)

            @block.vector
            def _(v):
                for m in range(3):
                    split_lo(v, 0, 0, m)

                def take(u, b):
                    for t in range(NT):
                        v.wait_ge(s_down, 4 * u + t + 1)
                        xs = keep.x[:, 4 * b + t, :]
                        scale = gate[:, ds((u - b) // 4 if isinstance(u, int) else gate_g[0], 1), 4 * b + t] if gate is not None else 1.0 / SC
                        nc.vector.scalar_tensor_tensor(xs, psD[t][:, :], scale, xs, ALU.mult, ALU.add).then_inc(s_acc, 1)

                gate_g = [0]

                def pair(i, last):
                    for par in range(2):
                        g = 2 * i + par
                        for b in range(B):
                            u = 4 * g + b
                            for j in range(NJ):
                                n = u * NJ + j
                                q = (b * NJ + j) % 2
                                v.wait_ge(s_silu, n + 1)
                                nc.vector.scalar_tensor_tensor(h32[q][:, :], psU[q][:, :], 1.0 / SC, sg[q][:, :],
                                                               ALU.mult, ALU.mult).then_inc(s_h32, 1)
                                if j == 0 and not (isinstance(u, int) and u < 2):
                                    v.drain()
                                    v.wait_ge(s_down, 4 * (u - 1))
                                else:
                                    v.drain()
                                hh = hT[b % 2]
                                nc.vector.tensor_copy(hh[:, j, 0, :], h32[q][:, :])
                                v.drain()
                                nc.vector.tensor_tensor(hh[:, j, 1, :], h32[q][:, :], hh[:, j, 0, :],
                                                        ALU.subtract).then_inc(s_h, 1)
                            if b >= 1 and not (last and par == 1):
                                split_lo(v, g + 1, 1 - par, b - 1)
                            if b >= 1:
                                gate_g[0] = g
                                take(u - 1, b - 1)
                            elif not (isinstance(u, int) and u == 0):
                                gate_g[0] = g - 1
                                take(u - 1, B - 1)

                pair(0, NG == 2)
                if NG > 4:
                    with v.Fori(1, NG // 2 - 1) as i:
                        pair(i, False)
                pair(NG // 2 - 1, True)
                gate_g[0] = NG - 1
                take(4 * NG - 1, B - 1)

            @block.tensor
            def _(pe):
                def up(u, g, par, b):
                    if b == 0:
                        pe.wait_ge(s_wlo, 3 * g + 2)
                    for j in range(NJ):
                        n = u * NJ + j
                        q = (b * NJ + j) % 2
                        if not (isinstance(n, int) and n < 2):
                            pe.wait_ge(s_h32, n - 1)
                        for m, bank in enumerate((psG, psU)):
                            w = wup[par][m]
                            last = split_matmuls(nc, bank[q][:, :],
                                                 [(lambda hl, k=k: w[:, hl, k, j * P:(j + 1) * P],
                                                   lambda hl, k=k: keep.xT[:, b, k, hl, :]) for k in range(KD)])
                        last.then_inc(s_up, 1)

                def down(u, g, par, b):
                    if b == 0:
                        pe.wait_ge(s_wlo, 3 * g + 3)
                    pe.wait_ge(s_h, NJ * (u + 1))
                    for t in range(NT):
                        if not (isinstance(u, int) and u == 0):
                            pe.wait_ge(s_acc, 4 * (u - 1) + t + 1)
                        split_matmuls(nc, psD[t][:, :],
                                      [(lambda hl, j=j: hT[b % 2][:, j, hl, t * P:(t + 1) * P],
                                        lambda hl, j=j: wdn[par][:, hl, j, :]) for j in range(NJ)]).then_inc(s_down, 1)

                def pair(i, last):
                    for par in range(2):
                        g = 2 * i + par
                        for b in range(B):
                            u = 4 * g + b
                            if b < B - 1:
                                up(u + 1, g, par, b + 1)
                            elif not (last and par == 1):
                                up(u + 1, g + 1, 1 - par, 0)
                            down(u, g, par, b)

                up(0, 0, 0, 0)
                pair(0, NG == 2)
                if NG > 4:
                    with pe.Fori(1, NG // 2 - 1) as i:
                        pair(i, False)
                pair(NG // 2 - 1, True)


def stage_norm(nc, keep, tag):
    with ExitStack() as ctx:
        sc = Scope(nc, ctx)
        xn = [sc.sb(f"{tag}_xn{i}", [P, D]) for i in range(2)]
        ps_T = [sc.ps(f"{tag}_psT{i}") for i in range(2)]
        ln = LayerNorm(sc, keep, tag, xn, ps_T)
        block = ctx.enter_context(nc.Block())

        @block.sync
        def _(sp):
            start_at_one(sp, ln.s_lo)

        @block.scalar
        def _(a):
            with a.Fori(0, B) as b:
                ln.scalar(nc, a, b, b)

        @block.vector
        def _(v):
            with v.Fori(0, B) as b:
                ln.vector(nc, v, b, b)

        @block.tensor
        def _(pe):
            with pe.Fori(0, B) as b:
                after(pe, ln.s_lo, 4 * b)
                ln.tensor(nc, pe, b)


def stage_attention(nc, keep):
    with ExitStack() as ctx:
        sc = Scope(nc, ctx)
        Q = [sc.sb(f"Q{i}", [P, S], FP16) for i in range(4)]
        KH = [sc.sb(f"KH{i}", [P, S], FP16) for i in range(2)]
        KL = [sc.sb(f"KL{i}", [P, S], FP16) for i in range(2)]
        p32 = [sc.sb(f"p32_{i}", [P, S]) for i in range(2)]
        pn = [sc.sb(f"pn{i}", [P, 2, S], FP16) for i in range(4)]
        pT = [sc.sb(f"pT{i}", [P, 2, NT, S], FP16) for i in range(2)]
        cx = sc.sb("cx", [P, 2, H, S], FP16)
        nmx = sc.sb("nmx", [P, NT])
        rsum, rinv = sc.sb("rsum", [P, NT]), sc.sb("rinv", [P, NT])
        psQ, psK = sc.ps("psQ"), sc.ps("psK")
        psC = [sc.ps(f"psC{i}") for i in range(2)]
        psO = [psQ, psK]
        psS = [sc.ps(f"psS{i}") for i in range(2)]
        psP = [sc.ps(f"psP{i}", (P, 2, NT, P), FP16) for i in range(2)]
        (s_qps, s_kps, s_qhi, s_qlo, s_khi, s_klo, s_S, s_max, s_exp, s_pn, s_T, s_ev, s_ctx, s_chi, s_clo, s_out,
         s_acc) = (sc.sem("at_" + n) for n in (
             "q_in_psum", "k_in_psum", "q_hi", "q_lo", "k_hi", "k_lo", "scores", "max", "exp", "probs",
             "probs_transposed", "probsT", "ctx", "ctx_hi", "ctx_lo", "out", "acc"))
        ln = LayerNorm(sc, keep, "ln3", p32, psS)
        block = ctx.enter_context(nc.Block())
        first = lambda s: isinstance(s, int) and s == 0

        def steps(eng, prologue, step, epilogue):
            with eng.Fori(0, B) as b:
                prologue(b)
                for c in range(3):
                    step(b, 0, c)
                with eng.Fori(0, 3) as i:
                    for c in range(3, 7):
                        step(b, i, c)
                for c in range(15, 18):
                    step(b, 0, c)
                epilogue(b)

        def has(s, what, st=0):
            if not isinstance(s, int):
                return True
            j = 4 * s + st - 3
            return {"next": s < H - 1, "scores": s < H, "transpose": 0 <= j < 4 * H, "ctx": s >= 2, "ctx_lo": s >= 3}[what]

        @block.sync
        def _(sp):
            start_at_one(sp, s_qlo, s_klo, s_exp, s_ev, s_ctx, s_clo, s_out, s_acc, s_S, s_pn, s_T, ln.s_lo)

        @block.tensor
        def _(pe):
            def project(b, i, c):
                s, sm = 4 * i + c, c % 4
                if sm % 2 == 0:
                    pair = 2 * i + c // 2
                    after(pe, s_qlo, 8 * b + pair)
                    split_matmuls(nc, psQ[:, :], [(lambda hl, k=k: keep.wqc[:, k, hl, ds(pair * 2 * R, 2 * R)],
                                                   lambda hl, k=k: keep.xT[:, b, k, hl, :])
                                                  for k in range(KD)]).then_inc(s_qps, 1)
                after(pe, s_klo, 16 * b + s)
                split_matmuls(nc, psK[:, :], [(lambda hl: keep.wkr[:, hl, s, :, :].rearrange("p a r -> p (a r)"),
                                               lambda hl: keep.kvs[:, 0, b, hl, :])]).then_inc(s_kps, 1)

            def step(b, i, c):
                s, sm = 4 * i + c, c % 4
                for st in range(NT):
                    jj = 64 * b + 4 * s + st
                    if has(s, "scores"):
                        if st == 0:
                            after(pe, s_klo, 16 * b + s + 1)
                            after(pe, s_qlo, 8 * b + 2 * i + c // 2 + 1)
                        if first(s) and st < 2:
                            after(pe, s_exp, 64 * b)
                            after(pe, ln.s_lo, 4 * b)
                        else:
                            after(pe, s_exp, jj - 1)
                        q = Q[sm][:, st * P:(st + 1) * P]
                        nc.tensor.matmul(psS[st % 2][:, :], q, KH[sm % 2][:, :], start=True, stop=False)
                        nc.tensor.matmul(psS[st % 2][:, :], q, KL[sm % 2][:, :], start=False, stop=True).then_inc(s_S, 1)
                    if has(s, "transpose", st):
                        jt, t = jj - 3, (st + 1) % 4
                        after(pe, s_pn, jt + 1)
                        if first(s) or (isinstance(s, int) and s == 1 and st == 0):
                            after(pe, s_ev, 64 * b)
                        else:
                            after(pe, s_ev, jt - 1)
                        for hl in range(2):
                            for l in range(NT):
                                last = nc.tensor.transpose(psP[t % 2][:, hl, l, :], pn[t][:, hl, l * P:(l + 1) * P],
                                                           keep.ident16[:, :])
                        last.then_inc(s_T, 1)
                    if has(s, "ctx") and st < 3:
                        h = s - 2
                        if st == 0:
                            after(pe, s_ev, 64 * b + 4 * h + 4)
                            if isinstance(h, int) and h < 2:
                                after(pe, s_clo, 16 * b)
                            else:
                                after(pe, s_clo, 16 * b + h - 1)
                        for l in ((0,), (1,), (2, 3))[st]:
                            kt = lambda hl: keep.kvs[:, 1, b, hl, l * P:(l + 1) * P]
                            pt = lambda hl: pT[sm % 2][:, hl, l, :]
                            nc.tensor.matmul(psC[c % 2][:, :], kt(0), pt(0), start=l == 0, stop=False)
                            nc.tensor.matmul(psC[c % 2][:, :], kt(0), pt(1), start=False, stop=False)
                            last = nc.tensor.matmul(psC[c % 2][:, :], kt(1), pt(0), start=False, stop=l == 3)
                        if st == 2:
                            last.then_inc(s_ctx, 1)
                    if st == 0 and has(s, "next"):
                        project(b, i, c + 1)

            def epilogue(b):
                after(pe, s_clo, 16 * b + 16)
                for t in range(NT):
                    if t >= 2:
                        after(pe, s_acc, 4 * b + t - 1)
                    split_matmuls(nc, psO[t % 2][:, :], [(lambda hl, h=h: cx[:, hl, h, t * P:(t + 1) * P],
                                                   lambda hl, h=h: keep.wvo[:, hl, h, :])
                                                  for h in range(H)]).then_inc(s_out, 1)
                ln.tensor(nc, pe, b)

            steps(pe, lambda b: project(b, 0, 0), step, epilogue)

        @block.scalar
        def _(a):
            def project(b, i, c):
                s, sm = 4 * i + c, c % 4
                if sm % 2 == 0:
                    pair = 2 * i + c // 2
                    a.wait_ge(s_qps, 8 * b + pair + 1)
                    if first(s):
                        after(a, s_S, 64 * b)
                    else:
                        after(a, s_S, 64 * b + 8 * pair - 8)
                    nc.scalar.activation(Q[sm][0:R, :], psQ[0:R, :], ACT.Copy, scale=1.0 / SC)
                    nc.scalar.activation(Q[sm + 1][R:P, :], psQ[R:P, :], ACT.Copy, scale=1.0 / SC).then_inc(s_qhi, 1)
                a.wait_ge(s_kps, 16 * b + s + 1)
                if first(s):
                    after(a, s_S, 64 * b)
                else:
                    after(a, s_S, 64 * b + 4 * s - 4)
                nc.scalar.activation(KH[sm % 2][:, :], psK[:, :], ACT.Copy, scale=1.0 / SC).then_inc(s_khi, 1)

            def step(b, i, c):
                s, sm = 4 * i + c, c % 4
                for st in range(NT):
                    jj = 64 * b + 4 * s + st
                    if has(s, "scores"):
                        a.wait_ge(s_max, jj + 1)
                        if first(s) and st < 2:
                            after(a, s_pn, 64 * b)
                        else:
                            after(a, s_pn, jj - 1)
                        nc.scalar.activation(p32[st % 2][:, :], psS[st % 2][:, :], ACT.Exp, bias=nmx[:, st:st + 1],
                                             accum_out=rsum[:, st:st + 1]).then_inc(s_exp, 1)
                    if has(s, "transpose", st):
                        jt, t = jj - 3, (st + 1) % 4
                        hp = (sm if st == 3 else sm + 1) % 2
                        after(a, s_T, jt + 1)
                        if t == 0:
                            if isinstance(s, int) and s < 2:
                                after(a, s_ctx, 16 * b)
                            else:
                                after(a, s_ctx, 16 * b + s - 1)
                        nc.scalar.activation(pT[hp][:, :, :, t * P:(t + 1) * P], psP[t % 2][:, :, :, :],
                                             ACT.Copy).then_inc(s_ev, 1)
                    if st == 1 and has(s, "next"):
                        project(b, i, c + 1)
                if has(s, "ctx"):
                    h = s - 2
                    after(a, s_ctx, 16 * b + h + 1)
                    if isinstance(h, int) and h == 0:
                        after(a, s_out, 4 * b)
                    nc.scalar.activation(cx[:, 0, h, :], psC[c % 2][:, :], ACT.Copy, scale=1.0 / PSC).then_inc(s_chi, 1)

            steps(a, lambda b: project(b, 0, 0), step, lambda b: ln.scalar(nc, a, b, b))

        @block.vector
        def _(v):
            def project(b, i, c):
                s, sm = 4 * i + c, c % 4
                if sm % 2 == 0:
                    pair = 2 * i + c // 2
                    v.wait_ge(s_qhi, 8 * b + pair + 1)
                    nc.vector.scalar_tensor_tensor(Q[sm][R:P, :], psQ[0:R, :], 1.0 / SC, Q[sm][0:R, :],
                                                   ALU.mult, ALU.subtract)
                    nc.vector.scalar_tensor_tensor(Q[sm + 1][0:R, :], psQ[R:P, :], 1.0 / SC, Q[sm + 1][R:P, :],
                                                   ALU.mult, ALU.subtract).then_inc(s_qlo, 1)
                v.wait_ge(s_khi, 16 * b + s + 1)
                nc.vector.scalar_tensor_tensor(KL[sm % 2][:, :], psK[:, :], 1.0 / SC, KH[sm % 2][:, :],
                                               ALU.mult, ALU.subtract).then_inc(s_klo, 1)

            def context_lo(b, h, q):
                v.wait_ge(s_chi, 16 * b + h + 1)
                nc.vector.scalar_tensor_tensor(cx[:, 1, h, :], psC[q][:, :], 1.0 / PSC, cx[:, 0, h, :],
                                               ALU.mult, ALU.subtract).then_inc(s_clo, 1)

            def normalise(b, s, st):
                jj = 64 * b + 4 * s + st
                after(v, s_exp, jj + 1)
                if first(s):
                    after(v, s_T, 64 * b)
                else:
                    after(v, s_T, jj - 3)
                r = rinv[:, st:st + 1]
                nc.vector.tensor_scalar(r, rsum[:, st:st + 1], 1.0 / PSC, None, ALU.mult)
                v.drain()
                nc.vector.reciprocal(r, r)
                v.drain()
                nc.vector.tensor_scalar(pn[st][:, 0, :], p32[st % 2][:, :], r, None, ALU.mult)
                v.drain()
                nc.vector.scalar_tensor_tensor(pn[st][:, 1, :], p32[st % 2][:, :], r, pn[st][:, 0, :],
                                               ALU.mult, ALU.subtract).then_inc(s_pn, 1)

            def step(b, i, c):
                s, sm = 4 * i + c, c % 4
                for st in range(NT):
                    if has(s, "scores"):
                        after(v, s_S, 64 * b + 4 * s + st + 1)
                        nc.vector.tensor_reduce(nmx[:, st:st + 1], psS[st % 2][:, :], AX.X, ALU.max,
                                                negate=True).then_inc(s_max, 1)
                    if st >= 1 and has(s, "scores"):
                        normalise(b, s, st - 1)
                    elif st == 0 and not first(s) and not (isinstance(s, int) and s > H):
                        normalise(b, s - 1, NT - 1)
                    if st == 0 and has(s, "ctx_lo"):
                        context_lo(b, s - 3, (c - 3) % 2)
                    if st == 2 and has(s, "next"):
                        project(b, i, c + 1)

            def epilogue(b):
                context_lo(b, H - 1, (H - 1) % 2)
                for t in range(NT):
                    after(v, s_out, 4 * b + t + 1)
                    xs = keep.x[:, 4 * b + t, :]
                    nc.vector.scalar_tensor_tensor(xs, psO[t % 2][:, :], 1.0 / SC, xs, ALU.mult, ALU.add).then_inc(s_acc, 1)
                v.drain()
                ln.vector(nc, v, b, b)

            steps(v, lambda b: project(b, 0, 0), step, epilogue)


def stage_store(nc, keep, out):
    with ExitStack() as ctx:
        sc = Scope(nc, ctx)
        s_out = sc.sem("stored")
        block = ctx.enter_context(nc.Block())

        @block.sync
        def _(sp):
            for b in range(B):
                sp.dma_start(out[b, :, :].rearrange("(t p) n -> p t n", p=P),
                             keep.x[:, 4 * b:4 * b + 4, :]).then_inc(s_out, 16)
            sp.wait_ge(s_out, 16 * B)


def build(nc, d, out, stages=9):
    with ExitStack() as ctx:
        sc = Scope(nc, ctx)
        keep = Keep(sc)
        with ExitStack() as c1:
            keep.attention(Scope(nc, c1))
            stage_adjacency(nc, keep, d)
            if stages >= 2:
                with ExitStack() as c2:
                    gate = Scope(nc, c2).sb("gate", [P, NG0, B * NT])
                    stage_router(nc, keep, gate)
                    stage_ffn(nc, keep, "f0", d["w13_0"], d["w2_0"], NG0, NJ0, gate)
            if stages >= 3:
                stage_norm(nc, keep, "ln2")
                stage_attention(nc, keep)
        if stages >= 4:
            stage_ffn(nc, keep, "f1", d["w13_1"], d["w2_1"], NG1, NJ1, None)
        stage_store(nc, keep, out)


def layout(i):
    import numpy as np

    f = np.float32

    def c(a):
        return np.ascontiguousarray(a)

    def swap(a):
        return np.concatenate([a[..., C // 2:], a[..., :C // 2]], axis=-1)

    def major(a):
        a = a.reshape(*a.shape[:-2], a.shape[-2] // P, P, a.shape[-1])
        return c(np.swapaxes(a, -3, -2))

    d = {}
    d["x"] = c(i["x"]).reshape(B * S, D)
    ctx = np.asarray(i["ctx_512"])
    ctxT = np.swapaxes(ctx, 1, 2)
    d["ctxT"] = c(ctxT)
    rot = swap(ctx)
    tok = lambda a: major(a).reshape(*a.shape[:-2], P, S)
    d["ctx_both"] = c(np.stack([ctxT, tok(ctx)]))
    d["ctx_rot"] = c(np.stack([np.swapaxes(rot, 1, 2), tok(rot)]))
    inv = (f(1.0) / np.power(f(10000.0), np.arange(0, C, 2, dtype=f) / f(C))).astype(f)
    ang = np.arange(S, dtype=f)[:, None] * inv[None, :]
    sin, cos = np.repeat(np.sin(ang), 2, axis=-1), np.repeat(np.cos(ang), 2, axis=-1)
    sin = np.concatenate([-sin[:, :C // 2], sin[:, C // 2:]], axis=-1)
    d["rope_cos"] = c(np.stack([cos.T, tok(cos)])).astype(f)
    d["rope_sin"] = c(np.stack([sin.T, tok(sin)])).astype(f)
    d["wq0T"], d["wk0T"] = c(np.asarray(i["L0_xattn_Wq"]).T), c(np.asarray(i["L0_xattn_Wk"]).T)
    d["gamma"] = c(np.broadcast_to(np.asarray(i["L0_xattn_gamma_raw"]).reshape(1, 1), (P, 1)))
    d["gate_wT"] = c(np.asarray(i["L0_ffn_gate_w"]).T)
    d["wq1"] = c(i["L1_xattn_Wq"])
    d["kcqT"] = c(np.swapaxes(np.asarray(i["L1_xattn_w_kc_q"]), 1, 2))
    d["wqr"] = c(i["L1_xattn_W_qr"])
    d["kckv"] = c(i["L1_xattn_w_kc_kv"])
    d["wkr"] = c(i["L1_xattn_W_kr"])
    d["woT"] = c(np.asarray(i["L1_xattn_Wo"]).T)

    def hidden_groups(w, n):
        out = np.zeros((w.shape[0], n, w.shape[2]), w.dtype)
        out[:, :w.shape[1]] = w
        return out

    def ffn(wg, wu, wd, n):
        up = [major(np.swapaxes(hidden_groups(w, n), 1, 2)) for w in (wg, wu)]
        return c(np.stack(up)), major(hidden_groups(np.swapaxes(wd, 1, 2), n))

    g = lambda a: np.asarray(i["L0_ffn_" + a])
    he = g("w1").shape[1]
    both = [np.concatenate([g(r), g(s).reshape(2, he, D)]) for r, s in (("w1", "sw1"), ("w3", "sw3"))]
    down = np.concatenate([g("w2"), np.swapaxes(g("sw2").reshape(D, 2, he), 0, 1)])
    d["w13_0"], d["w2_0"] = ffn(*both, down, NJ0 * P)
    l = lambda a: np.asarray(i["L1_ffn_" + a])
    hw = NJ1 * P
    d["w13_1"], d["w2_1"] = ffn(l("w_gate").reshape(NG1, hw, D), l("w_up").reshape(NG1, hw, D),
                                np.swapaxes(l("w_down").reshape(D, NG1, hw), 0, 1), hw)
    return d


def kernel(**inputs):
    import concourse.bacc as _bacc
    from concourse.bass_utils import run_bass_kernel_spmd as _run

    nc = _bacc.Bacc("TRN2", target_bir_lowering=False, num_devices=1)
    arrays, aps = {}, {}
    for name, a in layout(inputs).items():
        arrays[f"in_{name}"] = a
        aps[name] = nc.dram_tensor(f"in_{name}", a.shape, mybir.dt.from_np(a.dtype), kind="ExternalInput").ap()
    out = nc.dram_tensor("out", (B, S, D), FP32, kind="ExternalOutput").ap()
    build(nc, aps, out, STAGES)
    return _run(nc, [arrays], core_ids=[0]).results[0]["out"]


STAGES = 9
```

```python
import concourse.bass as bass
from concourse import mybir
from contextlib import ExitStack

FP32 = mybir.dt.float32
FP16 = mybir.dt.float16
U32 = mybir.dt.uint32
ALU = mybir.AluOpType
ACT = mybir.ActivationFunctionType
AX = mybir.AxisListType

P = 128
B, S, D = 4, 512, 512
KD = D // P
NT = S // P
C = 128
TOPK = int(S * 0.3)
EPS = 1e-5
E = 8
HE = 384
HV = 352
NS, NJ0 = 2, 3
TILES = 2 * B * NT + E
NG1, NJ1 = 4, 4
H, R, Q3 = 16, 64, 3
HG = 4
SC = 64.0
PSC = 1024.0
PROBES = 4
TARGET = TOPK - 4.5
Z_TARGET = 0.527
DENSITY = 178.0
FAR = 3.0e38
BISECT = 30


def ds(start, size):
    return bass.ds(start, size)


def start_at_one(eng, *sems):
    for s in sems:
        eng.nop().then_inc(s, 1)


def after(eng, sem, n):
    eng.wait_ge(sem, n + 1)


class Scope:

    def __init__(self, nc, ctx):
        self.nc, self.ctx = nc, ctx

    def sb(self, name, shape, dt=FP32):
        return self.ctx.enter_context(self.nc.sbuf_tensor(name, shape, dt))

    def ps(self, name, shape=(P, 512), dt=FP32):
        return self.ctx.enter_context(self.nc.psum_tensor(name, list(shape), dt))

    def sem(self, name):
        return self.ctx.enter_context(self.nc.semaphore(name))


class LayerNorm:

    def __init__(self, sc, keep, tag, xn, psT, mv=None, rstd=None):
        self.k, self.xn, self.psT = keep, xn, psT
        self.st = sc.sb(f"{tag}_stats", [P, NT, 6])
        self.mv, self.std, self.rstd = sc.sb(f"{tag}_meanvar", [P, NT, 2]), sc.sb(f"{tag}_std", [P, NT]), sc.sb(f"{tag}_rstd", [P, NT])
        self.all_mv, self.all_rstd = mv, rstd
        self.s_var = sc.sem(f"{tag}_var_ready")
        self.s_std = sc.sem(f"{tag}_std_ready")
        self.s_xn = sc.sem(f"{tag}_xn_ready")
        self.s_xt = sc.sem(f"{tag}_transposed")
        self.s_hi = sc.sem(f"{tag}_hi_ready")
        self.s_lo = sc.sem(f"{tag}_lo_ready")

    def stats(self, nc, v, b):
        for n in range(NT):
            nc.vector.bn_stats(self.st[:, n, :], self.k.x[:, 4 * b + n, :])
        nc.vector.drain()
        for n in range(NT):
            last = nc.vector.bn_aggr(self.mv[:, n, :], self.st[:, n, :])
        last.then_inc(self.s_var, 1)

    def root(self, nc, a, b, done):
        a.wait_ge(self.s_var, done + 1)
        nc.scalar.activation(self.std[:, :], self.mv[:, :, 1], ACT.Sqrt,
                             bias=self.k.eps[:, 0:1]).then_inc(self.s_std, 1)

    def inverse(self, nc, v, b, done):
        v.wait_ge(self.s_std, done + 1)
        nc.vector.reciprocal(self.rstd[:, :], self.std[:, :])
        nc.vector.drain()
        if self.all_mv is not None:
            nc.vector.tensor_copy(self.all_mv[:, ds(4 * b, NT), :], self.mv[:, :, :])
            nc.vector.tensor_copy(self.all_rstd[:, ds(4 * b, NT)], self.rstd[:, :])

    def vector(self, nc, v, b, done):
        self.stats(nc, v, b)
        self.inverse(nc, v, b, done)
        for n in range(NT + 1):
            if n < NT:
                if n >= 2:
                    v.wait_ge(self.s_xt, 4 * done + n - 1)
                nc.vector.tensor_scalar(self.xn[n % 2][:, :], self.k.x[:, 4 * b + n, :], self.mv[:, n, 0:1],
                                        self.rstd[:, n:n + 1], ALU.subtract, ALU.mult).then_inc(self.s_xn, 1)
            if n >= 1:
                m = n - 1
                v.wait_ge(self.s_hi, 4 * done + m + 1)
                nc.vector.tensor_tensor(self.k.xT[:, b, :, 1, m * P:(m + 1) * P],
                                        self.psT[m % 2][:, :].rearrange("p (k t) -> p k t", k=KD),
                                        self.k.xT[:, b, :, 0, m * P:(m + 1) * P],
                                        ALU.subtract).then_inc(self.s_lo, 1)

    def rows(self, nc, v, b, waits=True):
        self.inverse(nc, v, b, b)
        for n in range(NT):
            if waits and b > 0:
                v.wait_ge(self.s_xt, 4 * b - 3 + n)
            nc.vector.tensor_scalar(self.xn[n][:, :], self.k.x[:, 4 * b + n, :], self.mv[:, n, 0:1],
                                    self.rstd[:, n:n + 1], ALU.subtract, ALU.mult).then_inc(self.s_xn, 1)

    def highs(self, nc, a, b):
        for n in range(NT):
            a.wait_ge(self.s_xt, 4 * b + n + 1)
            nc.scalar.activation(self.k.xT[:, b, :, 0, n * P:(n + 1) * P],
                                 self.psT[n][:, :].rearrange("p (k t) -> p k t", k=KD),
                                 ACT.Copy).then_inc(self.s_hi, 1)

    def lows(self, nc, v, b):
        for n in range(NT):
            v.wait_ge(self.s_hi, 4 * b + n + 1)
            nc.vector.tensor_tensor(self.k.xT[:, b, :, 1, n * P:(n + 1) * P],
                                    self.psT[n][:, :].rearrange("p (k t) -> p k t", k=KD),
                                    self.k.xT[:, b, :, 0, n * P:(n + 1) * P],
                                    ALU.subtract).then_inc(self.s_lo, 1)

    def transposes(self, nc, pe, b, waits=True):
        for n in range(NT):
            pe.wait_ge(self.s_xn, 4 * b + n + 1)
            if waits and b > 0:
                pe.wait_ge(self.s_lo, 4 * b - 3 + n)
            for k in range(KD):
                last = nc.tensor.transpose(self.psT[n][:, k * P:(k + 1) * P],
                                           self.xn[n][:, k * P:(k + 1) * P], self.k.ident[:, :])
            last.then_inc(self.s_xt, 1)

    def scalar(self, nc, a, b, done):
        self.root(nc, a, b, done)
        for n in range(NT):
            a.wait_ge(self.s_xt, 4 * done + n + 1)
            nc.scalar.activation(self.k.xT[:, b, :, 0, n * P:(n + 1) * P],
                                 self.psT[n % 2][:, :].rearrange("p (k t) -> p k t", k=KD),
                                 ACT.Copy).then_inc(self.s_hi, 1)

    def tensor(self, nc, pe, done):
        for n in range(NT):
            pe.wait_ge(self.s_xn, 4 * done + n + 1)
            if n >= 2:
                after(pe, self.s_lo, 4 * done + n - 1)
            for k in range(KD):
                last = nc.tensor.transpose(self.psT[n % 2][:, k * P:(k + 1) * P],
                                           self.xn[n % 2][:, k * P:(k + 1) * P], self.k.ident[:, :])
            last.then_inc(self.s_xt, 1)


def split_matmuls(nc, out, pairs):
    n = len(pairs)
    for i, (lhs, rhs) in enumerate(pairs):
        nc.tensor.matmul(out, lhs(0), rhs(0), start=i == 0, stop=False)
        nc.tensor.matmul(out, lhs(0), rhs(1), start=False, stop=False)
        last = nc.tensor.matmul(out, lhs(1), rhs(0), start=False, stop=i == n - 1)
    return last


class Keep:

    def __init__(self, sc):
        self.x = sc.sb("x", [P, B * NT, D])
        self.ident = sc.sb("ident", [P, P])
        self.ident16 = sc.sb("ident16", [P, P], FP16)
        self.eps = sc.sb("eps", [P, 1])
        self.place = sc.sb("place_in_experts", [P, 2, B * NT], U32)
        self.gates = sc.sb("gates", [P, 2, B * NT])
        self.tile_expert = sc.sb("tile_expert", [P, TILES], mybir.dt.int32)

    def normed(self, sc, tag):
        self.xT = sc.sb(f"xT_{tag}", [P, B, KD, 2, S], FP16)

    def attention(self, sc):
        self.wvo = sc.sb("wvo", [P, H, 2, D], FP16)
        self.wqc = sc.sb("wqc", [P, H // 2, KD, 2, 2 * R], FP16)
        self.wkr = sc.sb("wkr", [P, H, 2, 2 * R], FP16)
        self.kvs = sc.sb("kvs", [P, 2 * B, 2, S], FP16)


class Scratch:

    def __init__(self, nc):
        t = lambda name, shape, dt: nc.dram_tensor(name, shape, dt).ap()
        self.wqc = t("wqc_scratch", (H // 2, P, KD * 2 * 2 * R), FP16)
        self.wvo = t("wvo_scratch", (H, P, 2 * D), FP16)
        self.wkr = t("wkr_scratch", (H, P, 4 * R), FP16)
        self.kvs = t("kvs_scratch", (2 * B, P, 2 * S), FP16)
        self.xs = t("expert_inputs", (TILES * P, D), FP32)
        self.ys = t("expert_outputs", (TILES * P, D), FP32)


def stage_adjacency(nc, keep, d, scratch, gate_w, mv1, rstd1):
    with ExitStack() as ctx:
        sc = Scope(nc, ctx)
        ctxT = sc.sb("ctxT", [P, B, S])
        wq, wk = sc.sb("wq0", [P, P]), sc.sb("wk0", [P, P])
        gam = sc.sb("gam", [P, 8])
        GR, GS, OMG, HG = (gam[:, i:i + 1] for i in range(4))
        gate_raw = sc.sb("gate_raw", [P, KD, E])
        gate32 = sc.sb("gate32", [P, KD, E])
        QT, KT = sc.sb("QT", [P, S]), sc.sb("KT", [P, S])
        sim = sc.sb("sim", [P, 2, NT, S])
        A = sc.sb("A", [P, NT, S])
        hit = sc.sb("hit", [P, NT, S], mybir.dt.uint8)
        rest = sc.sb("rest", [P, NT, D])
        xn = [rest[:, i, :] for i in range(NT)]
        lo_t = sc.sb("lo_t", [P, NT])
        step = sc.sb("step", [P, NT])
        probe = sc.sb("probe", [P, NT])
        cnt = sc.sb("cnt", [P, NT])
        top = sc.sb("top", [P, NT])
        st1 = sc.sb("st1", [P, NT, 6])
        mvs = sc.sb("mvs", [P, NT, 2])
        sds = sc.sb("sds", [P, NT])
        cur, low2, high2, dif = (sc.sb(n, [P, 2, NT]) for n in ("cur", "low2", "high2", "dif"))
        off, nxt = sc.sb("off", [P, NT]), sc.sb("nxt", [P, NT])
        above, below, miss = (sc.sb(n, [P, NT], U32) for n in ("above", "below", "miss"))
        eight, pick = sc.sb("eight", [P, NT, 8]), sc.sb("pick", [P, NT, 8])
        place = sc.sb("place", [P, 8])
        bad, badi = sc.sb("bad", [P, 1]), sc.sb("badi", [1, 1], mybir.dt.int32)
        ones = sc.sb("ones", [P, 1])
        fa, fb = sc.sb("fa", [P, NT]), sc.sb("fb", [P, NT])
        st0 = sc.sb("st0", [P, NT, 6])
        mv0 = sc.sb("mv0", [P, NT, 2])
        std0, rstd0 = sc.sb("std0", [P, NT]), sc.sb("rstd0", [P, NT])
        r_wq = [sc.sb(f"r_wq{i}", [P, D]) for i in range(2)]
        r_kcq = [sc.sb(f"r_kcq{i}", [P, Q3, P]) for i in range(2)]
        r_qr = [sc.sb(f"r_qr{i}", [P, Q3, R]) for i in range(2)]
        r_kckv = [sc.sb(f"r_kckv{i}", [P, C]) for i in range(2)]
        r_wo = [sc.sb(f"r_wo{i}", [P, D]) for i in range(2)]
        r_kr = [sc.sb(f"r_kr{i}", [P, R]) for i in range(2)]
        wc = sc.sb("wc", [P, R])
        st_q = [sc.sb(f"st_q{i}", [P, KD, 2, 2, R], FP16) for i in range(2)]
        st_v = [sc.sb(f"st_v{i}", [P, 2, 2, D], FP16) for i in range(2)]
        st_k = [sc.sb(f"st_k{i}", [P, 2, 2, 2, R], FP16) for i in range(2)]
        st_c = [sc.sb(f"st_c{i}", [P, 2, S], FP16) for i in range(2)]
        zeros = sc.sb("zeros", [P, D])
        c_q, c_vo, c_kr = sc.sb("c_q", [P, KD, R]), sc.sb("c_vo", [P, D]), sc.sb("c_kr", [P, R])
        cos = sc.sb("cos", [P, S])
        sin = sc.sb("sin", [P, S])
        craw, crot = sc.sb("craw", [P, S]), sc.sb("crot", [P, S])
        rope = craw

        ps_proj = sc.ps("ps_proj")
        ps_sim = [sc.ps(f"ps_sim{i}") for i in range(2)]
        ps_T = [sc.ps(f"ps_T{i}") for i in range(2)]
        ps_wc = sc.ps("ps_wc")
        ps_wq = sc.ps("ps_wq")
        ps_vo = sc.ps("ps_vo")
        ps_bad = ps_wc
        ln = LayerNorm(sc, keep, "ln1", xn, ps_T + ps_sim, mv1, rstd1)

        s_ctx, s_w0, s_x = sc.sem("ctx_loaded"), sc.sem("w0_loaded"), sc.sem("x_loaded")
        s_gam, s_gw = sc.sem("gamma_loaded"), sc.sem("gate_loaded")
        s_id = sc.sem("ident_built")
        s_const = sc.sem("constants_built")
        s_sig = sc.sem("gamma_sigmoid")
        s_qps, s_qk = sc.sem("proj_in_psum"), sc.sem("proj_in_sbuf")
        s_sps, s_sim = sc.sem("sim_in_psum"), sc.sem("sim_in_sbuf")
        s_sgm, s_mask, s_at = sc.sem("sigmoid_done"), sc.sem("masked"), sc.sem("A_transposed")
        s_blend, s_blend_t = sc.sem("blended"), sc.sem("blended_tile")
        s_var0, s_std0 = sc.sem("var0_ready"), sc.sem("std0_ready")
        s_raw = [sc.sem(f"prep_raw{i}") for i in range(2)]
        s_wcps, s_wc = sc.sem("wc_in_psum"), sc.sem("wc_in_sbuf")
        s_pps, s_p32 = sc.sem("prep_in_psum"), sc.sem("prep_in_sbuf")
        s_phi, s_plo = sc.sem("prep_hi"), sc.sem("prep_lo")
        s_rope_in, s_rope, s_rhi, s_rlo = sc.sem("rope_in"), sc.sem("rope_done"), sc.sem("rope_hi"), sc.sem("rope_lo")
        s_tab = sc.sem("rope_tables")
        s_gate = sc.sem("gate_split")
        s_wst = [sc.sem(f"weights_stored{i}") for i in range(2)]
        s_cst = [sc.sem(f"context_stored{i}") for i in range(2)]
        s_zero, s_zst = sc.sem("zeros_ready"), sc.sem("zeros_stored")
        s_vars, s_sds = sc.sem("row_var"), sc.sem("row_sd")
        s_bad, s_badsum = sc.sem("bad_rows"), sc.sem("bad_rows_summed")

        block = ctx.enter_context(nc.Block())

        @block.sync
        def _(sp):
            start_at_one(sp, ln.s_lo, s_phi, s_rhi, s_blend, s_qk, s_wc, s_plo, s_p32, *s_wst, *s_cst)
            sp.dma_start(ctxT[:, :, :], d["ctxT"].rearrange("b p s -> p b s")).then_inc(s_ctx, 16)
            sp.dma_start(wq[:, :], d["wq0T"]).then_inc(s_w0, 16)
            sp.dma_start(wk[:, :], d["wk0T"]).then_inc(s_w0, 16)
            sp.dma_start(GR, d["gamma"]).then_inc(s_gam, 16)
            for b in range(B):
                sp.dma_start(keep.x[:, 4 * b:4 * b + 4, :],
                             d["x"][b * S:(b + 1) * S, :].rearrange("(t p) n -> p t n", p=P)).then_inc(s_x, 16)
            sp.dma_start(gate_raw[:, :, :], d["gate_wT"].rearrange("(k p) e -> p k e", p=P)).then_inc(s_gw, 16)
            sp.wait_ge(s_zero, 1)

            def load_head(h, par):
                rows = ds(h * P, P)
                sp.dma_start(r_wq[par][:, :], d["wq1"][rows, :]).then_inc(s_raw[par], 16)
                sp.dma_start(r_kcq[par][:, :, :], d["kcqT"][h, :, :].rearrange("(t p) k -> p t k", p=P)).then_inc(s_raw[par], 16)
                sp.dma_start(r_qr[par][:, :, :], d["wqr"][h, :, :].rearrange("(t p) r -> p t r", p=P)).then_inc(s_raw[par], 16)
                sp.dma_start(r_kckv[par][:, :], d["kckv"][h, :, :]).then_inc(s_raw[par], 16)
                sp.dma_start(r_wo[par][:, :], d["woT"][rows, :]).then_inc(s_raw[par], 16)
                sp.dma_start(r_kr[par][:, :], d["wkr"][h, :, :]).then_inc(s_raw[par], 16)

            def batch(b, more):
                for hh in range(4):
                    pp = hh // 2
                    if more or hh < 2:
                        after(sp, s_phi, 12 * b + 3 * hh + 3)
                        load_head(4 * b + hh + 2, hh % 2)
                    if hh % 2:
                        pair = 2 * b + pp
                        after(sp, s_plo, 2 * pair + 2)
                        sp.dma_start(scratch.wqc[pair, :, :], st_q[pp][:, :, :, :, :].rearrange("p k l h r -> p (k l h r)")).then_inc(s_wst[pp], 16)
                        sp.dma_start(scratch.wvo[ds(2 * pair, 2), :, :].rearrange("h p n -> p h n"),
                                     st_v[pp][:, :, :, :].rearrange("p h l n -> p h (l n)")).then_inc(s_wst[pp], 16)
                        sp.dma_start(scratch.wkr[ds(2 * pair, 2), :, :].rearrange("h p n -> p h n"),
                                     st_k[pp][:, :, :, :, :].rearrange("p h l a r -> p h (l a r)")).then_inc(s_wst[pp], 16)
                for u in range(2):
                    rows = scratch.xs[ds((2 * b + u) * (TILES // E * P), TILES // E * P), :]
                    sp.dma_start(rows.rearrange("(t p) n -> p t n", p=P),
                                 zeros[:, :].unsqueeze(1).to_broadcast([P, TILES // E, D])).then_inc(s_zst, 16)
                for u in range(2):
                    sp.wait_ge(s_rlo, 2 * b + u + 1)
                    sp.dma_start(scratch.kvs[2 * b + u, :, :],
                                 st_c[u][:, :, :].rearrange("p l n -> p (l n)")).then_inc(s_cst[u], 16)

            for par in range(2):
                load_head(par, par)
            with sp.Fori(0, B - 1) as b:
                batch(b, True)
            batch(B - 1, False)
            for pp in range(2):
                sp.wait_ge(s_wst[pp], 48 * B + 1)
                sp.wait_ge(s_cst[pp], 16 * B + 1)
            sp.wait_ge(s_zst, 16 * E)

        @block.gpsimd
        def _(pool):
            nc.gpsimd.memset(keep.ident[:, :], 0.0)
            nc.gpsimd.memset(keep.eps[:, :], EPS)
            nc.gpsimd.memset(ones[:, :], 1.0)
            nc.gpsimd.memset(zeros[:, :], 0.0).then_inc(s_zero, 1)
            for j in range(8):
                nc.gpsimd.memset(place[:, j:j + 1], float(j))
            pool.drain()
            nc.gpsimd.affine_select(out=keep.ident[:, :], in_=keep.ident[:, :], compare_op=ALU.not_equal,
                                    fill=1.0, base=0, pattern=[[-1, P]], channel_multiplier=1)
            pool.drain()
            nc.gpsimd.tensor_copy(keep.ident16[:, :], keep.ident[:, :]).then_inc(s_id, 1)
            pool.wait_ge(s_gw, 16)
            nc.gpsimd.tensor_scalar(gate32[:, :, :], gate_raw[:, :, :], SC, 1.0, ALU.mult, ALU.mult)
            pool.drain()
            nc.gpsimd.tensor_copy(gate_w[:, :, 0, :], gate32[:, :, :])
            pool.drain()
            nc.gpsimd.tensor_tensor(gate_w[:, :, 1, :], gate32[:, :, :], gate_w[:, :, 0, :],
                                    ALU.subtract).then_inc(s_gate, 1)
            with pool.Fori(0, 2) as i:
                after(pool, s_rhi, 4 * i)
                pool.dma_start(cos[:, :], d["rope_cos"][i, :, :]).then_inc(s_tab, 16)
                pool.dma_start(sin[:, :], d["rope_sin"][i, :, :]).then_inc(s_tab, 16)
                for par in range(2):
                    for hh in range(4):
                        n = 8 * i + 4 * par + hh
                        pp, e = hh // 2, hh % 2
                        after(pool, s_phi, 3 * n + 3)
                        nc.gpsimd.tensor_tensor(st_q[pp][:, :, 1, e, :], c_q[:, :, :], st_q[pp][:, :, 0, e, :], ALU.subtract)
                        nc.gpsimd.tensor_tensor(st_v[pp][:, e, 1, :], c_vo[:, :], st_v[pp][:, e, 0, :], ALU.subtract)
                        for two in range(2):
                            last = nc.gpsimd.tensor_tensor(st_k[pp][:, e, 1, two, :], c_kr[:, :],
                                                           st_k[pp][:, e, 0, two, :], ALU.subtract)
                        last.then_inc(s_plo, 1)
                    for u in range(2):
                        n = 4 * i + 2 * par + u
                        if par + u > 0:
                            after(pool, s_rhi, n)
                        b = 2 * par + u
                        pool.dma_start(craw[:, :], d["ctx_both"][i, b, :, :]).then_inc(s_rope_in, 16)
                        pool.dma_start(crot[:, :], d["ctx_rot"][i, b, :, :]).then_inc(s_rope_in, 16)
                        pool.wait_ge(s_tab, 32 * i + 32)
                        pool.wait_ge(s_rope_in, 32 * n + 32)
                        nc.gpsimd.tensor_tensor(craw[:, :], craw[:, :], cos[:, :], ALU.mult)
                        nc.gpsimd.tensor_tensor(crot[:, :], crot[:, :], sin[:, :], ALU.mult)
                        pool.drain()
                        nc.gpsimd.tensor_tensor(rope[:, :], craw[:, :], crot[:, :], ALU.add).then_inc(s_rope, 1)
                        after(pool, s_rhi, n + 1)
                        nc.gpsimd.tensor_tensor(st_c[u][:, 1, :], rope[:, :], st_c[u][:, 0, :],
                                                ALU.subtract).then_inc(s_rlo, 1)
                        pool.drain()

        @block.scalar
        def _(a):
            a.wait_ge(s_gam, 16)
            nc.scalar.activation(GS, GR, ACT.Sigmoid).then_inc(s_sig, 1)
            a.wait_ge(s_id, 1)
            def similarities(b):
                for w, T in enumerate((QT, KT)):
                    a.wait_ge(s_qps, 2 * b + w + 1)
                    nc.scalar.activation(T[:, :], ps_proj[:, :], ACT.Copy).then_inc(s_qk, 1)
                for n in range(NT):
                    a.wait_ge(s_sps, 4 * b + n + 1)
                    nc.scalar.activation(sim[:, b % 2, n, :], ps_sim[n % 2][:, :], ACT.Copy,
                                         scale=1.0 / (float(C // 4) ** 0.5 * 4)).then_inc(s_sim, 1)

            def deviations(b):
                a.wait_ge(s_vars, b + 1)
                nc.scalar.activation(sds[:, :], mvs[:, :, 1], ACT.Sqrt).then_inc(s_sds, 1)
                a.wait_ge(s_var0, b + 1)
                nc.scalar.activation(std0[:, :], mv0[:, :, 1], ACT.Sqrt, bias=keep.eps[:, 0:1]).then_inc(s_std0, 1)

            def batch(b, more):
                after(a, s_blend, b)
                nc.scalar.activation(A[:, :, :], sim[:, b % 2, :, :], ACT.Sigmoid).then_inc(s_sgm, 1)
                for hh in range(4):
                    n = 4 * b + hh
                    q = hh % 2
                    a.wait_ge(s_wcps, n + 1)
                    nc.scalar.activation(wc[:, :], ps_wc[:, 0:R], ACT.Copy).then_inc(s_wc, 1)
                    a.wait_ge(s_pps, n + 1)
                    after(a, s_plo, n)
                    nc.scalar.activation(c_q[:, :, :], ps_wq[:, 0:KD * R].rearrange("p (k r) -> p k r", k=KD),
                                         ACT.Copy, scale=SC)
                    nc.scalar.activation(c_vo[:, :], ps_vo[:, :], ACT.Copy, scale=SC).then_inc(s_p32, 1)
                    nc.scalar.activation(c_kr[:, :], r_kr[q][:, :], ACT.Copy, scale=SC)
                    a.drain()
                    pp, e = hh // 2, hh % 2
                    after(a, s_wst[pp], 48 * b)
                    nc.scalar.activation(st_q[pp][:, :, 0, e, :], c_q[:, :, :], ACT.Copy).then_inc(s_phi, 1)
                    nc.scalar.activation(st_v[pp][:, e, 0, :], c_vo[:, :], ACT.Copy).then_inc(s_phi, 1)
                    nc.scalar.activation(st_k[pp][:, e, 0, :, :], c_kr[:, :].unsqueeze(1).to_broadcast([P, 2, R]),
                                         ACT.Copy).then_inc(s_phi, 1)
                if more:
                    similarities(b + 1)
                ln.root(nc, a, b, b)
                if more:
                    deviations(b + 1)
                ln.highs(nc, a, b)
                for u in range(2):
                    n = 2 * b + u
                    a.wait_ge(s_rope, n + 1)
                    after(a, s_cst[u], 16 * b)
                    nc.scalar.activation(st_c[u][:, 0, :], rope[:, :], ACT.Copy).then_inc(s_rhi, 1)

            similarities(0)
            deviations(0)
            with a.Fori(0, B - 1) as b:
                batch(b, True)
            batch(B - 1, False)

        def row_stats(v, b, par):
            for n in range(NT):
                nc.vector.bn_stats(st0[:, n, :], keep.x[:, 4 * b + n, :])
            v.wait_ge(s_sim, 4 * b + 4)
            for n in range(NT):
                nc.vector.bn_stats(st1[:, n, :], sim[:, par, n, 0:S // 2])
            v.drain()
            for n in range(NT):
                last = nc.vector.bn_aggr(mv0[:, n, :], st0[:, n, :])
            last.then_inc(s_var0, 1)
            for n in range(NT):
                last = nc.vector.bn_aggr(mvs[:, n, :], st1[:, n, :])
            last.then_inc(s_vars, 1)

        def search(v, b, par):
            v.wait_ge(s_sds, b + 1)
            for dst, z in ((cur, Z_TARGET), (low2, -3.0), (high2, 3.0)):
                nc.vector.scalar_tensor_tensor(dst[:, 0, :], sds[:, :], z, mvs[:, :, 0], ALU.mult, ALU.add)
            nc.vector.memset(low2[:, 1, :], float(S))
            nc.vector.memset(high2[:, 1, :], 0.0)
            v.drain()
            for k in range(PROBES):
                for n in range(NT):
                    nc.vector.tensor_scalar(hit[:, n, :], sim[:, par, n, :], cur[:, 0, n:n + 1], None,
                                            ALU.is_ge, ALU.add, accum_out=cur[:, 1, n:n + 1])
                v.drain()
                nc.vector.tensor_scalar(above[:, :], cur[:, 1, :], TARGET, None, ALU.is_gt)
                nc.vector.tensor_scalar(below[:, :], cur[:, 1, :], TARGET, None, ALU.is_lt)
                nc.vector.tensor_scalar(off[:, :], cur[:, 1, :], TARGET - 4.0, None, ALU.is_lt)
                v.drain()
                nc.vector.copy_predicated(low2[:, :, :], above[:, :].unsqueeze(1).to_broadcast([P, 2, NT]), cur[:, :, :])
                nc.vector.copy_predicated(high2[:, :, :], below[:, :].unsqueeze(1).to_broadcast([P, 2, NT]), cur[:, :, :])
                nc.vector.scalar_tensor_tensor(miss[:, :], cur[:, 1, :], TARGET + 4.0, off[:, :], ALU.is_gt, ALU.add)
                v.drain()
                if k == 0:
                    nc.vector.tensor_scalar(off[:, :], cur[:, 1, :], TARGET, 1.0 / DENSITY, ALU.subtract, ALU.mult)
                    v.drain()
                    nc.vector.tensor_tensor(off[:, :], off[:, :], sds[:, :], ALU.mult)
                    v.drain()
                    nc.vector.tensor_tensor(nxt[:, :], cur[:, 0, :], off[:, :], ALU.add)
                else:
                    nc.vector.tensor_tensor(dif[:, :, :], high2[:, :, :], low2[:, :, :], ALU.subtract)
                    nc.vector.tensor_scalar(off[:, :], low2[:, 1, :], TARGET, None, ALU.subtract)
                    v.drain()
                    nc.vector.reciprocal(dif[:, 1, :], dif[:, 1, :])
                    nc.vector.tensor_tensor(off[:, :], off[:, :], dif[:, 0, :], ALU.mult)
                    v.drain()
                    nc.vector.tensor_tensor(off[:, :], off[:, :], dif[:, 1, :], ALU.mult)
                    v.drain()
                    nc.vector.tensor_tensor(nxt[:, :], low2[:, 0, :], off[:, :], ALU.subtract)
                v.drain()
                nc.vector.copy_predicated(cur[:, 0, :], miss[:, :], nxt[:, :])
                v.drain()
            for n in range(NT):
                nc.vector.tensor_scalar(hit[:, n, :], sim[:, par, n, :], cur[:, 0, n:n + 1], None,
                                        ALU.is_ge, ALU.add, accum_out=cur[:, 1, n:n + 1])
            v.drain()
            nc.vector.tensor_scalar(off[:, :], cur[:, 1, :], TARGET - 4.0, None, ALU.is_lt)
            v.drain()
            nc.vector.scalar_tensor_tensor(off[:, :], cur[:, 1, :], TARGET + 4.0, off[:, :], ALU.is_gt, ALU.add,
                                           accum_out=bad[:, 0:1])
            v.drain()
            v.nop().then_inc(s_bad, 1)
            for n in range(NT):
                nc.vector.scalar_tensor_tensor(rest[:, n % 2, :], hit[:, n, :], -FAR, sim[:, par, n, :], ALU.mult, ALU.add)
                v.drain()
                nc.vector.max(eight[:, n, :], rest[:, n % 2, :])
            nc.vector.tensor_scalar(off[:, :], cur[:, 1, :], -1.0, TOPK - 1.0, ALU.mult, ALU.add)
            v.drain()
            nc.vector.tensor_tensor(pick[:, :, :], place[:, :].unsqueeze(1).to_broadcast([P, NT, 8]),
                                    off[:, :].unsqueeze(2).to_broadcast([P, NT, 8]), ALU.is_equal)
            v.drain()
            nc.vector.tensor_tensor(pick[:, :, :], pick[:, :, :], eight[:, :, :], ALU.mult)
            v.drain()
            nc.vector.tensor_reduce(lo_t[:, :], pick[:, :, :], AX.X, ALU.add)
            v.wait_ge(s_badsum, b + 1)
            nc.vector.tensor_copy(badi[:, :], ps_bad[0:1, 0:1])
            v.drain()
            failed = v.value_load(badi[0:1, 0:1], min_val=0, max_val=P * NT)
            with v.If(failed > 0):
                bisect(v, par)

        def bisect(v, par):
            nc.vector.tensor_reduce(lo_t[:, :], sim[:, par, :, :], AX.X, ALU.min)
            nc.vector.tensor_reduce(top[:, :], sim[:, par, :, :], AX.X, ALU.max)
            v.drain()
            nc.vector.tensor_tensor(step[:, :], top[:, :], lo_t[:, :], ALU.subtract)
            v.drain()
            with v.Fori(0, BISECT):
                nc.vector.tensor_scalar(step[:, :], step[:, :], 0.5, None, ALU.mult)
                v.drain()
                nc.vector.tensor_tensor(probe[:, :], lo_t[:, :], step[:, :], ALU.add)
                v.drain()
                for n in range(NT):
                    nc.vector.tensor_scalar(hit[:, n, :], sim[:, par, n, :], probe[:, n:n + 1], None,
                                            ALU.is_ge, ALU.add, accum_out=cnt[:, n:n + 1])
                v.drain()
                nc.vector.scalar_tensor_tensor(probe[:, :], cnt[:, :], TOPK - 0.5, step[:, :],
                                               ALU.is_ge, ALU.mult)
                v.drain()
                nc.vector.tensor_tensor(lo_t[:, :], lo_t[:, :], probe[:, :], ALU.add)
                v.drain()

        @block.vector
        def _(v):
            v.wait_ge(s_sig, 1)
            nc.vector.tensor_scalar(OMG, GS, -1.0, 1.0, ALU.mult, ALU.add)
            nc.vector.tensor_scalar(HG, GS, 0.5, None, ALU.mult)
            v.wait_ge(s_x, 64)
            row_stats(v, 0, 0)

            def batch(b, more):
                par = b % 2
                search(v, b, par)
                v.wait_ge(s_sgm, b + 1)
                for n in range(NT):
                    nc.vector.scalar_tensor_tensor(A[:, n, :], sim[:, par, n, :], lo_t[:, n:n + 1], A[:, n, :],
                                                   ALU.is_ge, ALU.mult).then_inc(s_mask, 1)
                v.wait_ge(s_std0, b + 1)
                nc.vector.reciprocal(rstd0[:, :], std0[:, :])
                v.drain()
                nc.vector.tensor_tensor(fb[:, :], mv0[:, :, 0], rstd0[:, :], ALU.mult)
                nc.vector.tensor_scalar(fa[:, :], rstd0[:, :], OMG, 1.0, ALU.mult, ALU.add)
                v.drain()
                nc.vector.tensor_scalar(fb[:, :], fb[:, :], OMG, -1.0, ALU.mult, ALU.mult)
                v.drain()
                for n in range(NT):
                    nc.vector.tensor_scalar(keep.x[:, 4 * b + n, :], keep.x[:, 4 * b + n, :], fa[:, n:n + 1],
                                            fb[:, n:n + 1], ALU.mult, ALU.add)
                v.drain()
                for n in range(NT):
                    nc.vector.scalar_tensor_tensor(keep.x[:, 4 * b + n, :], A[:, n, :], HG, keep.x[:, 4 * b + n, :],
                                                   ALU.mult, ALU.add)
                v.drain()
                for n in range(NT):
                    v.wait_ge(s_at, 4 * b + n + 1)
                    nc.vector.scalar_tensor_tensor(keep.x[:, 4 * b + n, :], ps_T[n % 2][:, :], HG,
                                                   keep.x[:, 4 * b + n, :], ALU.mult, ALU.add).then_inc(s_blend_t, 1)
                v.drain()
                v.nop().then_inc(s_blend, 1)
                ln.stats(nc, v, b)
                if more:
                    row_stats(v, b + 1, (b + 1) % 2)
                ln.rows(nc, v, b, waits=False)
                ln.lows(nc, v, b)

            with v.Fori(0, B - 1) as b:
                batch(b, True)
            batch(B - 1, False)

        @block.tensor
        def _(pe):
            pe.wait_ge(s_ctx, 16)
            pe.wait_ge(s_w0, 32)
            pe.wait_ge(s_id, 1)
            def similarities(b):
                for w, W in enumerate((wq, wk)):
                    after(pe, s_qk, 2 * b + w)
                    nc.tensor.matmul(ps_proj[:, :], W[:, :], ctxT[:, b, :], start=True, stop=True).then_inc(s_qps, 1)
                after(pe, s_qk, 2 * b + 2)
                for n in range(NT):
                    if n >= 2:
                        pe.wait_ge(s_sim, 4 * b + n - 1)
                    nc.tensor.matmul(ps_sim[n % 2][:, :], QT[:, n * P:(n + 1) * P], KT[:, :],
                                     start=True, stop=True).then_inc(s_sps, 1)

            def batch(b, more):
                for hh in range(4):
                    n = 4 * b + hh
                    q = hh % 2
                    pe.wait_ge(s_raw[q], 96 * (2 * b + hh // 2 + 1))
                    after(pe, s_wc, n)
                    for t in range(Q3):
                        last = nc.tensor.matmul(ps_wc[:, 0:R], r_kcq[q][:, t, :], r_qr[q][:, t, :],
                                                start=t == 0, stop=t == Q3 - 1)
                    last.then_inc(s_wcps, 1)
                    after(pe, s_p32, n)
                    nc.tensor.matmul(ps_vo[:, :], r_kckv[q][:, :], r_wo[q][:, :], start=True, stop=True)
                    after(pe, s_wc, n + 1)
                    for k in range(KD):
                        last = nc.tensor.matmul(ps_wq[:, k * R:(k + 1) * R], r_wq[q][:, k * P:(k + 1) * P],
                                                wc[:, :], start=True, stop=True)
                    last.then_inc(s_pps, 1)
                pe.wait_ge(s_bad, b + 1)
                nc.tensor.matmul(ps_bad[0:1, 0:1], bad[:, 0:1], ones[:, 0:1], start=True, stop=True).then_inc(s_badsum, 1)
                if more:
                    similarities(b + 1)
                pe.wait_ge(s_mask, 4 * b + 4)
                for n in range(NT):
                    if n >= 2:
                        pe.wait_ge(s_blend_t, 4 * b + n - 1)
                    for m in range(NT):
                        last = nc.tensor.transpose(ps_T[n % 2][:, m * P:(m + 1) * P],
                                                   A[:, m, n * P:(n + 1) * P], keep.ident[:, :])
                    last.then_inc(s_at, 1)
                pe.wait_ge(s_blend_t, 4 * b + 4)
                if more:
                    pe.wait_ge(s_sim, 4 * b + 8)
                ln.transposes(nc, pe, b, waits=False)

            similarities(0)
            with pe.Fori(0, B - 1) as b:
                batch(b, True)
            batch(B - 1, False)


def stage_router(nc, keep, gate_w, mv1, rstd1, xn):
    T = B * NT
    with ExitStack() as ctx:
        sc = Scope(nc, ctx)
        s8 = sc.sb("scores8", [P, T, E])
        m8 = sc.sb("sorted8", [P, T, E])
        i8 = sc.sb("index8", [P, T, E], U32)
        if8 = sc.sb("index8f", [P, T, 2])
        iota_i = sc.sb("iota_i", [P, TILES], mybir.dt.int32)
        iota = sc.sb("iota", [P, TILES])
        marks = sc.sb("marks", [P, T])
        tri = sc.sb("tri", [P, P])
        ones = sc.sb("ones_pp", [P, P])
        hot = sc.sb("hot", [P, 2, T, E])
        both = sc.sb("both", [P, T, E])
        cum = [sc.sb(f"cum{i}", [P, T, E]) for i in range(2)]
        total = sc.sb("total", [P, T, E])
        fill = sc.sb("fill", [P, E, T])
        nt = sc.sb("nt", [P, E])
        end = [sc.sb(f"end{i}", [P, E]) for i in range(2)]
        past = sc.sb("past", [P, TILES, E])
        tef = sc.sb("tef", [P, TILES])
        prod = sc.sb("prod", [P, 2, T, E])
        placef = sc.sb("placef", [P, 2, T])
        tot = sc.sb("tot", [P, T])
        ps = sc.ps("ps_router")
        ps_in, ps_all = sc.ps("ps_before"), sc.ps("ps_total")
        s_ps, s_cen, s_exp, s_iota, s_hot, s_cnt = (sc.sem(n) for n in (
            "router_scores", "router_centred", "router_exp", "iota_ready", "choices_ready", "choices_counted"))
        block = ctx.enter_context(nc.Block())

        @block.tensor
        def _(pe):
            with pe.Fori(0, B) as b:
                for n in range(NT):
                    col = ds((4 * b + n) * E, E)
                    last = split_matmuls(nc, ps[:, col],
                                         [(lambda hl, k=k, n=n: keep.xT[:, b, k, hl, n * P:(n + 1) * P],
                                           lambda hl, k=k: gate_w[:, k, hl, :]) for k in range(KD)])
                last.then_inc(s_ps, 1)
            pe.wait_ge(s_iota, 1)
            pe.wait_ge(s_hot, 1)
            rhs = both[:, :, :].rearrange("p t e -> p (t e)")
            nc.tensor.matmul(ps_in[:, 0:T * E], tri[:, :], rhs, start=True, stop=True)
            nc.tensor.matmul(ps_all[:, 0:T * E], ones[:, :], rhs, start=True, stop=True).then_inc(s_cnt, 1)

        @block.gpsimd
        def _(pool):
            nc.gpsimd.iota(iota_i[:, :], pattern=[[1, TILES]], base=0, channel_multiplier=0)
            nc.gpsimd.memset(ones[:, :], 1.0)
            pool.drain()
            nc.gpsimd.tensor_copy(iota[:, :], iota_i[:, :])
            nc.gpsimd.affine_select(out=tri[:, :], in_=ones[:, :], compare_op=ALU.is_gt, fill=0.0, base=0,
                                    pattern=[[1, P]], channel_multiplier=-1)
            pool.drain()
            nc.gpsimd.tensor_scalar(marks[:, :], iota[:, 0:T], float(P), 1.0, ALU.mult, ALU.mult).then_inc(s_iota, 1)

        @block.scalar
        def _(a):
            a.wait_ge(s_cen, 1)
            nc.scalar.activation(s8[:, :, :], s8[:, :, :], ACT.Exp).then_inc(s_exp, 1)

        @block.vector
        def _(v):
            for t in range(T):
                nc.vector.tensor_scalar(xn[:, t, :], keep.x[:, t, :], mv1[:, t, 0:1], rstd1[:, t:t + 1],
                                        ALU.subtract, ALU.mult)
            v.wait_ge(s_ps, B)
            nc.vector.tensor_scalar(s8[:, :, :], ps[:, 0:T * E].rearrange("p (t e) -> p t e", e=E), 1.0 / SC, None, ALU.mult)
            v.drain()
            for t in range(T):
                nc.vector.max(m8[:, t, :], s8[:, t, :])
            v.drain()
            for t in range(T):
                nc.vector.max_index(i8[:, t, :], m8[:, t, :], s8[:, t, :])
            v.drain()
            nc.vector.tensor_tensor(s8[:, :, :], s8[:, :, :], m8[:, :, 0:1].to_broadcast([P, T, E]),
                                    ALU.subtract).then_inc(s_cen, 1)
            nc.vector.tensor_copy(if8[:, :, :], i8[:, :, 0:2])
            v.drain()
            v.wait_ge(s_iota, 1)
            it = iota[:, 0:E].unsqueeze(1).to_broadcast([P, T, E])
            for c in range(2):
                nc.vector.tensor_tensor(hot[:, c, :, :], it, if8[:, :, c:c + 1].to_broadcast([P, T, E]), ALU.is_equal)
            v.drain()
            nc.vector.tensor_tensor(both[:, :, :], hot[:, 0, :, :], hot[:, 1, :, :], ALU.add).then_inc(s_hot, 1)
            v.wait_ge(s_exp, 1)
            nc.vector.tensor_reduce(tot[:, :], s8[:, :, :], AX.X, ALU.add)
            for c in range(2):
                nc.vector.tensor_tensor(prod[:, c, :, :], hot[:, c, :, :], s8[:, :, :], ALU.mult)
            v.drain()
            nc.vector.tensor_scalar(tot[:, :], tot[:, :], SC, None, ALU.mult)
            nc.vector.tensor_reduce(keep.gates[:, :, :], prod[:, :, :, :], AX.X, ALU.add)
            v.drain()
            nc.vector.reciprocal(tot[:, :], tot[:, :])
            v.drain()
            for c in range(2):
                nc.vector.tensor_tensor(keep.gates[:, c, :], keep.gates[:, c, :], tot[:, :], ALU.mult)
            v.wait_ge(s_cnt, 1)
            al = ps_all[:, 0:T * E].rearrange("p (t e) -> p t e", e=E)
            nc.vector.tensor_copy(total[:, :, :], al)
            nc.vector.tensor_copy(cum[0][:, :, :], al)
            v.drain()
            for k in range(4):
                w, src, dst = 1 << k, cum[k % 2], cum[(k + 1) % 2]
                nc.vector.tensor_copy(dst[:, 0:w, :], src[:, 0:w, :])
                nc.vector.tensor_tensor(dst[:, w:T, :], src[:, w:T, :], src[:, 0:T - w, :], ALU.add)
                v.drain()
            nc.vector.tensor_tensor(fill[:, :, :], cum[0][:, T - 1, :].unsqueeze(2).to_broadcast([P, E, T]),
                                    marks[:, :].unsqueeze(1).to_broadcast([P, E, T]), ALU.is_gt)
            v.drain()
            nc.vector.tensor_reduce(nt[:, :], fill[:, :, :], AX.X, ALU.add)
            v.drain()
            nc.vector.tensor_scalar(nt[:, :], nt[:, :], 1.0, None, ALU.max)
            v.drain()
            nc.vector.tensor_copy(end[0][:, :], nt[:, :])
            v.drain()
            for k in range(3):
                w, src, dst = 1 << k, end[k % 2], end[(k + 1) % 2]
                nc.vector.tensor_copy(dst[:, 0:w], src[:, 0:w])
                nc.vector.tensor_tensor(dst[:, w:E], src[:, w:E], src[:, 0:E - w], ALU.add)
                v.drain()
            nc.vector.tensor_tensor(past[:, :, :], iota[:, :].unsqueeze(2).to_broadcast([P, TILES, E]),
                                    end[1][:, :].unsqueeze(1).to_broadcast([P, TILES, E]), ALU.is_ge)
            nc.vector.tensor_tensor(nt[:, :], end[1][:, :], nt[:, :], ALU.subtract)
            nc.vector.tensor_tensor(cum[0][:, :, :], cum[0][:, :, :], total[:, :, :], ALU.subtract)
            v.drain()
            nc.vector.tensor_reduce(tef[:, :], past[:, :, :], AX.X, ALU.add)
            nc.vector.tensor_scalar(nt[:, :], nt[:, :], float(P), None, ALU.mult)
            nc.vector.tensor_tensor(cum[0][:, :, :], cum[0][:, :, :],
                                    ps_in[:, 0:T * E].rearrange("p (t e) -> p t e", e=E), ALU.add)
            v.drain()
            nc.vector.tensor_scalar(keep.tile_expert[:, :], tef[:, :], E - 1.0, None, ALU.min)
            nc.vector.tensor_tensor(cum[0][:, :, :], cum[0][:, :, :],
                                    nt[:, :].unsqueeze(1).to_broadcast([P, T, E]), ALU.add)
            v.drain()
            for c in range(2):
                nc.vector.tensor_tensor(prod[:, c, :, :], hot[:, c, :, :], cum[0][:, :, :], ALU.mult)
            v.drain()
            nc.vector.tensor_reduce(placef[:, :, :], prod[:, :, :, :], AX.X, ALU.add)
            v.drain()
            nc.vector.tensor_copy(keep.place[:, :, :], placef[:, :, :])


def stage_experts(nc, keep, scratch, w13, w2):
    with ExitStack() as ctx:
        sc = Scope(nc, ctx)
        wup = [sc.sb(f"e_w{m}", [P, E, 2, KD, HV], FP16) for m in range(2)]
        wdn = sc.sb("e_w2", [P, E, 2, NJ0, D], FP16)
        raw = [sc.sb(f"e_raw{i}", [P, KD * HE]) for i in range(2)]
        xr = [sc.sb(f"e_x{i}", [P, D]) for i in range(2)]
        xT = [sc.sb(f"e_xT{i}", [P, KD, 2, P], FP16) for i in range(2)]
        h32 = [sc.sb(f"e_h{i}", [P, HE]) for i in range(2)]
        hT = [sc.sb(f"e_hT{i}", [P, 2, NJ0, P], FP16) for i in range(2)]
        y = [sc.sb(f"e_y{i}", [P, D]) for i in range(2)]
        psX, psH = sc.ps("e_psX"), sc.ps("e_psH")
        psG = [sc.ps(f"e_psG{i}") for i in range(2)]
        psU = [sc.ps(f"e_psU{i}") for i in range(2)]
        psD = [sc.ps(f"e_psD{i}") for i in range(2)]
        s_raw = [sc.sem(f"e_raw_loaded{i}") for i in range(2)]
        s_x = [sc.sem(f"e_x_loaded{i}") for i in range(2)]
        s_st = [sc.sem(f"e_y_stored{i}") for i in range(2)]
        s_pad = sc.sem("e_pad")
        (s_whi, s_wlo, s_xT, s_xhi, s_xlo, s_up, s_silu, s_h32, s_hT, s_hhi, s_hlo, s_dn, s_y) = (
            sc.sem("e_" + n) for n in ("w_hi", "w_lo", "x_transposed", "x_hi", "x_lo", "up", "silu", "h32",
                                       "h_transposed", "h_hi", "h_lo", "down", "y"))
        block = ctx.enter_context(nc.Block())

        def turns(eng, turn):
            for t in range(E):
                turn(t, t % 2, t // 2, True)
            with eng.Fori(E // 2, TILES // 2 - 1) as i:
                for q in range(2):
                    turn(2 * i + q, q, i, False)
            for t in range(TILES - 2, TILES + 2):
                turn(t, t % 2, t // 2, False)

        def has(t, what):
            if not isinstance(t, int):
                return True
            return {"in": t + 1 < TILES, "up": t < TILES, "h": 1 <= t <= TILES, "down": t >= 2}[what]

        def piece(m):
            if m < 2:
                return KD, HE, HV
            return NJ0, D, D

        @block.sync
        def _(sp):
            def load(t, q):
                sp.dma_start(xr[q][:, :], scratch.xs[ds(t * P, P), :]).then_inc(s_x[q], 16)

            def load_piece(n):
                e, m = n // 3, n % 3
                src = w13[m, e, :, :, :] if m < 2 else w2[e, :, :, :]
                sp.dma_start(raw[n % 2][:, :].rearrange("p (k n) -> p k n", k=piece(m)[0]), src).then_inc(s_raw[n % 2], 16)

            load(0, 0)
            load(1, 1)
            for n in range(5):
                if n >= 2:
                    sp.wait_ge(s_wlo, n - 1)
                load_piece(n)

            def turn(t, q, r, weights):
                if has(t, "up") and not (isinstance(t, int) and t >= TILES - 2):
                    sp.wait_ge(s_xT, t + 1)
                    load(t + 2, q)
                if weights:
                    for n in range(3 * t + 5, min(3 * t + 8, 3 * E)):
                        sp.wait_ge(s_wlo, n - 1)
                        load_piece(n)
                if has(t, "down"):
                    sp.wait_ge(s_y, t - 1)
                    sp.dma_start(scratch.ys[ds((t - 2) * P, P), :], y[q][:, :]).then_inc(s_st[q], 16)

            turns(sp, turn)
            for q in range(2):
                sp.wait_ge(s_st[q], 16 * TILES // 2)

        @block.gpsimd
        def _(pool):
            for q in range(2):
                last = nc.gpsimd.memset(h32[q][:, HV:HE], 0.0)
            last.then_inc(s_pad, 1)

        def split_src(q, m):
            k, w, used = piece(m)
            return raw[q][:, :].rearrange("p (k n) -> p k n", k=k)[:, :, 0:used]

        def split_dst(e, m, hl):
            return wup[m][:, e, hl, :, :] if m < 2 else wdn[:, e, hl, :, :]

        @block.scalar
        def _(a):
            def split(e, q0, half):
                for m in range(3):
                    q = (q0 + m) % 2
                    a.wait_ge(s_raw[q], 16 * (half[m] + 1))
                    nc.scalar.activation(split_dst(e, m, 0), split_src(q, m), ACT.Copy, scale=SC).then_inc(s_whi, 1)

            def incoming(t, q):
                a.wait_ge(s_xT, t + 1)
                if not (isinstance(t, int) and t < 2):
                    a.wait_ge(s_up, t - 1)
                nc.scalar.activation(xT[q][:, :, 0, :], psX[:, :].rearrange("p (k t) -> p k t", k=KD),
                                     ACT.Copy).then_inc(s_xhi, 1)

            split(0, 0, (0, 0, 1))
            incoming(0, 0)
            a.wait_ge(s_pad, 1)

            def turn(t, q, r, weights):
                if has(t, "in"):
                    incoming(t + 1, 1 - q)
                if weights and not (isinstance(t, int) and t == E - 1):
                    split(t + 1, 1 - q, [3 * r + (3 * q + 3 + m) // 2 for m in range(3)])
                if has(t, "up"):
                    a.wait_ge(s_up, t + 1)
                    if not (isinstance(t, int) and t < 2):
                        a.wait_ge(s_hT, t - 1)
                    nc.scalar.activation(h32[q][:, 0:HV], psG[q][:, 0:HV], ACT.Silu, scale=1.0 / SC).then_inc(s_silu, 1)
                if has(t, "h"):
                    a.wait_ge(s_hT, t)
                    if not (isinstance(t, int) and t < 3):
                        a.wait_ge(s_dn, t - 2)
                    nc.scalar.activation(hT[1 - q][:, 0, :, :], psH[:, 0:HE].rearrange("p (j t) -> p j t", j=NJ0),
                                         ACT.Copy).then_inc(s_hhi, 1)
                if has(t, "down"):
                    a.wait_ge(s_dn, t - 1)
                    if not (isinstance(t, int) and t < 4):
                        a.wait_ge(s_st[q], 16 * (r - 1))
                    nc.scalar.activation(y[q][:, :], psD[q][:, :], ACT.Copy).then_inc(s_y, 1)

            turns(a, turn)

        @block.vector
        def _(v):
            def split(e, q0):
                for m in range(3):
                    v.wait_ge(s_whi, 3 * e + m + 1)
                    nc.vector.scalar_tensor_tensor(split_dst(e, m, 1), split_src((q0 + m) % 2, m), SC,
                                                   split_dst(e, m, 0), ALU.mult, ALU.subtract).then_inc(s_wlo, 1)

            def incoming(t, q):
                v.wait_ge(s_xhi, t + 1)
                nc.vector.tensor_tensor(xT[q][:, :, 1, :], psX[:, :].rearrange("p (k t) -> p k t", k=KD),
                                        xT[q][:, :, 0, :], ALU.subtract).then_inc(s_xlo, 1)

            split(0, 0)
            incoming(0, 0)

            def turn(t, q, r, weights):
                if has(t, "in"):
                    incoming(t + 1, 1 - q)
                if weights and not (isinstance(t, int) and t == E - 1):
                    split(t + 1, 1 - q)
                if has(t, "up"):
                    v.wait_ge(s_silu, t + 1)
                    nc.vector.scalar_tensor_tensor(h32[q][:, 0:HV], psU[q][:, 0:HV], 1.0 / SC, h32[q][:, 0:HV],
                                                   ALU.mult, ALU.mult).then_inc(s_h32, 1)
                if has(t, "h"):
                    v.wait_ge(s_hhi, t)
                    nc.vector.tensor_tensor(hT[1 - q][:, 1, :, :], psH[:, 0:HE].rearrange("p (j t) -> p j t", j=NJ0),
                                            hT[1 - q][:, 0, :, :], ALU.subtract).then_inc(s_hlo, 1)

            turns(v, turn)

        @block.tensor
        def _(pe):
            def incoming(t, q, rounds):
                pe.wait_ge(s_x[q], 16 * (rounds + 1))
                if not (isinstance(t, int) and t == 0):
                    pe.wait_ge(s_xlo, t)
                for k in range(KD):
                    last = nc.tensor.transpose(psX[:, k * P:(k + 1) * P], xr[q][:, k * P:(k + 1) * P], keep.ident[:, :])
                last.then_inc(s_xT, 1)

            incoming(0, 0, 0)

            def expert(t):
                return pe.value_load(keep.tile_expert[0:1, ds(t, 1)], min_val=0, max_val=E - 1)

            def turn(t, q, r, weights):
                if has(t, "in"):
                    incoming(t + 1, 1 - q, r + q)
                if has(t, "up"):
                    e = expert(t)
                    if weights:
                        pe.wait_ge(s_wlo, 3 * t + 3)
                    pe.wait_ge(s_xlo, t + 1)
                    if not (isinstance(t, int) and t < 2):
                        pe.wait_ge(s_h32, t - 1)
                    for m, bank in enumerate((psG, psU)):
                        last = split_matmuls(nc, bank[q][:, 0:HV],
                                             [(lambda hl, k=k: xT[q][:, k, hl, :],
                                               lambda hl, k=k: wup[m][:, e, hl, k, :]) for k in range(KD)])
                    last.then_inc(s_up, 1)
                if has(t, "h"):
                    pe.wait_ge(s_h32, t)
                    if not (isinstance(t, int) and t < 2):
                        pe.wait_ge(s_hlo, t - 1)
                    for j in range(NJ0):
                        last = nc.tensor.transpose(psH[:, j * P:(j + 1) * P], h32[1 - q][:, j * P:(j + 1) * P],
                                                   keep.ident[:, :])
                    last.then_inc(s_hT, 1)
                if has(t, "down"):
                    e = expert(t - 2)
                    pe.wait_ge(s_hlo, t - 1)
                    if not (isinstance(t, int) and t < 4):
                        pe.wait_ge(s_y, t - 3)
                    split_matmuls(nc, psD[q][:, :],
                                  [(lambda hl, j=j: hT[q][:, hl, j, :],
                                    lambda hl, j=j: wdn[:, e, hl, j, :]) for j in range(NJ0)]).then_inc(s_dn, 1)

            turns(pe, turn)


def stage_ffn(nc, keep, tag, w13, w2, NG, NJ, pool_program=None, norm=False):
    HW = NJ * P
    with ExitStack() as ctx:
        sc = Scope(nc, ctx)
        raw = [sc.sb(f"{tag}_raw{i}", [P, NJ * 512]) for i in range(3)]
        wup = [[sc.sb(f"{tag}_w{m}_{par}", [P, 2, KD, HW], FP16) for m in range(2)] for par in range(2)]
        wdn = [sc.sb(f"{tag}_w2_{par}", [P, 2, NJ, D], FP16) for par in range(2)]
        hT = [sc.sb(f"{tag}_hT{par}", [P, NJ, 2, S], FP16) for par in range(2)]
        sg = [sc.sb(f"{tag}_silu{i}", [P, S]) for i in range(2)]
        h32 = sg
        with ExitStack() as ps_ctx:
            ps_scope = Scope(nc, ps_ctx)
            psG = [ps_scope.ps(f"{tag}_psG{i}") for i in range(2)]
            psU = [ps_scope.ps(f"{tag}_psU{i}") for i in range(2)]
            psD = [ps_scope.ps(f"{tag}_psD{i}") for i in range(4)]
            s_raw = [sc.sem(f"{tag}_raw_loaded{i}") for i in range(3)]
            s_whi, s_wlo = sc.sem(f"{tag}_w_hi"), sc.sem(f"{tag}_w_lo")
            s_up, s_silu, s_h32, s_h = (sc.sem(f"{tag}_{n}") for n in ("up", "silu", "h32", "h"))
            s_down, s_acc = sc.sem(f"{tag}_down"), sc.sem(f"{tag}_acc")
            ln = LayerNorm(sc, keep, "ln3", [sc.sb(f"ln3_xn{n}", [P, D]) for n in range(NT)], psD) if norm else None
            block = ps_ctx.enter_context(nc.Block())

            if pool_program is not None:
                block.gpsimd(pool_program)

            def flat(t):
                return t.rearrange("p h k n -> p h (k n)")

            def split_dst(par, m):
                return flat((wup[par][m] if m < 2 else wdn[par])[:, :, :, :])

            @block.sync
            def _(sp):
                def load(g, m):
                    if m < 2:
                        src, k = w13[m, g, :, :, :], KD
                    else:
                        src, k = w2[g, :, :, :], NJ
                    sp.dma_start(raw[m][:, :].rearrange("p (k n) -> p k n", k=k), src).then_inc(s_raw[m], 16)

                for m in range(3):
                    load(0, m)
                with sp.Fori(1, NG) as g:
                    for m in range(3):
                        sp.wait_ge(s_wlo, 3 * g - 3 + m + 1)
                        load(g, m)

            def split_hi(a, g, par, m):
                a.wait_ge(s_raw[m], 16 * g + 16)
                nc.scalar.activation(split_dst(par, m)[:, 0, :], raw[m][:, :], ACT.Copy, scale=SC).then_inc(s_whi, 1)

            def split_lo(v, g, par, m):
                v.wait_ge(s_whi, 3 * g + m + 1)
                nc.vector.scalar_tensor_tensor(split_dst(par, m)[:, 1, :], raw[m][:, :], SC, split_dst(par, m)[:, 0, :],
                                               ALU.mult, ALU.subtract).then_inc(s_wlo, 1)

            @block.scalar
            def _(a):
                if norm:
                    ln.root(nc, a, 0, 0)
                for m in range(3):
                    split_hi(a, 0, 0, m)
                if norm:
                    ln.highs(nc, a, 0)
                    ln.root(nc, a, 1, 1)
                    ln.highs(nc, a, 1)

                def pair(i, last):
                    for par in range(2):
                        g = 2 * i + par
                        for b in range(B):
                            u = 4 * g + b
                            ahead = norm and isinstance(g, int) and g == 0 and b + 2 < B
                            if ahead:
                                ln.root(nc, a, b + 2, b + 2)
                            for j in range(NJ):
                                n = u * NJ + j
                                a.wait_ge(s_up, n + 1)
                                if not (isinstance(n, int) and n < 2):
                                    a.wait_ge(s_h, n - 1)
                                q = (b * NJ + j) % 2
                                nc.scalar.activation(sg[q][:, :], psG[q][:, :], ACT.Silu, scale=1.0 / SC).then_inc(s_silu, 1)
                            if b >= 1 and not (last and par == 1):
                                if b == 1 and not (isinstance(g, int) and g == 0):
                                    a.wait_ge(s_down, 16 * g)
                                split_hi(a, g + 1, 1 - par, b - 1)
                            if ahead:
                                ln.highs(nc, a, b + 2)

                pair(0, NG == 2)
                if NG > 4:
                    with a.Fori(1, NG // 2 - 1) as i:
                        pair(i, False)
                if NG > 2:
                    pair(NG // 2 - 1, True)

            @block.vector
            def _(v):
                if norm:
                    ln.stats(nc, v, 0)
                    ln.rows(nc, v, 0)
                for m in range(3):
                    split_lo(v, 0, 0, m)
                if norm:
                    ln.lows(nc, v, 0)
                    ln.stats(nc, v, 1)
                    ln.rows(nc, v, 1)
                    ln.lows(nc, v, 1)

                def take(u, b):
                    for t in range(NT):
                        v.wait_ge(s_down, 4 * u + t + 1)
                        xs = keep.x[:, 4 * b + t, :]
                        nc.vector.scalar_tensor_tensor(xs, psD[t][:, :], 1.0 / SC, xs, ALU.mult, ALU.add).then_inc(s_acc, 1)

                def pair(i, last):
                    for par in range(2):
                        g = 2 * i + par
                        for b in range(B):
                            u = 4 * g + b
                            ahead = norm and isinstance(g, int) and g == 0 and b + 2 < B
                            if ahead:
                                ln.stats(nc, v, b + 2)
                                ln.rows(nc, v, b + 2)
                            for j in range(NJ):
                                n = u * NJ + j
                                q = (b * NJ + j) % 2
                                v.wait_ge(s_silu, n + 1)
                                nc.vector.scalar_tensor_tensor(h32[q][:, :], psU[q][:, :], 1.0 / SC, sg[q][:, :],
                                                               ALU.mult, ALU.mult).then_inc(s_h32, 1)
                                if j == 0 and not (isinstance(u, int) and u < 2):
                                    v.drain()
                                    v.wait_ge(s_down, 4 * (u - 1))
                                else:
                                    v.drain()
                                hh = hT[b % 2]
                                nc.vector.tensor_copy(hh[:, j, 0, :], h32[q][:, :])
                                v.drain()
                                nc.vector.tensor_tensor(hh[:, j, 1, :], h32[q][:, :], hh[:, j, 0, :],
                                                        ALU.subtract).then_inc(s_h, 1)
                            if b >= 1 and not (last and par == 1):
                                split_lo(v, g + 1, 1 - par, b - 1)
                            if not (isinstance(u, int) and u == 0):
                                take(u - 1, (b - 1) % B)
                            if ahead:
                                ln.lows(nc, v, b + 2)

                pair(0, NG == 2)
                if NG > 4:
                    with v.Fori(1, NG // 2 - 1) as i:
                        pair(i, False)
                if NG > 2:
                    pair(NG // 2 - 1, True)
                take(4 * NG - 1, B - 1)

            @block.tensor
            def _(pe):
                def up(u, g, par, b):
                    if b == 0:
                        pe.wait_ge(s_wlo, 3 * g + 2)
                    if norm and isinstance(g, int) and g == 0:
                        pe.wait_ge(ln.s_lo, 4 * b + 4)
                    for j in range(NJ):
                        n = u * NJ + j
                        q = (b * NJ + j) % 2
                        if not (isinstance(n, int) and n < 2):
                            pe.wait_ge(s_h32, n - 1)
                        for m, bank in enumerate((psG, psU)):
                            w = wup[par][m]
                            last = split_matmuls(nc, bank[q][:, :],
                                                 [(lambda hl, k=k: w[:, hl, k, j * P:(j + 1) * P],
                                                   lambda hl, k=k: keep.xT[:, b, k, hl, :]) for k in range(KD)])
                        last.then_inc(s_up, 1)

                def down(u, g, par, b):
                    if b == 0:
                        pe.wait_ge(s_wlo, 3 * g + 3)
                    pe.wait_ge(s_h, NJ * (u + 1))
                    for t in range(NT):
                        if not (isinstance(u, int) and u == 0):
                            pe.wait_ge(s_acc, 4 * (u - 1) + t + 1)
                        if norm and isinstance(u, int) and u < B:
                            pe.wait_ge(ln.s_lo, min(4 * (u + 2), 4 * (B - 1)) + t + 1)
                        split_matmuls(nc, psD[t][:, :],
                                      [(lambda hl, j=j: hT[b % 2][:, j, hl, t * P:(t + 1) * P],
                                        lambda hl, j=j: wdn[par][:, hl, j, :]) for j in range(NJ)]).then_inc(s_down, 1)

                def pair(i, last):
                    for par in range(2):
                        g = 2 * i + par
                        for b in range(B):
                            u = 4 * g + b
                            if norm and isinstance(g, int) and g == 0 and b + 2 < B:
                                if u > 0:
                                    pe.wait_ge(s_acc, 4 * u)
                                ln.transposes(nc, pe, b + 2)
                            if b < B - 1:
                                up(u + 1, g, par, b + 1)
                            elif not (last and par == 1):
                                up(u + 1, g + 1, 1 - par, 0)
                            down(u, g, par, b)

                if norm:
                    for b in range(2):
                        ln.transposes(nc, pe, b)
                up(0, 0, 0, 0)
                pair(0, NG == 2)
                if NG > 4:
                    with pe.Fori(1, NG // 2 - 1) as i:
                        pair(i, False)
                if NG > 2:
                    pair(NG // 2 - 1, True)


def stage_combine(nc, keep, scratch):
    with ExitStack() as ctx:
        sc = Scope(nc, ctx)
        xn = [sc.sb(f"ln2_xn{i}", [P, D]) for i in range(2)]
        y = [[sc.sb(f"y{n}_{c}", [P, D]) for c in range(2)] for n in range(NT)]
        ps_T = [sc.ps(f"ln2_psT{i}") for i in range(2)]
        s_y = [sc.sem(f"y_loaded{n}") for n in range(NT)]
        s_add = sc.sem("y_added")
        s_w = sc.sem("attention_weights_back")
        ln = LayerNorm(sc, keep, "ln2", xn, ps_T)
        block = ctx.enter_context(nc.Block())

        @block.sync
        def _(sp):
            start_at_one(sp, ln.s_lo)
            sp.dma_start(keep.kvs[:, :, :, :].rearrange("p n l s -> p n (l s)"),
                         scratch.kvs[:, :, :].rearrange("n p s -> p n s")).then_inc(s_w, 16)
            sp.dma_start(keep.wkr[:, :, :, :].rearrange("p h l r -> p h (l r)"),
                         scratch.wkr[:, :, :].rearrange("h p r -> p h r")).then_inc(s_w, 16)
            sp.dma_start(keep.wqc[:, :, :, :, :].rearrange("p h k l r -> p h (k l r)"),
                         scratch.wqc[:, :, :].rearrange("h p r -> p h r")).then_inc(s_w, 16)
            sp.dma_start(keep.wvo[:, :, :, :].rearrange("p h l n -> p h (l n)"),
                         scratch.wvo[:, :, :].rearrange("h p n -> p h n")).then_inc(s_w, 16)
            sp.wait_ge(s_w, 64)

        @block.gpsimd
        def _(pool):
            for b in range(B):
                for n in range(NT):
                    t = 4 * b + n
                    if b > 0:
                        pool.wait_ge(s_add, t - NT + 1)
                    for c in range(2):
                        nc.gpsimd.indirect_dma_start(y[n][c][:, :], None, scratch.ys[:, :],
                                                     bass.IndirectOffsetOnAxis(keep.place[:, c, t:t + 1], 0)
                                                     ).then_inc(s_y[n], 16)

        @block.scalar
        def _(a):
            with a.Fori(0, B) as b:
                ln.scalar(nc, a, b, b)

        @block.vector
        def _(v):
            with v.Fori(0, B) as b:
                for n in range(NT):
                    v.wait_ge(s_y[n], 32 * b + 32)
                    for c in range(2):
                        xs = keep.x[:, 4 * b + n, :]
                        last = nc.vector.scalar_tensor_tensor(xs, y[n][c][:, :], keep.gates[:, c, ds(4 * b + n, 1)], xs,
                                                              ALU.mult, ALU.add)
                        if c == 0:
                            v.drain()
                    last.then_inc(s_add, 1)
                v.drain()
                ln.vector(nc, v, b, b)

        @block.tensor
        def _(pe):
            with pe.Fori(0, B) as b:
                after(pe, ln.s_lo, 4 * b)
                ln.tensor(nc, pe, b)


def stage_attention(nc, keep):
    with ExitStack() as ctx:
        sc = Scope(nc, ctx)
        Q = [sc.sb(f"Q{i}", [P, S], FP16) for i in range(4)]
        KH = [sc.sb(f"KH{i}", [P, S], FP16) for i in range(2)]
        KL = [sc.sb(f"KL{i}", [P, S], FP16) for i in range(2)]
        p32 = [sc.sb(f"p32_{i}", [P, S]) for i in range(NT)]
        pn = [sc.sb(f"pn{i}", [P, 2, S], FP16) for i in range(NT)]
        pT = [sc.sb(f"pT{i}", [P, 2, NT, S], FP16) for i in range(2)]
        cx = sc.sb("cx", [P, 2, 2 * HG, S], FP16)
        nmx = sc.sb("nmx", [P, NT])
        rsum, rinv = sc.sb("rsum", [P, NT]), sc.sb("rinv", [P, NT])
        psQK, psO = sc.ps("psQK"), sc.ps("psO")
        psC = [sc.ps(f"psC{i}") for i in range(2)]
        psS = [sc.ps(f"psS{i}") for i in range(2)]
        psP = [sc.ps(f"psP{i}", (P, 2, NT, P), FP16) for i in range(2)]
        (s_qps, s_kps, s_qhi, s_qlo, s_khi, s_klo, s_S, s_max, s_exp, s_r, s_phi, s_pn, s_T, s_ev, s_ctx, s_chi,
         s_clo, s_out, s_acc) = (sc.sem("at_" + n) for n in (
             "q_in_psum", "k_in_psum", "q_hi", "q_lo", "k_hi", "k_lo", "scores", "max", "exp", "inverse_sum",
             "probs_hi", "probs", "probs_transposed", "probsT", "ctx", "ctx_hi", "ctx_lo", "out", "acc"))
        block = ctx.enter_context(nc.Block())

        def steps(eng, step):
            for k in range(H - 2):
                step(0, k)
            with eng.Fori(1, B) as b:
                for k in range(-2, H - 2):
                    step(b, k)
            for k in range(-2, 7):
                step(B, k)

        def has(b, k, tiles):
            return not isinstance(b, int) or 0 <= 4 * (H * b + k) + tiles < 4 * H * B

        def head(b, k):
            return b + k // H, k % H

        def upto(eng, sem, n):
            if not (isinstance(n, int) and n <= 0):
                eng.wait_ge(sem, n)

        @block.tensor
        def _(pe):
            def queries(b, k):
                bb, h = head(b, k)
                split_matmuls(nc, psQK[:, :], [(lambda hl, c=c: keep.wqc[:, h // 2, c, hl, :],
                                                lambda hl, c=c: keep.xT[:, bb, c, hl, :])
                                               for c in range(KD)]).then_inc(s_qps, 1)

            def keys(b, k):
                bb, h = head(b, k)
                split_matmuls(nc, psQK[:, :], [(lambda hl: keep.wkr[:, h, hl, :],
                                                lambda hl: keep.kvs[:, bb, hl, :])]).then_inc(s_kps, 1)

            def step(b, k):
                G = H * b + k
                for st in range(NT):
                    jj = 4 * G + st
                    if has(b, k, st):
                        if st == 0:
                            pe.wait_ge(s_klo, G + 1)
                            pe.wait_ge(s_qlo, H // 2 * b + k // 2 + 1)
                        upto(pe, s_exp, jj - 1)
                        q = Q[k % 4][:, st * P:(st + 1) * P]
                        nc.tensor.matmul(psS[st % 2][:, :], q, KH[k % 2][:, :], start=True, stop=False)
                        nc.tensor.matmul(psS[st % 2][:, :], q, KL[k % 2][:, :], start=False, stop=True).then_inc(s_S, 1)
                    if has(b, k, st - 3):
                        jt, t = jj - 3, (st + 1) % 4
                        pe.wait_ge(s_pn, jt + 1)
                        upto(pe, s_ev, jt - 1)
                        for hl in range(2):
                            for l in range(NT):
                                last = nc.tensor.transpose(psP[t % 2][:, hl, l, :], pn[t][:, hl, l * P:(l + 1) * P],
                                                           keep.ident16[:, :])
                        last.then_inc(s_T, 1)
                    if st == (k % 2) and has(b, k + 1, 0):
                        if k % 2:
                            pe.wait_ge(s_qlo, H // 2 * b + (k + 1) // 2 + 1)
                        else:
                            pe.wait_ge(s_klo, G + 1)
                        keys(b, k + 1)
                    if st < 2 and has(b, k - 2, 0):
                        bb, h = head(b, k - 2)
                        if st == 0:
                            pe.wait_ge(s_ev, 4 * G - 4)
                            upto(pe, s_clo, G - 3)
                        for l in (2 * st, 2 * st + 1):
                            kt = lambda hl: keep.kvs[:, B + bb, hl, l * P:(l + 1) * P]
                            pt = lambda hl: pT[k % 2][:, hl, l, :]
                            nc.tensor.matmul(psC[k % 2][:, :], kt(0), pt(0), start=l == 0, stop=False)
                            nc.tensor.matmul(psC[k % 2][:, :], kt(0), pt(1), start=False, stop=False)
                            last = nc.tensor.matmul(psC[k % 2][:, :], kt(1), pt(0), start=False, stop=l == 3)
                        if st == 1:
                            last.then_inc(s_ctx, 1)
                    if st >= 2 and has(b, k - 6, 0):
                        bb, r = head(b, k - 6)
                        g0, t = r // HG * HG, r % HG
                        if st == 2:
                            pe.wait_ge(s_clo, H * b + (k - 6) // HG * HG + HG)
                            upto(pe, s_acc, G - 6)
                        for h in (g0 + 2 * (st - 2), g0 + 2 * (st - 2) + 1):
                            cs = lambda hl: cx[:, hl, h % (2 * HG), t * P:(t + 1) * P]
                            ws = lambda hl: keep.wvo[:, h, hl, :]
                            nc.tensor.matmul(psO[:, :], cs(0), ws(0), start=h == g0, stop=False)
                            nc.tensor.matmul(psO[:, :], cs(0), ws(1), start=False, stop=False)
                            last = nc.tensor.matmul(psO[:, :], cs(1), ws(0), start=False, stop=h == g0 + HG - 1)
                        if st == 3:
                            last.then_inc(s_out, 1)
                    if st == 3 and k % 2 == 0 and has(b, k + 2, 0):
                        pe.wait_ge(s_klo, G + 2)
                        queries(b, k + 2)

            queries(0, 0)
            pe.wait_ge(s_qlo, 1)
            keys(0, 0)
            steps(pe, step)

        @block.scalar
        def _(a):
            def queries(b, k):
                G = H * b + k
                a.wait_ge(s_qps, H // 2 * b + k // 2 + 1)
                upto(a, s_S, 4 * G - 8)
                nc.scalar.activation(Q[k % 4][0:R, :], psQK[0:R, :], ACT.Copy, scale=1.0 / SC)
                nc.scalar.activation(Q[k % 4 + 1][R:P, :], psQK[R:P, :], ACT.Copy, scale=1.0 / SC).then_inc(s_qhi, 1)

            def keys(b, k):
                G = H * b + k
                a.wait_ge(s_kps, G + 1)
                upto(a, s_S, 4 * G - 4)
                nc.scalar.activation(KH[k % 2][:, :], psQK[:, :], ACT.Copy, scale=1.0 / SC).then_inc(s_khi, 1)

            def step(b, k):
                G = H * b + k
                for st in range(NT):
                    jj = 4 * G + st
                    if st == 0 and k % 2 and has(b, k + 1, 0):
                        queries(b, k + 1)
                    if st == k % 2 + 1 and has(b, k + 1, 0):
                        keys(b, k + 1)
                    if has(b, k, st):
                        a.wait_ge(s_max, jj + 1)
                        upto(a, s_pn, jj - 3)
                        nc.scalar.activation(p32[st][:, :], psS[st % 2][:, :], ACT.Exp, bias=nmx[:, st:st + 1],
                                             accum_out=rsum[:, st:st + 1]).then_inc(s_exp, 1)
                    if has(b, k, st - 3):
                        jt, t = jj - 3, (st + 1) % 4
                        hp = (k if st == 3 else k + 1) % 2
                        a.wait_ge(s_T, jt + 1)
                        if t == 0:
                            upto(a, s_ctx, G - 1)
                        nc.scalar.activation(pT[hp][:, :, :, t * P:(t + 1) * P], psP[t % 2][:, :, :, :],
                                             ACT.Copy).then_inc(s_ev, 1)
                    if has(b, k, st - 1):
                        t = (st - 1) % 4
                        a.wait_ge(s_r, jj)
                        upto(a, s_T, jj - 4)
                        nc.scalar.activation(pn[t][:, 0, :], p32[t][:, :], ACT.Copy, scale=rinv[:, t:t + 1]).then_inc(s_phi, 1)
                    if st == 2 and has(b, k - 2, 0):
                        h = head(b, k - 2)[1]
                        a.wait_ge(s_ctx, G - 1)
                        upto(a, s_out, H * b + (k - 2 - 2 * HG) // HG * HG + HG)
                        nc.scalar.activation(cx[:, 0, h % (2 * HG), :], psC[k % 2][:, :], ACT.Copy,
                                             scale=1.0 / PSC).then_inc(s_chi, 1)

            queries(0, 0)
            keys(0, 0)
            steps(a, step)

        @block.vector
        def _(v):
            def queries(b, k):
                v.wait_ge(s_qhi, H // 2 * b + k // 2 + 1)
                q0, q1 = Q[k % 4], Q[k % 4 + 1]
                nc.vector.scalar_tensor_tensor(q0[R:P, :], psQK[0:R, :], 1.0 / SC, q0[0:R, :],
                                               ALU.mult, ALU.subtract)
                nc.vector.scalar_tensor_tensor(q1[0:R, :], psQK[R:P, :], 1.0 / SC, q1[R:P, :],
                                               ALU.mult, ALU.subtract).then_inc(s_qlo, 1)

            def keys(b, k):
                v.wait_ge(s_khi, H * b + k + 1)
                nc.vector.scalar_tensor_tensor(KL[k % 2][:, :], psQK[:, :], 1.0 / SC, KH[k % 2][:, :],
                                               ALU.mult, ALU.subtract).then_inc(s_klo, 1)

            def step(b, k):
                G = H * b + k
                for st in range(NT):
                    jj = 4 * G + st
                    if has(b, k, st):
                        v.wait_ge(s_S, jj + 1)
                        nc.vector.tensor_reduce(nmx[:, st:st + 1], psS[st % 2][:, :], AX.X, ALU.max,
                                                negate=True).then_inc(s_max, 1)
                    if has(b, k, st - 1):
                        r = rinv[:, (st - 1) % 4:(st - 1) % 4 + 1]
                        v.wait_ge(s_exp, jj)
                        nc.vector.tensor_scalar(r, rsum[:, (st - 1) % 4:(st - 1) % 4 + 1], 1.0 / PSC, None, ALU.mult)
                        v.drain()
                        nc.vector.reciprocal(r, r).then_inc(s_r, 1)
                    if has(b, k, st - 2):
                        t = (st - 2) % 4
                        v.wait_ge(s_phi, jj - 1)
                        nc.vector.scalar_tensor_tensor(pn[t][:, 1, :], p32[t][:, :], rinv[:, t:t + 1], pn[t][:, 0, :],
                                                       ALU.mult, ALU.subtract).then_inc(s_pn, 1)
                    if st == 0 and k % 2 and has(b, k + 1, 0):
                        queries(b, k + 1)
                    if st == 2 and has(b, k + 1, 0):
                        keys(b, k + 1)
                    if st == 0 and has(b, k - 3, 0):
                        h = head(b, k - 3)[1]
                        v.wait_ge(s_chi, G - 2)
                        nc.vector.scalar_tensor_tensor(cx[:, 1, h % (2 * HG), :], psC[(k + 1) % 2][:, :], 1.0 / PSC,
                                                       cx[:, 0, h % (2 * HG), :], ALU.mult, ALU.subtract).then_inc(s_clo, 1)
                    if st == 1 and has(b, k - 7, 0):
                        bb, t = head(b, k - 7)
                        v.wait_ge(s_out, G - 6)
                        xs = keep.x[:, 4 * bb + t % HG, :]
                        nc.vector.scalar_tensor_tensor(xs, psO[:, :], 1.0 / SC, xs, ALU.mult, ALU.add).then_inc(s_acc, 1)

            queries(0, 0)
            keys(0, 0)
            steps(v, step)


def stage_store(nc, keep, out):
    with ExitStack() as ctx:
        sc = Scope(nc, ctx)
        s_out = sc.sem("stored")
        block = ctx.enter_context(nc.Block())

        @block.sync
        def _(sp):
            for b in range(B):
                sp.dma_start(out[b, :, :].rearrange("(t p) n -> p t n", p=P),
                             keep.x[:, 4 * b:4 * b + 4, :]).then_inc(s_out, 16)
            sp.wait_ge(s_out, 16 * B)


def build(nc, d, out, stages=9):
    scratch = Scratch(nc)
    with ExitStack() as ctx:
        sc = Scope(nc, ctx)
        keep = Keep(sc)
        with ExitStack() as c1:
            s1 = Scope(nc, c1)
            keep.normed(s1, "ffn0")
            gate_w = s1.sb("gate_w_split", [P, KD, 2, E], FP16)
            mv1, rstd1 = s1.sb("mv1", [P, B * NT, 2]), s1.sb("rstd1", [P, B * NT])
            stage_adjacency(nc, keep, d, scratch, gate_w, mv1, rstd1)
            if stages >= 2:
                xn = s1.sb("xn_rows", [P, B * NT, D])
                s_rows = s1.sem("rows_scattered")
                stage_router(nc, keep, gate_w, mv1, rstd1, xn)

                def scatter(pool):
                    for t in range(B * NT):
                        for c in range(2):
                            nc.gpsimd.indirect_dma_start(scratch.xs[:, :],
                                                         bass.IndirectOffsetOnAxis(keep.place[:, c, t:t + 1], 0),
                                                         xn[:, t, :], None).then_inc(s_rows, 16)
                    pool.wait_ge(s_rows, 32 * B * NT)

                stage_ffn(nc, keep, "f0", d["w13_s"], d["w2_s"], NS, NJ0, scatter)
        if stages >= 2:
            stage_experts(nc, keep, scratch, d["w13_e"], d["w2_e"])
            keep.normed(sc, "later")
            with ExitStack() as c2:
                keep.attention(Scope(nc, c2))
                stage_combine(nc, keep, scratch)
                if stages >= 3:
                    stage_attention(nc, keep)
        if stages >= 4:
            stage_ffn(nc, keep, "f1", d["w13_1"], d["w2_1"], NG1, NJ1, norm=True)
        stage_store(nc, keep, out)


def layout(i):
    import numpy as np

    f = np.float32

    def c(a):
        return np.ascontiguousarray(a)

    def swap(a):
        return np.concatenate([a[..., C // 2:], a[..., :C // 2]], axis=-1)

    def major(a):
        a = a.reshape(*a.shape[:-2], a.shape[-2] // P, P, a.shape[-1])
        return c(np.swapaxes(a, -3, -2))

    d = {}
    d["x"] = c(i["x"]).reshape(B * S, D)
    ctx = np.asarray(i["ctx_512"])
    ctxT = np.swapaxes(ctx, 1, 2)
    d["ctxT"] = c(ctxT)
    rot = swap(ctx)
    tok = lambda a: major(a).reshape(*a.shape[:-2], P, S)
    d["ctx_both"] = c(np.stack([ctxT, tok(ctx)]))
    d["ctx_rot"] = c(np.stack([np.swapaxes(rot, 1, 2), tok(rot)]))
    inv = (f(1.0) / np.power(f(10000.0), np.arange(0, C, 2, dtype=f) / f(C))).astype(f)
    ang = np.arange(S, dtype=f)[:, None] * inv[None, :]
    sin, cos = np.repeat(np.sin(ang), 2, axis=-1), np.repeat(np.cos(ang), 2, axis=-1)
    sin = np.concatenate([-sin[:, :C // 2], sin[:, C // 2:]], axis=-1)
    d["rope_cos"] = c(np.stack([cos.T, tok(cos)])).astype(f)
    d["rope_sin"] = c(np.stack([sin.T, tok(sin)])).astype(f)
    d["wq0T"], d["wk0T"] = c(np.asarray(i["L0_xattn_Wq"]).T), c(np.asarray(i["L0_xattn_Wk"]).T)
    d["gamma"] = c(np.broadcast_to(np.asarray(i["L0_xattn_gamma_raw"]).reshape(1, 1), (P, 1)))
    d["gate_wT"] = c(np.asarray(i["L0_ffn_gate_w"]).T)
    d["wq1"] = c(i["L1_xattn_Wq"])
    d["kcqT"] = c(np.swapaxes(np.asarray(i["L1_xattn_w_kc_q"]), 1, 2))
    d["wqr"] = c(i["L1_xattn_W_qr"])
    d["kckv"] = c(i["L1_xattn_w_kc_kv"])
    d["wkr"] = c(i["L1_xattn_W_kr"])
    d["woT"] = c(np.asarray(i["L1_xattn_Wo"]).T)

    def hidden_groups(w, n):
        out = np.zeros((w.shape[0], n, w.shape[2]), w.dtype)
        out[:, :w.shape[1]] = w
        return out

    def ffn(wg, wu, wd, n):
        up = [major(np.swapaxes(hidden_groups(w, n), 1, 2)) for w in (wg, wu)]
        return c(np.stack(up)), major(hidden_groups(np.swapaxes(wd, 1, 2), n))

    g = lambda a: np.asarray(i["L0_ffn_" + a])
    he = g("w1").shape[1]
    d["w13_e"], d["w2_e"] = ffn(g("w1"), g("w3"), g("w2"), NJ0 * P)
    d["w13_s"], d["w2_s"] = ffn(g("sw1").reshape(NS, he, D), g("sw3").reshape(NS, he, D),
                                np.swapaxes(g("sw2").reshape(D, NS, he), 0, 1), NJ0 * P)
    l = lambda a: np.asarray(i["L1_ffn_" + a])
    hw = NJ1 * P
    d["w13_1"], d["w2_1"] = ffn(l("w_gate").reshape(NG1, hw, D), l("w_up").reshape(NG1, hw, D),
                                np.swapaxes(l("w_down").reshape(D, NG1, hw), 0, 1), hw)
    return d


def kernel(**inputs):
    import concourse.bacc as _bacc
    from concourse.bass_utils import run_bass_kernel_spmd as _run

    nc = _bacc.Bacc("TRN2", target_bir_lowering=False, num_devices=1)
    arrays, aps = {}, {}
    for name, a in layout(inputs).items():
        arrays[f"in_{name}"] = a
        aps[name] = nc.dram_tensor(f"in_{name}", a.shape, mybir.dt.from_np(a.dtype), kind="ExternalInput").ap()
    out = nc.dram_tensor("out", (B, S, D), FP32, kind="ExternalOutput").ap()
    build(nc, aps, out, STAGES)
    return _run(nc, [arrays], core_ids=[0]).results[0]["out"]


STAGES = 9
```

```python
import concourse.bass as bass
from concourse import mybir
from contextlib import ExitStack

FP32 = mybir.dt.float32
FP16 = mybir.dt.float16
U32 = mybir.dt.uint32
ALU = mybir.AluOpType
ACT = mybir.ActivationFunctionType
AX = mybir.AxisListType

P = 128
B, S, D = 4, 512, 512
KD = D // P
NT = S // P
C = 128
TOPK = int(S * 0.3)
EPS = 1e-5
E = 8
HE = 384
HV = 352
NS, NJ0 = 2, 3
TILES = 2 * B * NT + E - 1
NG1, NJ1 = 4, 4
H, R, Q3 = 16, 64, 3
HG = 4
SC = 64.0
PSC = 1024.0
PROBES = 4
TARGET = TOPK - 4.5
Z_TARGET = 0.527
DENSITY = 178.0
FAR = 3.0e38
BISECT = 30
ZT = -(-TILES // E)


def ds(start, size):
    return bass.ds(start, size)


def start_at_one(eng, *sems):
    for s in sems:
        eng.nop().then_inc(s, 1)


def after(eng, sem, n):
    eng.wait_ge(sem, n + 1)


class Scope:

    def __init__(self, nc, ctx):
        self.nc, self.ctx = nc, ctx

    def sb(self, name, shape, dt=FP32):
        return self.ctx.enter_context(self.nc.sbuf_tensor(name, shape, dt))

    def ps(self, name, shape=(P, 512), dt=FP32):
        return self.ctx.enter_context(self.nc.psum_tensor(name, list(shape), dt))

    def sem(self, name):
        return self.ctx.enter_context(self.nc.semaphore(name))


class LayerNorm:

    def __init__(self, sc, keep, tag, xn, psT, mv=None, rstd=None):
        self.k, self.xn, self.psT = keep, xn, psT
        self.st = sc.sb(f"{tag}_stats", [P, NT, 6])
        self.mv, self.std, self.rstd = sc.sb(f"{tag}_meanvar", [P, NT, 2]), sc.sb(f"{tag}_std", [P, NT]), sc.sb(f"{tag}_rstd", [P, NT])
        self.all_mv, self.all_rstd = mv, rstd
        self.s_var = sc.sem(f"{tag}_var_ready")
        self.s_std = sc.sem(f"{tag}_std_ready")
        self.s_xn = sc.sem(f"{tag}_xn_ready")
        self.s_xt = sc.sem(f"{tag}_transposed")
        self.s_hi = sc.sem(f"{tag}_hi_ready")
        self.s_lo = sc.sem(f"{tag}_lo_ready")

    def stats(self, nc, v, b):
        for n in range(NT):
            nc.vector.bn_stats(self.st[:, n, :], self.k.x[:, 4 * b + n, :])
        nc.vector.drain()
        for n in range(NT):
            last = nc.vector.bn_aggr(self.mv[:, n, :], self.st[:, n, :])
        last.then_inc(self.s_var, 1)

    def root(self, nc, a, b, done):
        a.wait_ge(self.s_var, done + 1)
        nc.scalar.activation(self.std[:, :], self.mv[:, :, 1], ACT.Sqrt,
                             bias=self.k.eps[:, 0:1]).then_inc(self.s_std, 1)

    def inverse(self, nc, v, b, done):
        v.wait_ge(self.s_std, done + 1)
        nc.vector.reciprocal(self.rstd[:, :], self.std[:, :])
        nc.vector.drain()
        if self.all_mv is not None:
            nc.vector.tensor_copy(self.all_mv[:, ds(4 * b, NT), :], self.mv[:, :, :])
            nc.vector.tensor_copy(self.all_rstd[:, ds(4 * b, NT)], self.rstd[:, :])

    def rows(self, nc, v, b, waits=True):
        self.inverse(nc, v, b, b)
        for n in range(NT):
            if waits and b > 0:
                v.wait_ge(self.s_xt, 4 * b - 3 + n)
            nc.vector.tensor_scalar(self.xn[n][:, :], self.k.x[:, 4 * b + n, :], self.mv[:, n, 0:1],
                                    self.rstd[:, n:n + 1], ALU.subtract, ALU.mult).then_inc(self.s_xn, 1)

    def highs(self, nc, a, b):
        for n in range(NT):
            a.wait_ge(self.s_xt, 4 * b + n + 1)
            nc.scalar.activation(self.k.xT[:, b, :, 0, n * P:(n + 1) * P],
                                 self.psT[n][:, :].rearrange("p (k t) -> p k t", k=KD),
                                 ACT.Copy).then_inc(self.s_hi, 1)

    def lows(self, nc, v, b):
        for n in range(NT):
            v.wait_ge(self.s_hi, 4 * b + n + 1)
            nc.vector.tensor_tensor(self.k.xT[:, b, :, 1, n * P:(n + 1) * P],
                                    self.psT[n][:, :].rearrange("p (k t) -> p k t", k=KD),
                                    self.k.xT[:, b, :, 0, n * P:(n + 1) * P],
                                    ALU.subtract).then_inc(self.s_lo, 1)

    def transposes(self, nc, pe, b, waits=True):
        for n in range(NT):
            pe.wait_ge(self.s_xn, 4 * b + n + 1)
            if waits and b > 0:
                pe.wait_ge(self.s_lo, 4 * b - 3 + n)
            for k in range(KD):
                last = nc.tensor.transpose(self.psT[n][:, k * P:(k + 1) * P],
                                           self.xn[n][:, k * P:(k + 1) * P], self.k.ident[:, :])
            last.then_inc(self.s_xt, 1)


def split_matmuls(nc, out, pairs):
    n = len(pairs)
    for i, (lhs, rhs) in enumerate(pairs):
        nc.tensor.matmul(out, lhs(0), rhs(0), start=i == 0, stop=False)
        nc.tensor.matmul(out, lhs(0), rhs(1), start=False, stop=False)
        last = nc.tensor.matmul(out, lhs(1), rhs(0), start=False, stop=i == n - 1)
    return last


class Keep:

    def __init__(self, sc):
        self.x = sc.sb("x", [P, B * NT, D])
        self.ident = sc.sb("ident", [P, P])
        self.ident16 = sc.sb("ident16", [P, P], FP16)
        self.eps = sc.sb("eps", [P, 1])
        self.place = sc.sb("place_in_experts", [P, 2, B * NT], U32)
        self.gates = sc.sb("gates", [P, 2, B * NT])
        self.tile_expert = sc.sb("tile_expert", [P, TILES], mybir.dt.int32)

    def normed(self, sc, tag):
        self.xT = sc.sb(f"xT_{tag}", [P, B, KD, 2, S], FP16)

    def attention(self, sc):
        self.wvo = sc.sb("wvo", [P, H, 2, D], FP16)
        self.wqc = sc.sb("wqc", [P, H // 2, KD, 2, 2 * R], FP16)
        self.wkr = sc.sb("wkr", [P, H, 2, 2 * R], FP16)
        self.kvs = sc.sb("kvs", [P, 2 * B, 2, S], FP16)


class Scratch:

    def __init__(self, nc):
        t = lambda name, shape, dt: nc.dram_tensor(name, shape, dt).ap()
        self.wqc = t("wqc_scratch", (H // 2, P, KD * 2 * 2 * R), FP16)
        self.wvo = t("wvo_scratch", (H, P, 2 * D), FP16)
        self.wkr = t("wkr_scratch", (H, P, 4 * R), FP16)
        self.kvs = t("kvs_scratch", (2 * B, P, 2 * S), FP16)
        self.xs = t("expert_inputs", (E * ZT * P, D), FP32)
        self.ys = t("expert_outputs", (TILES * P, D), FP32)


def stage_adjacency(nc, keep, d, scratch, gate_w, mv1, rstd1, s8):
    with ExitStack() as ctx:
        sc = Scope(nc, ctx)
        ctxT = sc.sb("ctxT", [P, B, S])
        wq, wk = sc.sb("wq0", [P, P]), sc.sb("wk0", [P, P])
        gam = sc.sb("gam", [P, 8])
        GR, GS, OMG, HG = (gam[:, i:i + 1] for i in range(4))
        gate_raw = sc.sb("gate_raw", [P, KD, E])
        gate32 = sc.sb("gate32", [P, KD, E])
        QT, KT = sc.sb("QT", [P, S]), sc.sb("KT", [P, S])
        sim = sc.sb("sim", [P, 2, NT, S])
        A = sc.sb("A", [P, NT, S])
        hit = sc.sb("hit", [P, NT, S], mybir.dt.uint8)
        rest = sc.sb("rest", [P, NT, D])
        xn = [rest[:, i, :] for i in range(NT)]
        lo_t = sc.sb("lo_t", [P, NT])
        step = sc.sb("step", [P, NT])
        probe = sc.sb("probe", [P, NT])
        cnt = sc.sb("cnt", [P, NT])
        top = sc.sb("top", [P, NT])
        st1 = sc.sb("st1", [P, NT, 6])
        mvs = sc.sb("mvs", [P, NT, 2])
        sds = sc.sb("sds", [P, NT])
        cur, low2, high2, dif = (sc.sb(n, [P, 2, NT]) for n in ("cur", "low2", "high2", "dif"))
        off, nxt = sc.sb("off", [P, NT]), sc.sb("nxt", [P, NT])
        above, below, miss = (sc.sb(n, [P, NT], U32) for n in ("above", "below", "miss"))
        eight, pick = sc.sb("eight", [P, NT, 8]), sc.sb("pick", [P, NT, 8])
        place = sc.sb("place", [P, 8])
        bad, badi = sc.sb("bad", [P, 1]), sc.sb("badi", [1, 1], mybir.dt.int32)
        ones = sc.sb("ones", [P, 1])
        fa, fb = sc.sb("fa", [P, NT]), sc.sb("fb", [P, NT])
        st0 = sc.sb("st0", [P, NT, 6])
        mv0 = sc.sb("mv0", [P, NT, 2])
        std0, rstd0 = sc.sb("std0", [P, NT]), sc.sb("rstd0", [P, NT])
        r_wq = [sc.sb(f"r_wq{i}", [P, D]) for i in range(2)]
        r_kcq = [sc.sb(f"r_kcq{i}", [P, Q3, P]) for i in range(2)]
        r_qr = [sc.sb(f"r_qr{i}", [P, Q3, R]) for i in range(2)]
        r_kckv = [sc.sb(f"r_kckv{i}", [P, C]) for i in range(2)]
        r_wo = [sc.sb(f"r_wo{i}", [P, D]) for i in range(2)]
        r_kr = [sc.sb(f"r_kr{i}", [P, R]) for i in range(2)]
        wc = sc.sb("wc", [P, R])
        st_q = [sc.sb(f"st_q{i}", [P, KD, 2, 2, R], FP16) for i in range(2)]
        st_v = [sc.sb(f"st_v{i}", [P, 2, 2, D], FP16) for i in range(2)]
        st_k = [sc.sb(f"st_k{i}", [P, 2, 2, 2, R], FP16) for i in range(2)]
        st_c = [sc.sb(f"st_c{i}", [P, 2, S], FP16) for i in range(2)]
        zeros = sc.sb("zeros", [P, D])
        c_q, c_vo, c_kr = sc.sb("c_q", [P, KD, R]), sc.sb("c_vo", [P, D]), sc.sb("c_kr", [P, R])
        cos = sc.sb("cos", [P, S])
        sin = sc.sb("sin", [P, S])
        craw, crot = sc.sb("craw", [P, S]), sc.sb("crot", [P, S])
        rope = craw

        ps_proj = sc.ps("ps_proj")
        ps_sim = [sc.ps(f"ps_sim{i}") for i in range(2)]
        ps_T = [sc.ps(f"ps_T{i}") for i in range(2)]
        ps_wc = sc.ps("ps_wc")
        ps_wq = sc.ps("ps_wq")
        ps_vo = sc.ps("ps_vo")
        ps_bad = ps_wc
        ln = LayerNorm(sc, keep, "ln1", xn, ps_T + ps_sim, mv1, rstd1)

        s_ctx0, s_x0 = sc.sem("first_ctx_loaded"), sc.sem("first_x_loaded")
        s_ctx, s_w0, s_x = sc.sem("ctx_loaded"), sc.sem("w0_loaded"), sc.sem("x_loaded")
        s_gam, s_gw = sc.sem("gamma_loaded"), sc.sem("gate_loaded")
        s_id = sc.sem("ident_built")
        s_const = sc.sem("constants_built")
        s_sig = sc.sem("gamma_sigmoid")
        s_qps, s_qk = sc.sem("proj_in_psum"), sc.sem("proj_in_sbuf")
        s_sps, s_sim = sc.sem("sim_in_psum"), sc.sem("sim_in_sbuf")
        s_sgm, s_mask, s_at = sc.sem("sigmoid_done"), sc.sem("masked"), sc.sem("A_transposed")
        s_blend, s_blend_t = sc.sem("blended"), sc.sem("blended_tile")
        s_var0, s_std0 = sc.sem("var0_ready"), sc.sem("std0_ready")
        s_raw = [sc.sem(f"prep_raw{i}") for i in range(2)]
        s_wcps, s_wc = sc.sem("wc_in_psum"), sc.sem("wc_in_sbuf")
        s_pps, s_p32 = sc.sem("prep_in_psum"), sc.sem("prep_in_sbuf")
        s_phi, s_plo = sc.sem("prep_hi"), sc.sem("prep_lo")
        s_rope_in, s_rope, s_rhi, s_rlo = sc.sem("rope_in"), sc.sem("rope_done"), sc.sem("rope_hi"), sc.sem("rope_lo")
        s_tab = sc.sem("rope_tables")
        s_gate = sc.sem("gate_split")
        s_wst = [sc.sem(f"weights_stored{i}") for i in range(2)]
        s_cst = [sc.sem(f"context_stored{i}") for i in range(2)]
        s_zero, s_zst = sc.sem("zeros_ready"), sc.sem("zeros_stored")
        s_vars, s_sds = sc.sem("row_var"), sc.sem("row_sd")
        s_sc = sc.sem("router_scores_in_psum")
        s_bad, s_badsum = sc.sem("bad_rows"), sc.sem("bad_rows_summed")

        block = ctx.enter_context(nc.Block())

        @block.sync
        def _(sp):
            def load_head(h, par):
                rows = ds(h * P, P)
                sp.dma_start(r_wq[par][:, :], d["wq1"][rows, :]).then_inc(s_raw[par], 16)
                sp.dma_start(r_kcq[par][:, :, :], d["kcqT"][h, :, :].rearrange("(t p) k -> p t k", p=P)).then_inc(s_raw[par], 16)
                sp.dma_start(r_qr[par][:, :, :], d["wqr"][h, :, :].rearrange("(t p) r -> p t r", p=P)).then_inc(s_raw[par], 16)
                sp.dma_start(r_kckv[par][:, :], d["kckv"][h, :, :]).then_inc(s_raw[par], 16)
                sp.dma_start(r_wo[par][:, :], d["woT"][rows, :]).then_inc(s_raw[par], 16)
                sp.dma_start(r_kr[par][:, :], d["wkr"][h, :, :]).then_inc(s_raw[par], 16)

            def load_x(b, sem):
                sp.dma_start(keep.x[:, 4 * b:4 * b + 4, :],
                             d["x"][b * S:(b + 1) * S, :].rearrange("(t p) n -> p t n", p=P)).then_inc(sem, 16)

            start_at_one(sp, ln.s_lo, s_phi, s_rhi, s_blend, s_qk, s_wc, s_plo, s_p32, *s_wst, *s_cst)
            sp.dma_start(ctxT[:, 0, :], d["ctxT"][0, :, :]).then_inc(s_ctx0, 16)
            sp.dma_start(wq[:, :], d["wq0T"]).then_inc(s_w0, 16)
            sp.dma_start(wk[:, :], d["wk0T"]).then_inc(s_w0, 16)
            sp.dma_start(GR, d["gamma"]).then_inc(s_gam, 16)
            load_x(0, s_x0)
            for par in range(2):
                load_head(par, par)
            sp.dma_start(ctxT[:, 1:B, :], d["ctxT"][1:B, :, :].rearrange("b p s -> p b s")).then_inc(s_ctx, 16)
            for b in range(1, B):
                load_x(b, s_x)
            sp.dma_start(gate_raw[:, :, :], d["gate_wT"].rearrange("(k p) e -> p k e", p=P)).then_inc(s_gw, 16)
            sp.wait_ge(s_zero, 1)

            def batch(b, more):
                for hh in range(4):
                    pp = hh // 2
                    if more or hh < 2:
                        after(sp, s_phi, 12 * b + 3 * hh + 3)
                        load_head(4 * b + hh + 2, hh % 2)
                    if hh % 2:
                        pair = 2 * b + pp
                        after(sp, s_plo, 2 * pair + 2)
                        sp.dma_start(scratch.wqc[pair, :, :], st_q[pp][:, :, :, :, :].rearrange("p k l h r -> p (k l h r)")).then_inc(s_wst[pp], 16)
                        sp.dma_start(scratch.wvo[ds(2 * pair, 2), :, :].rearrange("h p n -> p h n"),
                                     st_v[pp][:, :, :, :].rearrange("p h l n -> p h (l n)")).then_inc(s_wst[pp], 16)
                        sp.dma_start(scratch.wkr[ds(2 * pair, 2), :, :].rearrange("h p n -> p h n"),
                                     st_k[pp][:, :, :, :, :].rearrange("p h l a r -> p h (l a r)")).then_inc(s_wst[pp], 16)
                for u in range(2):
                    rows = scratch.xs[ds((2 * b + u) * (ZT * P), ZT * P), :]
                    sp.dma_start(rows.rearrange("(t p) n -> p t n", p=P),
                                 zeros[:, :].unsqueeze(1).to_broadcast([P, ZT, D])).then_inc(s_zst, 16)
                for u in range(2):
                    sp.wait_ge(s_rlo, 2 * b + u + 1)
                    sp.dma_start(scratch.kvs[2 * b + u, :, :],
                                 st_c[u][:, :, :].rearrange("p l n -> p (l n)")).then_inc(s_cst[u], 16)

            with sp.Fori(0, B - 1) as b:
                batch(b, True)
            batch(B - 1, False)
            for pp in range(2):
                sp.wait_ge(s_wst[pp], 48 * B + 1)
                sp.wait_ge(s_cst[pp], 16 * B + 1)
            sp.wait_ge(s_zst, 16 * E)

        @block.gpsimd
        def _(pool):
            nc.gpsimd.memset(keep.ident[:, :], 0.0)
            nc.gpsimd.memset(keep.eps[:, :], EPS)
            nc.gpsimd.memset(ones[:, :], 1.0)
            nc.gpsimd.memset(zeros[:, :], 0.0).then_inc(s_zero, 1)
            for j in range(8):
                nc.gpsimd.memset(place[:, j:j + 1], float(j))
            pool.drain()
            nc.gpsimd.affine_select(out=keep.ident[:, :], in_=keep.ident[:, :], compare_op=ALU.not_equal,
                                    fill=1.0, base=0, pattern=[[-1, P]], channel_multiplier=1)
            pool.drain()
            nc.gpsimd.tensor_copy(keep.ident16[:, :], keep.ident[:, :]).then_inc(s_id, 1)
            pool.wait_ge(s_gw, 16)
            nc.gpsimd.tensor_scalar(gate32[:, :, :], gate_raw[:, :, :], SC, 1.0, ALU.mult, ALU.mult)
            pool.drain()
            nc.gpsimd.tensor_copy(gate_w[:, :, 0, :], gate32[:, :, :])
            pool.drain()
            nc.gpsimd.tensor_tensor(gate_w[:, :, 1, :], gate32[:, :, :], gate_w[:, :, 0, :],
                                    ALU.subtract).then_inc(s_gate, 1)
            def load_context(i, b):
                pool.dma_start(craw[:, :], d["ctx_both"][i, b, :, :]).then_inc(s_rope_in, 16)
                pool.dma_start(crot[:, :], d["ctx_rot"][i, b, :, :]).then_inc(s_rope_in, 16)

            with pool.Fori(0, 2) as i:
                after(pool, s_rhi, 4 * i)
                pool.dma_start(cos[:, :], d["rope_cos"][i, :, :]).then_inc(s_tab, 16)
                pool.dma_start(sin[:, :], d["rope_sin"][i, :, :]).then_inc(s_tab, 16)
                load_context(i, 0)
                for par in range(2):
                    for hh in range(4):
                        n = 8 * i + 4 * par + hh
                        pp, e = hh // 2, hh % 2
                        after(pool, s_phi, 3 * n + 3)
                        nc.gpsimd.tensor_tensor(st_q[pp][:, :, 1, e, :], c_q[:, :, :], st_q[pp][:, :, 0, e, :], ALU.subtract)
                        nc.gpsimd.tensor_tensor(st_v[pp][:, e, 1, :], c_vo[:, :], st_v[pp][:, e, 0, :], ALU.subtract)
                        for two in range(2):
                            last = nc.gpsimd.tensor_tensor(st_k[pp][:, e, 1, two, :], c_kr[:, :],
                                                           st_k[pp][:, e, 0, two, :], ALU.subtract)
                        last.then_inc(s_plo, 1)
                    for u in range(2):
                        n = 4 * i + 2 * par + u
                        pool.wait_ge(s_tab, 32 * i + 32)
                        pool.wait_ge(s_rope_in, 32 * n + 32)
                        nc.gpsimd.tensor_tensor(craw[:, :], craw[:, :], cos[:, :], ALU.mult)
                        nc.gpsimd.tensor_tensor(crot[:, :], crot[:, :], sin[:, :], ALU.mult)
                        pool.drain()
                        nc.gpsimd.tensor_tensor(rope[:, :], craw[:, :], crot[:, :], ALU.add).then_inc(s_rope, 1)
                        after(pool, s_rhi, n + 1)
                        nc.gpsimd.tensor_tensor(st_c[u][:, 1, :], rope[:, :], st_c[u][:, 0, :],
                                                ALU.subtract).then_inc(s_rlo, 1)
                        pool.drain()
                        if 2 * par + u < B - 1:
                            load_context(i, 2 * par + u + 1)

        @block.scalar
        def _(a):
            a.wait_ge(s_gam, 16)
            nc.scalar.activation(GS, GR, ACT.Sigmoid).then_inc(s_sig, 1)
            a.wait_ge(s_id, 1)
            def similarities(b):
                for w, T in enumerate((QT, KT)):
                    a.wait_ge(s_qps, 2 * b + w + 1)
                    nc.scalar.activation(T[:, :], ps_proj[:, :], ACT.Copy).then_inc(s_qk, 1)
                for n in range(NT):
                    a.wait_ge(s_sps, 4 * b + n + 1)
                    nc.scalar.activation(sim[:, b % 2, n, :], ps_sim[n % 2][:, :], ACT.Copy,
                                         scale=1.0 / (float(C // 4) ** 0.5 * 4)).then_inc(s_sim, 1)

            def rotated(b):
                for u in range(2):
                    a.wait_ge(s_rope, 2 * b + u + 1)
                    after(a, s_cst[u], 16 * b)
                    nc.scalar.activation(st_c[u][:, 0, :], rope[:, :], ACT.Copy).then_inc(s_rhi, 1)

            def deviations(b):
                a.wait_ge(s_vars, b + 1)
                nc.scalar.activation(sds[:, :], mvs[:, :, 1], ACT.Sqrt).then_inc(s_sds, 1)
                a.wait_ge(s_var0, b + 1)
                nc.scalar.activation(std0[:, :], mv0[:, :, 1], ACT.Sqrt, bias=keep.eps[:, 0:1]).then_inc(s_std0, 1)

            def batch(b, more):
                after(a, s_blend, b)
                nc.scalar.activation(A[:, :, :], sim[:, b % 2, :, :], ACT.Sigmoid).then_inc(s_sgm, 1)
                for hh in range(4):
                    n = 4 * b + hh
                    q = hh % 2
                    a.wait_ge(s_wcps, n + 1)
                    nc.scalar.activation(wc[:, :], ps_wc[:, 0:R], ACT.Copy).then_inc(s_wc, 1)
                    a.wait_ge(s_pps, n + 1)
                    after(a, s_plo, n)
                    nc.scalar.activation(c_q[:, :, :], ps_wq[:, 0:KD * R].rearrange("p (k r) -> p k r", k=KD),
                                         ACT.Copy, scale=SC)
                    nc.scalar.activation(c_vo[:, :], ps_vo[:, :], ACT.Copy, scale=SC).then_inc(s_p32, 1)
                    nc.scalar.activation(c_kr[:, :], r_kr[q][:, :], ACT.Copy, scale=SC)
                    a.drain()
                    pp, e = hh // 2, hh % 2
                    after(a, s_wst[pp], 48 * b)
                    nc.scalar.activation(st_q[pp][:, :, 0, e, :], c_q[:, :, :], ACT.Copy).then_inc(s_phi, 1)
                    nc.scalar.activation(st_v[pp][:, e, 0, :], c_vo[:, :], ACT.Copy).then_inc(s_phi, 1)
                    nc.scalar.activation(st_k[pp][:, e, 0, :, :], c_kr[:, :].unsqueeze(1).to_broadcast([P, 2, R]),
                                         ACT.Copy).then_inc(s_phi, 1)
                if more:
                    similarities(b + 1)
                else:
                    rotated(b)
                ln.root(nc, a, b, b)
                if more:
                    deviations(b + 1)
                ln.highs(nc, a, b)
                if more:
                    rotated(b)

            similarities(0)
            deviations(0)
            with a.Fori(0, B - 1) as b:
                batch(b, True)
            batch(B - 1, False)
            a.wait_ge(s_sc, 1)
            nc.scalar.activation(s8[:, :, :], ps_proj[:, 0:B * NT * E].rearrange("p (t e) -> p t e", e=E),
                                 ACT.Copy, scale=1.0 / SC)

        def row_stats(v, b, par):
            for n in range(NT):
                nc.vector.bn_stats(st0[:, n, :], keep.x[:, 4 * b + n, :])
            v.wait_ge(s_sim, 4 * b + 4)
            for n in range(NT):
                nc.vector.bn_stats(st1[:, n, :], sim[:, par, n, 0:S // 2])
            v.drain()
            for n in range(NT):
                last = nc.vector.bn_aggr(mv0[:, n, :], st0[:, n, :])
            last.then_inc(s_var0, 1)
            for n in range(NT):
                last = nc.vector.bn_aggr(mvs[:, n, :], st1[:, n, :])
            last.then_inc(s_vars, 1)

        def search(v, b, par):
            v.wait_ge(s_sds, b + 1)
            for dst, z in ((cur, Z_TARGET), (low2, -3.0), (high2, 3.0)):
                nc.vector.scalar_tensor_tensor(dst[:, 0, :], sds[:, :], z, mvs[:, :, 0], ALU.mult, ALU.add)
            nc.vector.memset(low2[:, 1, :], float(S))
            nc.vector.memset(high2[:, 1, :], 0.0)
            v.drain()
            for k in range(PROBES):
                for n in range(NT):
                    nc.vector.tensor_scalar(hit[:, n, :], sim[:, par, n, :], cur[:, 0, n:n + 1], None,
                                            ALU.is_ge, ALU.add, accum_out=cur[:, 1, n:n + 1])
                v.drain()
                nc.vector.tensor_scalar(above[:, :], cur[:, 1, :], TARGET, None, ALU.is_gt)
                nc.vector.tensor_scalar(below[:, :], cur[:, 1, :], TARGET, None, ALU.is_lt)
                nc.vector.tensor_scalar(off[:, :], cur[:, 1, :], TARGET - 4.0, None, ALU.is_lt)
                v.drain()
                nc.vector.copy_predicated(low2[:, :, :], above[:, :].unsqueeze(1).to_broadcast([P, 2, NT]), cur[:, :, :])
                nc.vector.copy_predicated(high2[:, :, :], below[:, :].unsqueeze(1).to_broadcast([P, 2, NT]), cur[:, :, :])
                nc.vector.scalar_tensor_tensor(miss[:, :], cur[:, 1, :], TARGET + 4.0, off[:, :], ALU.is_gt, ALU.add)
                v.drain()
                if k == 0:
                    nc.vector.tensor_scalar(off[:, :], cur[:, 1, :], TARGET, 1.0 / DENSITY, ALU.subtract, ALU.mult)
                    v.drain()
                    nc.vector.tensor_tensor(off[:, :], off[:, :], sds[:, :], ALU.mult)
                    v.drain()
                    nc.vector.tensor_tensor(nxt[:, :], cur[:, 0, :], off[:, :], ALU.add)
                else:
                    nc.vector.tensor_tensor(dif[:, :, :], high2[:, :, :], low2[:, :, :], ALU.subtract)
                    nc.vector.tensor_scalar(off[:, :], low2[:, 1, :], TARGET, None, ALU.subtract)
                    v.drain()
                    nc.vector.reciprocal(dif[:, 1, :], dif[:, 1, :])
                    nc.vector.tensor_tensor(off[:, :], off[:, :], dif[:, 0, :], ALU.mult)
                    v.drain()
                    nc.vector.tensor_tensor(off[:, :], off[:, :], dif[:, 1, :], ALU.mult)
                    v.drain()
                    nc.vector.tensor_tensor(nxt[:, :], low2[:, 0, :], off[:, :], ALU.subtract)
                v.drain()
                nc.vector.copy_predicated(cur[:, 0, :], miss[:, :], nxt[:, :])
                v.drain()
            for n in range(NT):
                nc.vector.tensor_scalar(hit[:, n, :], sim[:, par, n, :], cur[:, 0, n:n + 1], None,
                                        ALU.is_ge, ALU.add, accum_out=cur[:, 1, n:n + 1])
            v.drain()
            nc.vector.tensor_scalar(off[:, :], cur[:, 1, :], TARGET - 4.0, None, ALU.is_lt)
            v.drain()
            nc.vector.scalar_tensor_tensor(off[:, :], cur[:, 1, :], TARGET + 4.0, off[:, :], ALU.is_gt, ALU.add,
                                           accum_out=bad[:, 0:1])
            v.drain()
            v.nop().then_inc(s_bad, 1)
            for n in range(NT):
                nc.vector.scalar_tensor_tensor(rest[:, n % 2, :], hit[:, n, :], -FAR, sim[:, par, n, :], ALU.mult, ALU.add)
                v.drain()
                nc.vector.max(eight[:, n, :], rest[:, n % 2, :])
            nc.vector.tensor_scalar(off[:, :], cur[:, 1, :], -1.0, TOPK - 1.0, ALU.mult, ALU.add)
            v.drain()
            nc.vector.tensor_tensor(pick[:, :, :], place[:, :].unsqueeze(1).to_broadcast([P, NT, 8]),
                                    off[:, :].unsqueeze(2).to_broadcast([P, NT, 8]), ALU.is_equal)
            v.drain()
            nc.vector.tensor_tensor(pick[:, :, :], pick[:, :, :], eight[:, :, :], ALU.mult)
            v.drain()
            nc.vector.tensor_reduce(lo_t[:, :], pick[:, :, :], AX.X, ALU.add)
            v.wait_ge(s_badsum, b + 1)
            nc.vector.tensor_copy(badi[:, :], ps_bad[0:1, 0:1])
            v.drain()
            failed = v.value_load(badi[0:1, 0:1], min_val=0, max_val=P * NT)
            with v.If(failed > 0):
                bisect(v, par)

        def bisect(v, par):
            nc.vector.tensor_reduce(lo_t[:, :], sim[:, par, :, :], AX.X, ALU.min)
            nc.vector.tensor_reduce(top[:, :], sim[:, par, :, :], AX.X, ALU.max)
            v.drain()
            nc.vector.tensor_tensor(step[:, :], top[:, :], lo_t[:, :], ALU.subtract)
            v.drain()
            with v.Fori(0, BISECT):
                nc.vector.tensor_scalar(step[:, :], step[:, :], 0.5, None, ALU.mult)
                v.drain()
                nc.vector.tensor_tensor(probe[:, :], lo_t[:, :], step[:, :], ALU.add)
                v.drain()
                for n in range(NT):
                    nc.vector.tensor_scalar(hit[:, n, :], sim[:, par, n, :], probe[:, n:n + 1], None,
                                            ALU.is_ge, ALU.add, accum_out=cnt[:, n:n + 1])
                v.drain()
                nc.vector.scalar_tensor_tensor(probe[:, :], cnt[:, :], TOPK - 0.5, step[:, :],
                                               ALU.is_ge, ALU.mult)
                v.drain()
                nc.vector.tensor_tensor(lo_t[:, :], lo_t[:, :], probe[:, :], ALU.add)
                v.drain()

        @block.vector
        def _(v):
            v.wait_ge(s_sig, 1)
            nc.vector.tensor_scalar(OMG, GS, -1.0, 1.0, ALU.mult, ALU.add)
            nc.vector.tensor_scalar(HG, GS, 0.5, None, ALU.mult)
            v.wait_ge(s_x0, 16)
            row_stats(v, 0, 0)

            def batch(b, more):
                par = b % 2
                search(v, b, par)
                v.wait_ge(s_sgm, b + 1)
                for n in range(NT):
                    nc.vector.scalar_tensor_tensor(A[:, n, :], sim[:, par, n, :], lo_t[:, n:n + 1], A[:, n, :],
                                                   ALU.is_ge, ALU.mult).then_inc(s_mask, 1)
                v.wait_ge(s_std0, b + 1)
                nc.vector.reciprocal(rstd0[:, :], std0[:, :])
                v.drain()
                nc.vector.tensor_tensor(fb[:, :], mv0[:, :, 0], rstd0[:, :], ALU.mult)
                nc.vector.tensor_scalar(fa[:, :], rstd0[:, :], OMG, 1.0, ALU.mult, ALU.add)
                v.drain()
                nc.vector.tensor_scalar(fb[:, :], fb[:, :], OMG, -1.0, ALU.mult, ALU.mult)
                v.drain()
                for n in range(NT):
                    nc.vector.tensor_scalar(keep.x[:, 4 * b + n, :], keep.x[:, 4 * b + n, :], fa[:, n:n + 1],
                                            fb[:, n:n + 1], ALU.mult, ALU.add)
                v.drain()
                for n in range(NT):
                    nc.vector.scalar_tensor_tensor(keep.x[:, 4 * b + n, :], A[:, n, :], HG, keep.x[:, 4 * b + n, :],
                                                   ALU.mult, ALU.add)
                v.drain()
                for n in range(NT):
                    v.wait_ge(s_at, 4 * b + n + 1)
                    nc.vector.scalar_tensor_tensor(keep.x[:, 4 * b + n, :], ps_T[n % 2][:, :], HG,
                                                   keep.x[:, 4 * b + n, :], ALU.mult, ALU.add).then_inc(s_blend_t, 1)
                v.drain()
                v.nop().then_inc(s_blend, 1)
                ln.stats(nc, v, b)
                if more:
                    v.wait_ge(s_x, 16 * (B - 1))
                    row_stats(v, b + 1, (b + 1) % 2)
                ln.rows(nc, v, b, waits=False)
                ln.lows(nc, v, b)

            with v.Fori(0, B - 1) as b:
                batch(b, True)
            batch(B - 1, False)

        @block.tensor
        def _(pe):
            pe.wait_ge(s_ctx0, 16)
            pe.wait_ge(s_w0, 32)
            pe.wait_ge(s_id, 1)
            def similarities(b):
                for w, W in enumerate((wq, wk)):
                    after(pe, s_qk, 2 * b + w)
                    nc.tensor.matmul(ps_proj[:, :], W[:, :], ctxT[:, b, :], start=True, stop=True).then_inc(s_qps, 1)
                after(pe, s_qk, 2 * b + 2)
                for n in range(NT):
                    if n >= 2:
                        pe.wait_ge(s_sim, 4 * b + n - 1)
                    nc.tensor.matmul(ps_sim[n % 2][:, :], QT[:, n * P:(n + 1) * P], KT[:, :],
                                     start=True, stop=True).then_inc(s_sps, 1)

            def scores(b):
                for n in range(NT):
                    col = (4 * b + n) * E
                    last = split_matmuls(nc, ps_proj[:, col:col + E],
                                         [(lambda hl, k=k: keep.xT[:, b, k, hl, n * P:(n + 1) * P],
                                           lambda hl, k=k: gate_w[:, k, hl, :]) for k in range(KD)])
                return last

            def batch(b, more):
                for hh in range(4):
                    n = 4 * b + hh
                    q = hh % 2
                    pe.wait_ge(s_raw[q], 96 * (2 * b + hh // 2 + 1))
                    after(pe, s_wc, n)
                    for t in range(Q3):
                        last = nc.tensor.matmul(ps_wc[:, 0:R], r_kcq[q][:, t, :], r_qr[q][:, t, :],
                                                start=t == 0, stop=t == Q3 - 1)
                    last.then_inc(s_wcps, 1)
                    after(pe, s_p32, n)
                    nc.tensor.matmul(ps_vo[:, :], r_kckv[q][:, :], r_wo[q][:, :], start=True, stop=True)
                    after(pe, s_wc, n + 1)
                    for k in range(KD):
                        last = nc.tensor.matmul(ps_wq[:, k * R:(k + 1) * R], r_wq[q][:, k * P:(k + 1) * P],
                                                wc[:, :], start=True, stop=True)
                    last.then_inc(s_pps, 1)
                pe.wait_ge(s_bad, b + 1)
                nc.tensor.matmul(ps_bad[0:1, 0:1], bad[:, 0:1], ones[:, 0:1], start=True, stop=True).then_inc(s_badsum, 1)
                if more:
                    pe.wait_ge(s_ctx, 16)
                    similarities(b + 1)
                else:
                    after(pe, s_qk, 2 * B)
                    pe.wait_ge(s_gate, 1)
                    pe.wait_ge(ln.s_lo, 4 * (B - 1) + 1)
                    for bb in range(B - 1):
                        scores(bb)
                pe.wait_ge(s_mask, 4 * b + 4)
                for n in range(NT):
                    if n >= 2:
                        pe.wait_ge(s_blend_t, 4 * b + n - 1)
                    for m in range(NT):
                        last = nc.tensor.transpose(ps_T[n % 2][:, m * P:(m + 1) * P],
                                                   A[:, m, n * P:(n + 1) * P], keep.ident[:, :])
                    last.then_inc(s_at, 1)
                pe.wait_ge(s_blend_t, 4 * b + 4)
                if more:
                    pe.wait_ge(s_sim, 4 * b + 8)
                ln.transposes(nc, pe, b, waits=False)
                if not more:
                    pe.wait_ge(ln.s_lo, 4 * B + 1)
                    scores(B - 1).then_inc(s_sc, 1)

            similarities(0)
            with pe.Fori(0, B - 1) as b:
                batch(b, True)
            batch(B - 1, False)


def stage_router(nc, keep, s8, mv1, rstd1, xn, load_ahead):
    T = B * NT
    with ExitStack() as ctx:
        sc = Scope(nc, ctx)
        m8 = sc.sb("sorted8", [P, T, E])
        i8 = sc.sb("index8", [P, T, E], U32)
        if8 = sc.sb("index8f", [P, T, 2])
        iota_i = sc.sb("iota_i", [P, TILES], mybir.dt.int32)
        iota = sc.sb("iota", [P, TILES])
        marks = sc.sb("marks", [P, T])
        tri = sc.sb("tri", [P, P])
        ones = sc.sb("ones_pp", [P, P])
        hot = sc.sb("hot", [P, 2, T, E])
        both = sc.sb("both", [P, T, E])
        cum = [sc.sb(f"cum{i}", [P, T, E]) for i in range(2)]
        total = sc.sb("total", [P, T, E])
        fill = sc.sb("fill", [P, E, T])
        nt = sc.sb("nt", [P, E])
        end = [sc.sb(f"end{i}", [P, E]) for i in range(2)]
        past = sc.sb("past", [P, TILES, E])
        tef = sc.sb("tef", [P, TILES])
        prod = sc.sb("prod", [P, 2, T, E])
        placef = sc.sb("placef", [P, 2, T])
        tot = sc.sb("tot", [P, T])
        shift = sc.sb("shift", [P, T])
        s_shift = sc.sem("shift_ready")
        ps_in, ps_all = sc.ps("ps_before"), sc.ps("ps_total")
        s_cen, s_exp, s_iota, s_hot, s_cnt = (sc.sem(n) for n in (
            "router_centred", "router_exp", "iota_ready", "choices_ready", "choices_counted"))
        block = ctx.enter_context(nc.Block())

        @block.sync
        def _(sp):
            load_ahead(sp)

        @block.tensor
        def _(pe):
            pe.wait_ge(s_iota, 1)
            pe.wait_ge(s_hot, 1)
            rhs = both[:, :, :].rearrange("p t e -> p (t e)")
            nc.tensor.matmul(ps_in[:, 0:T * E], tri[:, :], rhs, start=True, stop=True)
            nc.tensor.matmul(ps_all[:, 0:T * E], ones[:, :], rhs, start=True, stop=True).then_inc(s_cnt, 1)

        @block.gpsimd
        def _(pool):
            nc.gpsimd.iota(iota_i[:, :], pattern=[[1, TILES]], base=0, channel_multiplier=0)
            nc.gpsimd.memset(ones[:, :], 1.0)
            pool.drain()
            nc.gpsimd.tensor_copy(iota[:, :], iota_i[:, :])
            nc.gpsimd.affine_select(out=tri[:, :], in_=ones[:, :], compare_op=ALU.is_gt, fill=0.0, base=0,
                                    pattern=[[1, P]], channel_multiplier=-1)
            pool.drain()
            nc.gpsimd.tensor_scalar(marks[:, :], iota[:, 0:T], float(P), 1.0, ALU.mult, ALU.mult).then_inc(s_iota, 1)

        @block.scalar
        def _(a):
            a.wait_ge(s_cen, 1)
            nc.scalar.activation(s8[:, :, :], s8[:, :, :], ACT.Exp).then_inc(s_exp, 1)
            a.wait_ge(s_shift, 1)
            for t in range(T):
                nc.scalar.activation(xn[:, t, :], keep.x[:, t, :], ACT.Identity, bias=shift[:, t:t + 1],
                                     scale=rstd1[:, t:t + 1])

        @block.vector
        def _(v):
            for t in range(T):
                nc.vector.max(m8[:, t, :], s8[:, t, :])
            v.drain()
            for t in range(T):
                nc.vector.max_index(i8[:, t, :], m8[:, t, :], s8[:, t, :])
            v.drain()
            nc.vector.tensor_tensor(s8[:, :, :], s8[:, :, :], m8[:, :, 0:1].to_broadcast([P, T, E]),
                                    ALU.subtract).then_inc(s_cen, 1)
            nc.vector.tensor_copy(if8[:, :, :], i8[:, :, 0:2])
            v.drain()
            v.wait_ge(s_iota, 1)
            it = iota[:, 0:E].unsqueeze(1).to_broadcast([P, T, E])
            for c in range(2):
                nc.vector.tensor_tensor(hot[:, c, :, :], it, if8[:, :, c:c + 1].to_broadcast([P, T, E]), ALU.is_equal)
            v.drain()
            nc.vector.tensor_tensor(both[:, :, :], hot[:, 0, :, :], hot[:, 1, :, :], ALU.add).then_inc(s_hot, 1)
            nc.vector.scalar_tensor_tensor(shift[:, :], mv1[:, :, 0], -1.0, rstd1[:, :], ALU.mult, ALU.mult).then_inc(s_shift, 1)
            v.wait_ge(s_exp, 1)
            nc.vector.tensor_reduce(tot[:, :], s8[:, :, :], AX.X, ALU.add)
            for c in range(2):
                nc.vector.tensor_tensor(prod[:, c, :, :], hot[:, c, :, :], s8[:, :, :], ALU.mult)
            v.drain()
            nc.vector.tensor_scalar(tot[:, :], tot[:, :], SC, None, ALU.mult)
            nc.vector.tensor_reduce(keep.gates[:, :, :], prod[:, :, :, :], AX.X, ALU.add)
            v.drain()
            nc.vector.reciprocal(tot[:, :], tot[:, :])
            v.drain()
            for c in range(2):
                nc.vector.tensor_tensor(keep.gates[:, c, :], keep.gates[:, c, :], tot[:, :], ALU.mult)
            v.wait_ge(s_cnt, 1)
            al = ps_all[:, 0:T * E].rearrange("p (t e) -> p t e", e=E)
            nc.vector.tensor_copy(total[:, :, :], al)
            nc.vector.tensor_copy(cum[0][:, :, :], al)
            v.drain()
            for k in range(4):
                w, src, dst = 1 << k, cum[k % 2], cum[(k + 1) % 2]
                nc.vector.tensor_copy(dst[:, 0:w, :], src[:, 0:w, :])
                nc.vector.tensor_tensor(dst[:, w:T, :], src[:, w:T, :], src[:, 0:T - w, :], ALU.add)
                v.drain()
            nc.vector.tensor_tensor(fill[:, :, :], cum[0][:, T - 1, :].unsqueeze(2).to_broadcast([P, E, T]),
                                    marks[:, :].unsqueeze(1).to_broadcast([P, E, T]), ALU.is_gt)
            v.drain()
            nc.vector.tensor_reduce(nt[:, :], fill[:, :, :], AX.X, ALU.add)
            v.drain()
            nc.vector.tensor_scalar(nt[:, :], nt[:, :], 1.0, None, ALU.max)
            v.drain()
            nc.vector.tensor_copy(end[0][:, :], nt[:, :])
            v.drain()
            for k in range(3):
                w, src, dst = 1 << k, end[k % 2], end[(k + 1) % 2]
                nc.vector.tensor_copy(dst[:, 0:w], src[:, 0:w])
                nc.vector.tensor_tensor(dst[:, w:E], src[:, w:E], src[:, 0:E - w], ALU.add)
                v.drain()
            nc.vector.tensor_tensor(past[:, :, :], iota[:, :].unsqueeze(2).to_broadcast([P, TILES, E]),
                                    end[1][:, :].unsqueeze(1).to_broadcast([P, TILES, E]), ALU.is_ge)
            nc.vector.tensor_tensor(nt[:, :], end[1][:, :], nt[:, :], ALU.subtract)
            nc.vector.tensor_tensor(cum[0][:, :, :], cum[0][:, :, :], total[:, :, :], ALU.subtract)
            v.drain()
            nc.vector.tensor_reduce(tef[:, :], past[:, :, :], AX.X, ALU.add)
            nc.vector.tensor_scalar(nt[:, :], nt[:, :], float(P), None, ALU.mult)
            nc.vector.tensor_tensor(cum[0][:, :, :], cum[0][:, :, :],
                                    ps_in[:, 0:T * E].rearrange("p (t e) -> p t e", e=E), ALU.add)
            v.drain()
            nc.vector.tensor_scalar(keep.tile_expert[:, :], tef[:, :], E - 1.0, None, ALU.min)
            nc.vector.tensor_tensor(cum[0][:, :, :], cum[0][:, :, :],
                                    nt[:, :].unsqueeze(1).to_broadcast([P, T, E]), ALU.add)
            v.drain()
            for c in range(2):
                nc.vector.tensor_tensor(prod[:, c, :, :], hot[:, c, :, :], cum[0][:, :, :], ALU.mult)
            v.drain()
            nc.vector.tensor_reduce(placef[:, :, :], prod[:, :, :, :], AX.X, ALU.add)
            v.drain()
            nc.vector.tensor_copy(keep.place[:, :, :], placef[:, :, :])


def expert_raw(sc):
    return ([sc.sb(f"e_raw{i}", [P, KD * HE]) for i in range(2)],
            [sc.sem(f"e_raw_loaded{i}") for i in range(2)])


def expert_piece(m):
    return (KD, HE, HV) if m < 2 else (NJ0, D, D)


def expert_load(sp, raw, s_raw, w13, w2, n):
    e, m = n // 3, n % 3
    src = w13[m, e, :, :, :] if m < 2 else w2[e, :, :, :]
    sp.dma_start(raw[n % 2][:, :].rearrange("p (k n) -> p k n", k=expert_piece(m)[0]), src).then_inc(s_raw[n % 2], 16)


def stage_experts(nc, keep, scratch, w13, w2, raw, s_raw):
    with ExitStack() as ctx:
        sc = Scope(nc, ctx)
        wup = [sc.sb(f"e_w{m}", [P, E, 2, KD, HV], FP16) for m in range(2)]
        wdn = sc.sb("e_w2", [P, E, 2, NJ0, D], FP16)
        xr = [sc.sb(f"e_x{i}", [P, D]) for i in range(2)]
        xT = [sc.sb(f"e_xT{i}", [P, KD, 2, P], FP16) for i in range(2)]
        h32 = [sc.sb(f"e_h{i}", [P, HE]) for i in range(2)]
        hT = [sc.sb(f"e_hT{i}", [P, 2, NJ0, P], FP16) for i in range(2)]
        y = [sc.sb(f"e_y{i}", [P, D]) for i in range(2)]
        psX, psH = sc.ps("e_psX"), sc.ps("e_psH")
        psG = [sc.ps(f"e_psG{i}") for i in range(2)]
        psU = [sc.ps(f"e_psU{i}") for i in range(2)]
        psD = [sc.ps(f"e_psD{i}") for i in range(2)]
        s_x = [sc.sem(f"e_x_loaded{i}") for i in range(2)]
        s_st = [sc.sem(f"e_y_stored{i}") for i in range(2)]
        s_pad = sc.sem("e_pad")
        (s_whi, s_wlo, s_xT, s_xhi, s_xlo, s_up, s_silu, s_h32, s_hT, s_hhi, s_hlo, s_dn, s_y) = (
            sc.sem("e_" + n) for n in ("w_hi", "w_lo", "x_transposed", "x_hi", "x_lo", "up", "silu", "h32",
                                       "h_transposed", "h_hi", "h_lo", "down", "y"))
        block = ctx.enter_context(nc.Block())

        def turns(eng, turn):
            for t in range(E):
                turn(t, t % 2, t // 2, True)
            with eng.Fori(E // 2, (TILES - 2) // 2) as i:
                for q in range(2):
                    turn(2 * i + q, q, i, False)
            for t in range((TILES - 2) // 2 * 2, TILES + 2):
                turn(t, t % 2, t // 2, False)

        def has(t, what):
            if not isinstance(t, int):
                return True
            return {"in": t + 1 < TILES, "up": t < TILES, "h": 1 <= t <= TILES, "down": t >= 2}[what]

        @block.sync
        def _(sp):
            def load(t, q):
                sp.dma_start(xr[q][:, :], scratch.xs[ds(t * P, P), :]).then_inc(s_x[q], 16)

            load(0, 0)
            load(1, 1)
            for n in range(2, 5):
                sp.wait_ge(s_wlo, n - 1)
                expert_load(sp, raw, s_raw, w13, w2, n)

            def turn(t, q, r, weights):
                if has(t, "up") and not (isinstance(t, int) and t >= TILES - 2):
                    sp.wait_ge(s_xT, t + 1)
                    load(t + 2, q)
                if weights:
                    for n in range(3 * t + 5, min(3 * t + 8, 3 * E)):
                        sp.wait_ge(s_wlo, n - 1)
                        expert_load(sp, raw, s_raw, w13, w2, n)
                if has(t, "down"):
                    sp.wait_ge(s_y, t - 1)
                    sp.dma_start(scratch.ys[ds((t - 2) * P, P), :], y[q][:, :]).then_inc(s_st[q], 16)

            turns(sp, turn)
            for q in range(2):
                sp.wait_ge(s_st[q], 16 * ((TILES + 1 - q) // 2))

        @block.gpsimd
        def _(pool):
            for q in range(2):
                last = nc.gpsimd.memset(h32[q][:, HV:HE], 0.0)
            last.then_inc(s_pad, 1)

        def split_src(q, m):
            k, w, used = expert_piece(m)
            return raw[q][:, :].rearrange("p (k n) -> p k n", k=k)[:, :, 0:used]

        def split_dst(e, m, hl):
            return wup[m][:, e, hl, :, :] if m < 2 else wdn[:, e, hl, :, :]

        @block.scalar
        def _(a):
            def split(e, q0, half):
                for m in range(3):
                    q = (q0 + m) % 2
                    a.wait_ge(s_raw[q], 16 * (half[m] + 1))
                    nc.scalar.activation(split_dst(e, m, 0), split_src(q, m), ACT.Copy, scale=SC).then_inc(s_whi, 1)

            def incoming(t, q):
                a.wait_ge(s_xT, t + 1)
                if not (isinstance(t, int) and t < 2):
                    a.wait_ge(s_up, t - 1)
                nc.scalar.activation(xT[q][:, :, 0, :], psX[:, :].rearrange("p (k t) -> p k t", k=KD),
                                     ACT.Copy).then_inc(s_xhi, 1)

            split(0, 0, (0, 0, 1))
            incoming(0, 0)
            a.wait_ge(s_pad, 1)

            def turn(t, q, r, weights):
                if has(t, "in"):
                    incoming(t + 1, 1 - q)
                if weights and not (isinstance(t, int) and t == E - 1):
                    split(t + 1, 1 - q, [3 * r + (3 * q + 3 + m) // 2 for m in range(3)])
                if has(t, "up"):
                    a.wait_ge(s_up, t + 1)
                    if not (isinstance(t, int) and t < 2):
                        a.wait_ge(s_hT, t - 1)
                    nc.scalar.activation(h32[q][:, 0:HV], psG[q][:, 0:HV], ACT.Silu, scale=1.0 / SC).then_inc(s_silu, 1)
                if has(t, "h"):
                    a.wait_ge(s_hT, t)
                    if not (isinstance(t, int) and t < 3):
                        a.wait_ge(s_dn, t - 2)
                    nc.scalar.activation(hT[1 - q][:, 0, :, :], psH[:, 0:HE].rearrange("p (j t) -> p j t", j=NJ0),
                                         ACT.Copy).then_inc(s_hhi, 1)
                if has(t, "down"):
                    a.wait_ge(s_dn, t - 1)
                    if not (isinstance(t, int) and t < 4):
                        a.wait_ge(s_st[q], 16 * (r - 1))
                    nc.scalar.activation(y[q][:, :], psD[q][:, :], ACT.Copy).then_inc(s_y, 1)

            turns(a, turn)

        @block.vector
        def _(v):
            def split(e, q0):
                for m in range(3):
                    v.wait_ge(s_whi, 3 * e + m + 1)
                    nc.vector.scalar_tensor_tensor(split_dst(e, m, 1), split_src((q0 + m) % 2, m), SC,
                                                   split_dst(e, m, 0), ALU.mult, ALU.subtract).then_inc(s_wlo, 1)

            def incoming(t, q):
                v.wait_ge(s_xhi, t + 1)
                nc.vector.tensor_tensor(xT[q][:, :, 1, :], psX[:, :].rearrange("p (k t) -> p k t", k=KD),
                                        xT[q][:, :, 0, :], ALU.subtract).then_inc(s_xlo, 1)

            split(0, 0)
            incoming(0, 0)

            def turn(t, q, r, weights):
                if has(t, "in"):
                    incoming(t + 1, 1 - q)
                if weights and not (isinstance(t, int) and t == E - 1):
                    split(t + 1, 1 - q)
                if has(t, "up"):
                    v.wait_ge(s_silu, t + 1)
                    nc.vector.scalar_tensor_tensor(h32[q][:, 0:HV], psU[q][:, 0:HV], 1.0 / SC, h32[q][:, 0:HV],
                                                   ALU.mult, ALU.mult).then_inc(s_h32, 1)
                if has(t, "h"):
                    v.wait_ge(s_hhi, t)
                    nc.vector.tensor_tensor(hT[1 - q][:, 1, :, :], psH[:, 0:HE].rearrange("p (j t) -> p j t", j=NJ0),
                                            hT[1 - q][:, 0, :, :], ALU.subtract).then_inc(s_hlo, 1)

            turns(v, turn)

        @block.tensor
        def _(pe):
            def incoming(t, q, rounds):
                pe.wait_ge(s_x[q], 16 * (rounds + 1))
                if not (isinstance(t, int) and t == 0):
                    pe.wait_ge(s_xlo, t)
                for k in range(KD):
                    last = nc.tensor.transpose(psX[:, k * P:(k + 1) * P], xr[q][:, k * P:(k + 1) * P], keep.ident[:, :])
                last.then_inc(s_xT, 1)

            incoming(0, 0, 0)

            def expert(t):
                return pe.value_load(keep.tile_expert[0:1, ds(t, 1)], min_val=0, max_val=E - 1)

            def turn(t, q, r, weights):
                if has(t, "in"):
                    incoming(t + 1, 1 - q, r + q)
                if has(t, "up"):
                    e = expert(t)
                    if weights:
                        pe.wait_ge(s_wlo, 3 * t + 3)
                    pe.wait_ge(s_xlo, t + 1)
                    if not (isinstance(t, int) and t < 2):
                        pe.wait_ge(s_h32, t - 1)
                    for m, bank in enumerate((psG, psU)):
                        last = split_matmuls(nc, bank[q][:, 0:HV],
                                             [(lambda hl, k=k: xT[q][:, k, hl, :],
                                               lambda hl, k=k: wup[m][:, e, hl, k, :]) for k in range(KD)])
                    last.then_inc(s_up, 1)
                if has(t, "h"):
                    pe.wait_ge(s_h32, t)
                    if not (isinstance(t, int) and t < 2):
                        pe.wait_ge(s_hlo, t - 1)
                    for j in range(NJ0):
                        last = nc.tensor.transpose(psH[:, j * P:(j + 1) * P], h32[1 - q][:, j * P:(j + 1) * P],
                                                   keep.ident[:, :])
                    last.then_inc(s_hT, 1)
                if has(t, "down"):
                    e = expert(t - 2)
                    pe.wait_ge(s_hlo, t - 1)
                    if not (isinstance(t, int) and t < 4):
                        pe.wait_ge(s_y, t - 3)
                    split_matmuls(nc, psD[q][:, :],
                                  [(lambda hl, j=j: hT[q][:, hl, j, :],
                                    lambda hl, j=j: wdn[:, e, hl, j, :]) for j in range(NJ0)]).then_inc(s_dn, 1)

            turns(pe, turn)


def ffn_raw(sc, tag, NJ):
    return ([sc.sb(f"{tag}_raw{i}", [P, NJ * 512]) for i in range(3)],
            [sc.sem(f"{tag}_raw_loaded{i}") for i in range(3)])


def ffn_load(sp, raw, s_raw, w13, w2, g, m, NJ):
    src, k = (w13[m, g, :, :, :], KD) if m < 2 else (w2[g, :, :, :], NJ)
    sp.dma_start(raw[m][:, :].rearrange("p (k n) -> p k n", k=k), src).then_inc(s_raw[m], 16)


def ffn_load_group(sp, raw, s_raw, w13, w2, g, NJ):
    for m in range(3):
        ffn_load(sp, raw, s_raw, w13, w2, g, m, NJ)


def stage_ffn(nc, keep, tag, w13, w2, NG, NJ, pool_program=None, norm=False, first=None,
              ahead_load=None, out=None):
    HW = NJ * P
    with ExitStack() as ctx:
        sc = Scope(nc, ctx)
        raw, s_raw = first or ffn_raw(sc, tag, NJ)
        wup = [[sc.sb(f"{tag}_w{m}_{par}", [P, 2, KD, HW], FP16) for m in range(2)] for par in range(2)]
        wdn = [sc.sb(f"{tag}_w2_{par}", [P, 2, NJ, D], FP16) for par in range(2)]
        hT = [sc.sb(f"{tag}_hT{par}", [P, NJ, 2, S], FP16) for par in range(2)]
        sg = [sc.sb(f"{tag}_silu{i}", [P, S]) for i in range(2)]
        h32 = sg
        with ExitStack() as ps_ctx:
            ps_scope = Scope(nc, ps_ctx)
            psG = [ps_scope.ps(f"{tag}_psG{i}") for i in range(2)]
            psU = [ps_scope.ps(f"{tag}_psU{i}") for i in range(2)]
            psD = [ps_scope.ps(f"{tag}_psD{i}") for i in range(4)]
            s_out = sc.sem(f"{tag}_stored")
            s_whi, s_wlo = sc.sem(f"{tag}_w_hi"), sc.sem(f"{tag}_w_lo")
            s_up, s_silu, s_h32, s_h = (sc.sem(f"{tag}_{n}") for n in ("up", "silu", "h32", "h"))
            s_down, s_acc = sc.sem(f"{tag}_down"), sc.sem(f"{tag}_acc")
            ln = LayerNorm(sc, keep, "ln3", [sc.sb(f"ln3_xn{n}", [P, D]) for n in range(NT)], psD) if norm else None
            block = ps_ctx.enter_context(nc.Block())

            if pool_program is not None:
                block.gpsimd(pool_program)

            def flat(t):
                return t.rearrange("p h k n -> p h (k n)")

            def split_dst(par, m):
                return flat((wup[par][m] if m < 2 else wdn[par])[:, :, :, :])

            @block.sync
            def _(sp):
                if first is None:
                    ffn_load_group(sp, raw, s_raw, w13, w2, 0, NJ)
                with sp.Fori(1, NG) as g:
                    for m in range(3):
                        sp.wait_ge(s_wlo, 3 * g - 3 + m + 1)
                        ffn_load(sp, raw, s_raw, w13, w2, g, m, NJ)
                if ahead_load is not None:
                    ahead_load(sp)
                if out is not None:
                    for b in range(B):
                        for t in range(NT):
                            sp.wait_ge(s_acc, 4 * (B * (NG - 1) + b) + t + 1)
                            sp.dma_start(out[b, t * P:(t + 1) * P, :], keep.x[:, 4 * b + t, :]).then_inc(s_out, 16)
                    sp.wait_ge(s_out, 16 * B * NT)

            def split_hi(a, g, par, m):
                a.wait_ge(s_raw[m], 16 * g + 16)
                nc.scalar.activation(split_dst(par, m)[:, 0, :], raw[m][:, :], ACT.Copy, scale=SC).then_inc(s_whi, 1)

            def split_lo(v, g, par, m):
                v.wait_ge(s_whi, 3 * g + m + 1)
                nc.vector.scalar_tensor_tensor(split_dst(par, m)[:, 1, :], raw[m][:, :], SC, split_dst(par, m)[:, 0, :],
                                               ALU.mult, ALU.subtract).then_inc(s_wlo, 1)

            @block.scalar
            def _(a):
                if norm:
                    ln.root(nc, a, 0, 0)
                for m in range(3):
                    split_hi(a, 0, 0, m)
                if norm:
                    ln.highs(nc, a, 0)
                    ln.root(nc, a, 1, 1)

                def pair(i, last):
                    for par in range(2):
                        g = 2 * i + par
                        for b in range(B):
                            u = 4 * g + b
                            ahead = norm and isinstance(g, int) and g == 0 and b + 2 < B
                            if ahead and b > 0:
                                ln.root(nc, a, b + 2, b + 2)
                            for j in range(NJ):
                                n = u * NJ + j
                                a.wait_ge(s_up, n + 1)
                                if not (isinstance(n, int) and n < 2):
                                    a.wait_ge(s_h, n - 1)
                                q = (b * NJ + j) % 2
                                nc.scalar.activation(sg[q][:, :], psG[q][:, :], ACT.Silu, scale=1.0 / SC).then_inc(s_silu, 1)
                                if ahead and b == 0 and j == 1:
                                    ln.highs(nc, a, 1)
                                    ln.root(nc, a, 2, 2)
                            if b >= 1 and not (last and par == 1):
                                if b == 1 and not (isinstance(g, int) and g == 0):
                                    a.wait_ge(s_down, 16 * g)
                                split_hi(a, g + 1, 1 - par, b - 1)
                            if ahead:
                                ln.highs(nc, a, b + 2)

                pair(0, NG == 2)
                if NG > 4:
                    with a.Fori(1, NG // 2 - 1) as i:
                        pair(i, False)
                if NG > 2:
                    pair(NG // 2 - 1, True)

            @block.vector
            def _(v):
                if norm:
                    ln.stats(nc, v, 0)
                    ln.rows(nc, v, 0)
                for m in range(3):
                    split_lo(v, 0, 0, m)
                if norm:
                    ln.lows(nc, v, 0)
                    ln.stats(nc, v, 1)
                    ln.rows(nc, v, 1)

                def take(u, b):
                    for t in range(NT):
                        v.wait_ge(s_down, 4 * u + t + 1)
                        xs = keep.x[:, 4 * b + t, :]
                        nc.vector.scalar_tensor_tensor(xs, psD[t][:, :], 1.0 / SC, xs, ALU.mult, ALU.add).then_inc(s_acc, 1)

                def pair(i, last):
                    for par in range(2):
                        g = 2 * i + par
                        for b in range(B):
                            u = 4 * g + b
                            ahead = norm and isinstance(g, int) and g == 0 and b + 2 < B
                            if ahead and b > 0:
                                ln.stats(nc, v, b + 2)
                                ln.rows(nc, v, b + 2)
                            for j in range(NJ):
                                n = u * NJ + j
                                q = (b * NJ + j) % 2
                                v.wait_ge(s_silu, n + 1)
                                nc.vector.scalar_tensor_tensor(h32[q][:, :], psU[q][:, :], 1.0 / SC, sg[q][:, :],
                                                               ALU.mult, ALU.mult).then_inc(s_h32, 1)
                                if j == 0 and not (isinstance(u, int) and u < 2):
                                    v.drain()
                                    v.wait_ge(s_down, 4 * (u - 1))
                                else:
                                    v.drain()
                                hh = hT[b % 2]
                                nc.vector.tensor_copy(hh[:, j, 0, :], h32[q][:, :])
                                v.drain()
                                nc.vector.tensor_tensor(hh[:, j, 1, :], h32[q][:, :], hh[:, j, 0, :],
                                                        ALU.subtract).then_inc(s_h, 1)
                                if ahead and b == 0 and j == 1:
                                    ln.lows(nc, v, 1)
                                    ln.stats(nc, v, 2)
                                    ln.rows(nc, v, 2)
                            if b >= 1 and not (last and par == 1):
                                split_lo(v, g + 1, 1 - par, b - 1)
                            if not (isinstance(u, int) and u == 0):
                                take(u - 1, (b - 1) % B)
                            if ahead:
                                ln.lows(nc, v, b + 2)

                pair(0, NG == 2)
                if NG > 4:
                    with v.Fori(1, NG // 2 - 1) as i:
                        pair(i, False)
                if NG > 2:
                    pair(NG // 2 - 1, True)
                take(4 * NG - 1, B - 1)

            @block.tensor
            def _(pe):
                def up(u, g, par, b):
                    if b == 0:
                        pe.wait_ge(s_wlo, 3 * g + 2)
                    if norm and isinstance(g, int) and g == 0:
                        pe.wait_ge(ln.s_lo, 4 * b + 4)
                    for j in range(NJ):
                        n = u * NJ + j
                        q = (b * NJ + j) % 2
                        if norm and isinstance(n, int) and n == 2:
                            ln.transposes(nc, pe, 1)
                        if not (isinstance(n, int) and n < 2):
                            pe.wait_ge(s_h32, n - 1)
                        for m, bank in enumerate((psG, psU)):
                            w = wup[par][m]
                            last = split_matmuls(nc, bank[q][:, :],
                                                 [(lambda hl, k=k: w[:, hl, k, j * P:(j + 1) * P],
                                                   lambda hl, k=k: keep.xT[:, b, k, hl, :]) for k in range(KD)])
                        last.then_inc(s_up, 1)

                def down(u, g, par, b):
                    if b == 0:
                        pe.wait_ge(s_wlo, 3 * g + 3)
                    pe.wait_ge(s_h, NJ * (u + 1))
                    for t in range(NT):
                        if not (isinstance(u, int) and u == 0):
                            pe.wait_ge(s_acc, 4 * (u - 1) + t + 1)
                        if norm and isinstance(u, int) and u < B:
                            pe.wait_ge(ln.s_lo, min(4 * (u + 2), 4 * (B - 1)) + t + 1)
                        split_matmuls(nc, psD[t][:, :],
                                      [(lambda hl, j=j: hT[b % 2][:, j, hl, t * P:(t + 1) * P],
                                        lambda hl, j=j: wdn[par][:, hl, j, :]) for j in range(NJ)]).then_inc(s_down, 1)

                def pair(i, last):
                    for par in range(2):
                        g = 2 * i + par
                        for b in range(B):
                            u = 4 * g + b
                            if norm and isinstance(g, int) and g == 0 and b + 2 < B:
                                if u > 0:
                                    pe.wait_ge(s_acc, 4 * u)
                                ln.transposes(nc, pe, b + 2)
                            if b < B - 1:
                                up(u + 1, g, par, b + 1)
                            elif not (last and par == 1):
                                up(u + 1, g + 1, 1 - par, 0)
                            down(u, g, par, b)

                if norm:
                    ln.transposes(nc, pe, 0)
                up(0, 0, 0, 0)
                pair(0, NG == 2)
                if NG > 4:
                    with pe.Fori(1, NG // 2 - 1) as i:
                        pair(i, False)
                if NG > 2:
                    pair(NG // 2 - 1, True)


def kvs_back(sp, keep, scratch, b, sem):
    for n in (b, B + b):
        sp.dma_start(keep.kvs[:, n, :, :].rearrange("p l s -> p (l s)"), scratch.kvs[n, :, :]).then_inc(sem, 16)


def wqc_back(sp, keep, scratch, start, end, sem):
    sp.dma_start(keep.wqc[:, start:end, :, :, :].rearrange("p h k l r -> p h (k l r)"),
                 scratch.wqc[start:end, :, :].rearrange("h p r -> p h r")).then_inc(sem, 16)


def stage_combine(nc, keep, scratch):
    with ExitStack() as ctx:
        sc = Scope(nc, ctx)
        xn = [sc.sb(f"ln2_xn{n}", [P, D]) for n in range(NT)]
        y = [[sc.sb(f"y{n}_{c}", [P, D]) for c in range(2)] for n in range(NT)]
        ps_T = [sc.ps(f"ln2_psT{i}") for i in range(NT)]
        s_y = [sc.sem(f"y_loaded{n}") for n in range(NT)]
        s_w = sc.sem("attention_weights_back")
        ln = LayerNorm(sc, keep, "ln2", xn, ps_T)
        block = ctx.enter_context(nc.Block())

        @block.sync
        def _(sp):
            kvs_back(sp, keep, scratch, 0, s_w)
            sp.dma_start(keep.wkr[:, :, :, :].rearrange("p h l r -> p h (l r)"),
                         scratch.wkr[:, :, :].rearrange("h p r -> p h r")).then_inc(s_w, 16)
            wqc_back(sp, keep, scratch, 0, 2, s_w)
            sp.wait_ge(s_w, 64)

        @block.gpsimd
        def _(pool):
            for n in range(NT):
                for c in range(2):
                    nc.gpsimd.indirect_dma_start(y[n][c][:, :], None, scratch.ys[:, :],
                                                 bass.IndirectOffsetOnAxis(keep.place[:, c, n:n + 1], 0)
                                                 ).then_inc(s_y[n], 16)

        @block.scalar
        def _(a):
            ln.root(nc, a, 0, 0)
            ln.highs(nc, a, 0)

        @block.vector
        def _(v):
            for n in range(NT):
                v.wait_ge(s_y[n], 32)
                xs = keep.x[:, n, :]
                for c in range(2):
                    nc.vector.scalar_tensor_tensor(xs, y[n][c][:, :], keep.gates[:, c, n:n + 1], xs, ALU.mult, ALU.add)
                    v.drain()
            ln.stats(nc, v, 0)
            ln.rows(nc, v, 0)
            ln.lows(nc, v, 0)

        @block.tensor
        def _(pe):
            ln.transposes(nc, pe, 0)


def stage_attention(nc, keep, scratch):
    with ExitStack() as ctx:
        sc = Scope(nc, ctx)
        Q = [sc.sb(f"Q{i}", [P, S], FP16) for i in range(4)]
        KH = [sc.sb(f"KH{i}", [P, S], FP16) for i in range(2)]
        KL = [sc.sb(f"KL{i}", [P, S], FP16) for i in range(2)]
        p32 = [sc.sb(f"p32_{i}", [P, S]) for i in range(NT)]
        pn = [sc.sb(f"pn{i}", [P, 2, S], FP16) for i in range(NT)]
        pT = [sc.sb(f"pT{i}", [P, 2, NT, S], FP16) for i in range(2)]
        cx = sc.sb("cx", [P, 2, 2 * HG, S], FP16)
        nmx = sc.sb("nmx", [P, NT])
        rsum, rinv = sc.sb("rsum", [P, NT]), sc.sb("rinv", [P, NT])
        psQK, psO = sc.ps("psQK"), sc.ps("psO")
        psC = [sc.ps(f"psC{i}") for i in range(2)]
        psS = [sc.ps(f"psS{i}") for i in range(2)]
        psP = [sc.ps(f"psP{i}", (P, 2, NT, P), FP16) for i in range(2)]
        (s_qps, s_kps, s_qhi, s_qlo, s_khi, s_klo, s_S, s_max, s_exp, s_r, s_phi, s_pn, s_T, s_ev, s_ctx, s_chi,
         s_clo, s_out, s_acc) = (sc.sem("at_" + n) for n in (
             "q_in_psum", "k_in_psum", "q_hi", "q_lo", "k_hi", "k_lo", "scores", "max", "exp", "inverse_sum",
             "probs_hi", "probs", "probs_transposed", "probsT", "ctx", "ctx_hi", "ctx_lo", "out", "acc"))
        y = [[sc.sb(f"at_y{n}_{c}", [P, D]) for c in range(2)] for n in range(2)]
        xn = sc.sb("at_xn", [P, D])
        xst, xmv, xstd, xrstd = (sc.sb("at_x" + n, shape) for n, shape in (
            ("stats", [P, NT, 6]), ("meanvar", [P, NT, 2]), ("std", [P, NT]), ("rstd", [P, NT])))
        s_y = [sc.sem(f"at_y_loaded{n}") for n in range(2)]
        s_wqc, s_wvo, s_kvs = sc.sem("wqc_back"), sc.sem("wvo_back"), sc.sem("kvs_back")
        s_add, s_var, s_std, s_xn, s_xt, s_xhi, s_xlo = (sc.sem("at_" + n) for n in (
            "y_added", "x_var", "x_std", "xn", "xn_transposed", "xT_hi", "xT_lo"))
        block = ctx.enter_context(nc.Block())

        def steps(eng, step):
            for k in range(H - 2):
                step(0, k, True)
            with eng.Fori(1, B - 1) as b:
                for k in range(-2, H - 2):
                    step(b, k, True)
            for k in range(-2, H - 2):
                step(B - 1, k, False)
            for k in range(-2, 7):
                step(B, k, False)

        def has(b, k, tiles):
            return not isinstance(b, int) or 0 <= 4 * (H * b + k) + tiles < 4 * H * B

        def head(b, k):
            return b + k // H, k % H

        def upto(eng, sem, n):
            if not (isinstance(n, int) and n <= 0):
                eng.wait_ge(sem, n)

        @block.sync
        def _(sp):
            wqc_back(sp, keep, scratch, 2, H // 2, s_wqc)
            sp.dma_start(keep.wvo[:, :, :, :].rearrange("p h l n -> p h (l n)"),
                         scratch.wvo[:, :, :].rearrange("h p n -> p h n")).then_inc(s_wvo, 16)
            for b in range(1, B):
                kvs_back(sp, keep, scratch, b, s_kvs)

        @block.gpsimd
        def _(pool):
            for n in range((B - 1) * NT):
                if n >= 2:
                    pool.wait_ge(s_add, n - 1)
                for c in range(2):
                    nc.gpsimd.indirect_dma_start(y[n % 2][c][:, :], None, scratch.ys[:, :],
                                                 bass.IndirectOffsetOnAxis(keep.place[:, c, NT + n:NT + n + 1], 0)
                                                 ).then_inc(s_y[n % 2], 16)

        @block.tensor
        def _(pe):
            def queries(b, k):
                bb, h = head(b, k)
                split_matmuls(nc, psQK[:, :], [(lambda hl, c=c: keep.wqc[:, h // 2, c, hl, :],
                                                lambda hl, c=c: keep.xT[:, bb, c, hl, :])
                                               for c in range(KD)]).then_inc(s_qps, 1)

            def keys(b, k):
                bb, h = head(b, k)
                split_matmuls(nc, psQK[:, :], [(lambda hl: keep.wkr[:, h, hl, :],
                                                lambda hl: keep.kvs[:, bb, hl, :])]).then_inc(s_kps, 1)

            def step(b, k, more):
                G = H * b + k
                if isinstance(G, int) and G == H - 3:
                    pe.wait_ge(s_kvs, 32 * (B - 1))
                for st in range(NT):
                    jj = 4 * G + st
                    if has(b, k, st):
                        if st == 0:
                            pe.wait_ge(s_klo, G + 1)
                            pe.wait_ge(s_qlo, H // 2 * b + k // 2 + 1)
                        upto(pe, s_exp, jj - 1)
                        q = Q[k % 4][:, st * P:(st + 1) * P]
                        nc.tensor.matmul(psS[st % 2][:, :], q, KH[k % 2][:, :], start=True, stop=False)
                        nc.tensor.matmul(psS[st % 2][:, :], q, KL[k % 2][:, :], start=False, stop=True).then_inc(s_S, 1)
                    if has(b, k, st - 3):
                        jt, t = jj - 3, (st + 1) % 4
                        pe.wait_ge(s_pn, jt + 1)
                        upto(pe, s_ev, jt - 1)
                        for hl in range(2):
                            for l in range(NT):
                                last = nc.tensor.transpose(psP[t % 2][:, hl, l, :], pn[t][:, hl, l * P:(l + 1) * P],
                                                           keep.ident16[:, :])
                        last.then_inc(s_T, 1)
                    if st == 1 and has(b, k + 1, 0):
                        if k % 2:
                            pe.wait_ge(s_qlo, H // 2 * b + (k + 1) // 2 + 1)
                        else:
                            pe.wait_ge(s_klo, G + 1)
                            if more and k in (6, 8, 10, 12):
                                pe.wait_ge(s_xlo, 4 * b + (k - 4) // 2)
                        keys(b, k + 1)
                    if st < 2 and has(b, k - 2, 0):
                        bb, h = head(b, k - 2)
                        if st == 0:
                            pe.wait_ge(s_ev, 4 * G - 4)
                            upto(pe, s_clo, G - 3)
                        for l in (2 * st, 2 * st + 1):
                            kt = lambda hl: keep.kvs[:, B + bb, hl, l * P:(l + 1) * P]
                            pt = lambda hl: pT[k % 2][:, hl, l, :]
                            nc.tensor.matmul(psC[k % 2][:, :], kt(0), pt(0), start=l == 0, stop=False)
                            nc.tensor.matmul(psC[k % 2][:, :], kt(0), pt(1), start=False, stop=False)
                            last = nc.tensor.matmul(psC[k % 2][:, :], kt(1), pt(0), start=False, stop=l == 3)
                        if st == 1:
                            last.then_inc(s_ctx, 1)
                    if st >= 2 and has(b, k - 6, 0):
                        bb, r = head(b, k - 6)
                        g0, t = r // HG * HG, r % HG
                        if st == 2:
                            if isinstance(G, int) and G == 6:
                                pe.wait_ge(s_wvo, 16)
                            pe.wait_ge(s_clo, H * b + (k - 6) // HG * HG + HG)
                            upto(pe, s_acc, G - 6)
                        for h in (g0 + 2 * (st - 2), g0 + 2 * (st - 2) + 1):
                            cs = lambda hl: cx[:, hl, h % (2 * HG), t * P:(t + 1) * P]
                            ws = lambda hl: keep.wvo[:, h, hl, :]
                            nc.tensor.matmul(psO[:, :], cs(0), ws(0), start=h == g0, stop=False)
                            nc.tensor.matmul(psO[:, :], cs(0), ws(1), start=False, stop=False)
                            last = nc.tensor.matmul(psO[:, :], cs(1), ws(0), start=False, stop=h == g0 + HG - 1)
                        if st == 3:
                            last.then_inc(s_out, 1)
                    if st == 3 and k % 2 == 0 and has(b, k + 2, 0):
                        if isinstance(G, int) and G == 2:
                            pe.wait_ge(s_wqc, 16)
                        pe.wait_ge(s_klo, G + 2)
                        queries(b, k + 2)
                    if st == 3 and more and k in (5, 7, 9, 11):
                        pe.wait_ge(s_klo, G + 2)
                        pe.wait_ge(s_xn, 4 * b + (k - 5) // 2 + 1)
                        for c in range(KD):
                            last = nc.tensor.transpose(psQK[:, c * P:(c + 1) * P], xn[:, c * P:(c + 1) * P],
                                                       keep.ident[:, :])
                        last.then_inc(s_xt, 1)

            queries(0, 0)
            pe.wait_ge(s_qlo, 1)
            keys(0, 0)
            steps(pe, step)

        @block.scalar
        def _(a):
            def queries(b, k):
                G = H * b + k
                a.wait_ge(s_qps, H // 2 * b + k // 2 + 1)
                upto(a, s_S, 4 * G - 8)
                nc.scalar.activation(Q[k % 4][0:R, :], psQK[0:R, :], ACT.Copy, scale=1.0 / SC)
                nc.scalar.activation(Q[k % 4 + 1][R:P, :], psQK[R:P, :], ACT.Copy, scale=1.0 / SC).then_inc(s_qhi, 1)

            def keys(b, k):
                G = H * b + k
                a.wait_ge(s_kps, G + 1)
                upto(a, s_S, 4 * G - 4)
                nc.scalar.activation(KH[k % 2][:, :], psQK[:, :], ACT.Copy, scale=1.0 / SC).then_inc(s_khi, 1)

            def step(b, k, more):
                G = H * b + k
                for st in range(NT):
                    jj = 4 * G + st
                    if st == 0 and k % 2 and has(b, k + 1, 0):
                        queries(b, k + 1)
                    if st == 0 and more and k in (6, 8, 10, 12):
                        n = (k - 6) // 2
                        a.wait_ge(s_xt, 4 * b + n + 1)
                        nc.scalar.activation(keep.xT[:, b + 1, :, 0, n * P:(n + 1) * P],
                                             psQK[:, :].rearrange("p (k t) -> p k t", k=KD), ACT.Copy).then_inc(s_xhi, 1)
                    if st == 2 and more and k == 4:
                        a.wait_ge(s_var, b + 1)
                        nc.scalar.activation(xstd[:, :], xmv[:, :, 1], ACT.Sqrt, bias=keep.eps[:, 0:1]).then_inc(s_std, 1)
                    if st == 2 and has(b, k + 1, 0):
                        keys(b, k + 1)
                    if has(b, k, st):
                        a.wait_ge(s_max, jj + 1)
                        upto(a, s_pn, jj - 3)
                        nc.scalar.activation(p32[st][:, :], psS[st % 2][:, :], ACT.Exp, bias=nmx[:, st:st + 1],
                                             accum_out=rsum[:, st:st + 1]).then_inc(s_exp, 1)
                    if has(b, k, st - 1):
                        t = (st - 1) % 4
                        a.wait_ge(s_r, jj)
                        upto(a, s_T, jj - 4)
                        nc.scalar.activation(pn[t][:, 0, :], p32[t][:, :], ACT.Copy, scale=rinv[:, t:t + 1]).then_inc(s_phi, 1)
                    if has(b, k, st - 3):
                        jt, t = jj - 3, (st + 1) % 4
                        hp = (k if st == 3 else k + 1) % 2
                        a.wait_ge(s_T, jt + 1)
                        if t == 0:
                            upto(a, s_ctx, G - 1)
                        nc.scalar.activation(pT[hp][:, :, :, t * P:(t + 1) * P], psP[t % 2][:, :, :, :],
                                             ACT.Copy).then_inc(s_ev, 1)
                    if st == 2 and has(b, k - 2, 0):
                        h = head(b, k - 2)[1]
                        a.wait_ge(s_ctx, G - 1)
                        upto(a, s_out, H * b + (k - 2 - 2 * HG) // HG * HG + HG)
                        nc.scalar.activation(cx[:, 0, h % (2 * HG), :], psC[k % 2][:, :], ACT.Copy,
                                             scale=1.0 / PSC).then_inc(s_chi, 1)

            queries(0, 0)
            keys(0, 0)
            steps(a, step)

        @block.vector
        def _(v):
            def queries(b, k):
                v.wait_ge(s_qhi, H // 2 * b + k // 2 + 1)
                q0, q1 = Q[k % 4], Q[k % 4 + 1]
                nc.vector.scalar_tensor_tensor(q0[R:P, :], psQK[0:R, :], 1.0 / SC, q0[0:R, :],
                                               ALU.mult, ALU.subtract)
                nc.vector.scalar_tensor_tensor(q1[0:R, :], psQK[R:P, :], 1.0 / SC, q1[R:P, :],
                                               ALU.mult, ALU.subtract).then_inc(s_qlo, 1)

            def keys(b, k):
                v.wait_ge(s_khi, H * b + k + 1)
                nc.vector.scalar_tensor_tensor(KL[k % 2][:, :], psQK[:, :], 1.0 / SC, KH[k % 2][:, :],
                                               ALU.mult, ALU.subtract).then_inc(s_klo, 1)

            def step(b, k, more):
                G = H * b + k
                for st in range(NT):
                    jj = 4 * G + st
                    if has(b, k, st):
                        v.wait_ge(s_S, jj + 1)
                        nc.vector.tensor_reduce(nmx[:, st:st + 1], psS[st % 2][:, :], AX.X, ALU.max,
                                                negate=True).then_inc(s_max, 1)
                    if has(b, k, st - 1):
                        r = rinv[:, (st - 1) % 4:(st - 1) % 4 + 1]
                        v.wait_ge(s_exp, jj)
                        nc.vector.tensor_scalar(r, rsum[:, (st - 1) % 4:(st - 1) % 4 + 1], 1.0 / PSC, None, ALU.mult)
                        v.drain()
                        nc.vector.reciprocal(r, r).then_inc(s_r, 1)
                    if has(b, k, st - 2):
                        t = (st - 2) % 4
                        v.wait_ge(s_phi, jj - 1)
                        nc.vector.scalar_tensor_tensor(pn[t][:, 1, :], p32[t][:, :], rinv[:, t:t + 1], pn[t][:, 0, :],
                                                       ALU.mult, ALU.subtract).then_inc(s_pn, 1)
                    if st == 0 and k % 2 and has(b, k + 1, 0):
                        queries(b, k + 1)
                    if st == 2 and has(b, k + 1, 0):
                        keys(b, k + 1)
                    if st == 0 and has(b, k - 3, 0):
                        h = head(b, k - 3)[1]
                        v.wait_ge(s_chi, G - 2)
                        nc.vector.scalar_tensor_tensor(cx[:, 1, h % (2 * HG), :], psC[(k + 1) % 2][:, :], 1.0 / PSC,
                                                       cx[:, 0, h % (2 * HG), :], ALU.mult, ALU.subtract).then_inc(s_clo, 1)
                    if more and k in range(NT) and st in (1, 2):
                        c, xs = st - 1, keep.x[:, 4 * b + 4 + k, :]
                        if c == 0:
                            v.wait_ge(s_y[k % 2], 32 * (2 * b + k // 2 + 1))
                        last = nc.vector.scalar_tensor_tensor(xs, y[k % 2][c][:, :], keep.gates[:, c, ds(4 * b + 4 + k, 1)],
                                                              xs, ALU.mult, ALU.add)
                        if c == 1:
                            last.then_inc(s_add, 1)
                    if more and k in range(NT) and st == 3:
                        nc.vector.bn_stats(xst[:, k, :], keep.x[:, 4 * b + 4 + k, :])
                    if more and k == 4 and st == 1:
                        for n in range(NT):
                            last = nc.vector.bn_aggr(xmv[:, n, :], xst[:, n, :])
                        last.then_inc(s_var, 1)
                    if more and k == 4 and st == 3:
                        v.wait_ge(s_std, b + 1)
                        nc.vector.reciprocal(xrstd[:, :], xstd[:, :])
                    if more and k in (5, 7, 9, 11) and st == 1:
                        n = (k - 5) // 2
                        nc.vector.tensor_scalar(xn[:, :], keep.x[:, 4 * b + 4 + n, :], xmv[:, n, 0:1], xrstd[:, n:n + 1],
                                                ALU.subtract, ALU.mult).then_inc(s_xn, 1)
                    if more and k in (6, 8, 10, 12) and st == 0:
                        n = (k - 6) // 2
                        v.wait_ge(s_xhi, 4 * b + n + 1)
                        nc.vector.tensor_tensor(keep.xT[:, b + 1, :, 1, n * P:(n + 1) * P],
                                                psQK[:, :].rearrange("p (k t) -> p k t", k=KD),
                                                keep.xT[:, b + 1, :, 0, n * P:(n + 1) * P], ALU.subtract).then_inc(s_xlo, 1)
                    if st == 1 and has(b, k - 7, 0):
                        bb, t = head(b, k - 7)
                        v.wait_ge(s_out, G - 6)
                        xs = keep.x[:, 4 * bb + t % HG, :]
                        nc.vector.scalar_tensor_tensor(xs, psO[:, :], 1.0 / SC, xs, ALU.mult, ALU.add).then_inc(s_acc, 1)

            queries(0, 0)
            keys(0, 0)
            steps(v, step)


def build(nc, d, out):
    scratch = Scratch(nc)
    with ExitStack() as ctx:
        sc = Scope(nc, ctx)
        keep = Keep(sc)
        with ExitStack() as c0:
            e_raw, s_eraw = expert_raw(Scope(nc, c0))
            with ExitStack() as c1:
                s1 = Scope(nc, c1)
                keep.normed(s1, "ffn0")
                gate_w = s1.sb("gate_w_split", [P, KD, 2, E], FP16)
                mv1, rstd1 = s1.sb("mv1", [P, B * NT, 2]), s1.sb("rstd1", [P, B * NT])
                s8 = s1.sb("router_scores8", [P, B * NT, E])
                stage_adjacency(nc, keep, d, scratch, gate_w, mv1, rstd1, s8)
                xn = s1.sb("xn_rows", [P, B * NT, D])
                s_rows = s1.sem("rows_scattered")
                f_raw, s_fraw = ffn_raw(s1, "f0", NJ0)
                stage_router(nc, keep, s8, mv1, rstd1, xn, lambda sp: ffn_load_group(
                    sp, f_raw, s_fraw, d["w13_s"], d["w2_s"], 0, NJ0))

                def scatter(pool):
                    for t in range(B * NT):
                        for c in range(2):
                            nc.gpsimd.indirect_dma_start(scratch.xs[:, :],
                                                         bass.IndirectOffsetOnAxis(keep.place[:, c, t:t + 1], 0),
                                                         xn[:, t, :], None).then_inc(s_rows, 16)
                    pool.wait_ge(s_rows, 32 * B * NT)

                def first_expert(sp):
                    for n in range(2):
                        expert_load(sp, e_raw, s_eraw, d["w13_e"], d["w2_e"], n)

                stage_ffn(nc, keep, "f0", d["w13_s"], d["w2_s"], NS, NJ0, pool_program=scatter,
                          first=(f_raw, s_fraw), ahead_load=first_expert)
            stage_experts(nc, keep, scratch, d["w13_e"], d["w2_e"], e_raw, s_eraw)
        keep.normed(sc, "later")
        with ExitStack() as c2:
            keep.attention(Scope(nc, c2))
            stage_combine(nc, keep, scratch)
            stage_attention(nc, keep, scratch)
        stage_ffn(nc, keep, "f1", d["w13_1"], d["w2_1"], NG1, NJ1, norm=True, out=out)


def layout(i):
    import numpy as np

    f = np.float32

    def c(a):
        return np.ascontiguousarray(a)

    def swap(a):
        return np.concatenate([a[..., C // 2:], a[..., :C // 2]], axis=-1)

    def major(a):
        a = a.reshape(*a.shape[:-2], a.shape[-2] // P, P, a.shape[-1])
        return c(np.swapaxes(a, -3, -2))

    d = {}
    d["x"] = c(i["x"]).reshape(B * S, D)
    ctx = np.asarray(i["ctx_512"])
    ctxT = np.swapaxes(ctx, 1, 2)
    d["ctxT"] = c(ctxT)
    rot = swap(ctx)
    tok = lambda a: major(a).reshape(*a.shape[:-2], P, S)
    d["ctx_both"] = c(np.stack([ctxT, tok(ctx)]))
    d["ctx_rot"] = c(np.stack([np.swapaxes(rot, 1, 2), tok(rot)]))
    inv = (f(1.0) / np.power(f(10000.0), np.arange(0, C, 2, dtype=f) / f(C))).astype(f)
    ang = np.arange(S, dtype=f)[:, None] * inv[None, :]
    sin, cos = np.repeat(np.sin(ang), 2, axis=-1), np.repeat(np.cos(ang), 2, axis=-1)
    sin = np.concatenate([-sin[:, :C // 2], sin[:, C // 2:]], axis=-1)
    d["rope_cos"] = c(np.stack([cos.T, tok(cos)])).astype(f)
    d["rope_sin"] = c(np.stack([sin.T, tok(sin)])).astype(f)
    d["wq0T"], d["wk0T"] = c(np.asarray(i["L0_xattn_Wq"]).T), c(np.asarray(i["L0_xattn_Wk"]).T)
    d["gamma"] = c(np.broadcast_to(np.asarray(i["L0_xattn_gamma_raw"]).reshape(1, 1), (P, 1)))
    d["gate_wT"] = c(np.asarray(i["L0_ffn_gate_w"]).T)
    d["wq1"] = c(i["L1_xattn_Wq"])
    d["kcqT"] = c(np.swapaxes(np.asarray(i["L1_xattn_w_kc_q"]), 1, 2))
    d["wqr"] = c(i["L1_xattn_W_qr"])
    d["kckv"] = c(i["L1_xattn_w_kc_kv"])
    d["wkr"] = c(i["L1_xattn_W_kr"])
    d["woT"] = c(np.asarray(i["L1_xattn_Wo"]).T)

    def hidden_groups(w, n):
        out = np.zeros((w.shape[0], n, w.shape[2]), w.dtype)
        out[:, :w.shape[1]] = w
        return out

    def ffn(wg, wu, wd, n):
        up = [major(np.swapaxes(hidden_groups(w, n), 1, 2)) for w in (wg, wu)]
        return c(np.stack(up)), major(hidden_groups(np.swapaxes(wd, 1, 2), n))

    g = lambda a: np.asarray(i["L0_ffn_" + a])
    he = g("w1").shape[1]
    d["w13_e"], d["w2_e"] = ffn(g("w1"), g("w3"), g("w2"), NJ0 * P)
    d["w13_s"], d["w2_s"] = ffn(g("sw1").reshape(NS, he, D), g("sw3").reshape(NS, he, D),
                                np.swapaxes(g("sw2").reshape(D, NS, he), 0, 1), NJ0 * P)
    l = lambda a: np.asarray(i["L1_ffn_" + a])
    hw = NJ1 * P
    d["w13_1"], d["w2_1"] = ffn(l("w_gate").reshape(NG1, hw, D), l("w_up").reshape(NG1, hw, D),
                                np.swapaxes(l("w_down").reshape(D, NG1, hw), 0, 1), hw)
    return d


def kernel(**inputs):
    import concourse.bacc as _bacc
    from concourse.bass_utils import run_bass_kernel_spmd as _run

    nc = _bacc.Bacc("TRN2", target_bir_lowering=False, num_devices=1)
    arrays, aps = {}, {}
    for name, a in layout(inputs).items():
        arrays[f"in_{name}"] = a
        aps[name] = nc.dram_tensor(f"in_{name}", a.shape, mybir.dt.from_np(a.dtype), kind="ExternalInput").ap()
    out = nc.dram_tensor("out", (B, S, D), FP32, kind="ExternalOutput").ap()
    build(nc, aps, out)
    return _run(nc, [arrays], core_ids=[0]).results[0]["out"]
```
